# Optimizing a Trainium2 kernel written in Bass

```python
import numpy as np
import jax
import jax.numpy as jnp

def _softmax(x, axis=-1):
    return jax.nn.softmax(x, axis=axis)

def _gelu(x):
    return jax.nn.gelu(x, approximate=True)

def _silu(x):
    return jax.nn.silu(x)

def _sigmoid(x):
    return jax.nn.sigmoid(x)

def _layernorm(x, axis=-1, eps=1e-05):
    m = jnp.mean(x, axis=axis, keepdims=True)
    v = jnp.var(x, axis=axis, keepdims=True)
    return (x - m) / jnp.sqrt(v + eps)

def _scatter_add(tgt, idx, src, axis=0):
    return tgt.at[idx].add(src)

def _segment_sum(src, seg, n):
    return jax.ops.segment_sum(src, seg, n)
kernel_name = 'mk_gnn_resnorm_d2_gnn_r64_a34fed'

def setup_inputs(seed: int=0):
    np.random.seed(seed)
    _w = jnp.asarray

    def _rec_inputs():
        import jax
        import jax.numpy as jnp
        _gk = jax.random.key(seed)
        x = -0.0008691 + 1 * jax.random.normal(jax.random.fold_in(_gk, 1), (100000, 64), jnp.float32)
        src = jax.random.randint(jax.random.fold_in(_gk, 2), (50000,), 0, 100000, jnp.int32)
        dst = jnp.minimum((100000 * jax.random.uniform(jax.random.fold_in(_gk, 3), (50000,)) ** 2.0).astype(jnp.int32), 99999)
        _o = jnp.argsort(dst, stable=True)
        src = src[_o]
        dst = dst[_o]
        edge_weight = jax.random.uniform(jax.random.fold_in(_gk, 12), (50000,), jnp.float32, 0.0, 0.999999)
        return (x, src, dst, edge_weight)
    x, src, dst, edge_weight = _rec_inputs()

    def _L0_gnn_setup():
        import jax, jax.numpy as jnp
        import numpy as np
        N_NODES = 20000
        N_EDGES = 5000
        IN_CH = 64
        GROWTH = 64
        N_BLOCKS = 3

        def _edge_conv(x, src, dst, W, b, n_nodes):
            xi = x[dst]
            xj = x[src]
            feat = jnp.concatenate([xi, xj - xi], axis=-1)
            msg = jax.nn.relu(feat @ W + b)
            agg = jax.ops.segment_max(msg, dst, num_segments=n_nodes)
            return jnp.where(jnp.isfinite(agg), agg, 0.0)
        key = jax.random.key(seed)
        ks = jax.random.split(key, 8)
        x = jax.random.normal(ks[0], (N_NODES, IN_CH), dtype=jnp.float32)
        edge_index = jax.random.randint(ks[1], (2, N_EDGES), 0, N_NODES, dtype=jnp.int32)
        params = {}
        for i in range(N_BLOCKS):
            fan_in = 2 * (IN_CH + i * GROWTH)
            scale = 1.0 / np.sqrt(fan_in)
            params[f'W{i}'] = jax.random.normal(ks[2 + i], (fan_in, GROWTH), dtype=jnp.float32) * scale
            params[f'b{i}'] = jnp.zeros((GROWTH,), dtype=jnp.float32)
        return {'x': x, 'W0': params['W0'], 'b0': params['b0'], 'W1': params['W1'], 'b1': params['b1'], 'W2': params['W2'], 'b2': params['b2'], 'edge_index': edge_index}
    _L0_gnn_all = _L0_gnn_setup()
    _L0_gnn_in = {k: v for k, v in _L0_gnn_all.items() if k in ('W0', 'b0', 'W1', 'b1', 'W2', 'b2')}
    del _L0_gnn_all

    def _L1_gnn_setup():
        import jax, jax.numpy as jnp
        import numpy as np
        import math
        N_NODES = 100000
        N_EDGES = 25000
        IN_CH = 64
        OUT_CH = 64
        EPS = 1e-12
        key = jax.random.key(seed)
        k1, k2, k3, k4, k5 = jax.random.split(key, 5)
        x = jax.random.normal(k1, (N_NODES, IN_CH), dtype=jnp.float32)
        edge_index = jax.random.randint(k2, (2, N_EDGES), 0, N_NODES, dtype=jnp.int64)
        edge_attr = jax.random.uniform(k3, (N_EDGES,), dtype=jnp.float32)
        stdv = 1.0 / math.sqrt(IN_CH)
        weight = jax.random.uniform(k4, (IN_CH, OUT_CH), dtype=jnp.float32, minval=-stdv, maxval=stdv)
        bias = jax.random.uniform(k5, (OUT_CH,), dtype=jnp.float32, minval=-stdv, maxval=stdv)
        return {'x': x, 'edge_index': edge_index, 'edge_attr': edge_attr, 'weight': weight, 'bias': bias}
    _L1_gnn_all = _L1_gnn_setup()
    _L1_gnn_in = {k: v for k, v in _L1_gnn_all.items() if k in ('weight', 'bias')}
    del _L1_gnn_all
    return {'x': x, 'src': src, 'dst': dst, 'edge_weight': edge_weight, 'L0_gnn_W0': _L0_gnn_in['W0'], 'L0_gnn_b0': _L0_gnn_in['b0'], 'L0_gnn_W1': _L0_gnn_in['W1'], 'L0_gnn_b1': _L0_gnn_in['b1'], 'L0_gnn_W2': _L0_gnn_in['W2'], 'L0_gnn_b2': _L0_gnn_in['b2'], 'L1_gnn_weight': _L1_gnn_in['weight'], 'L1_gnn_bias': _L1_gnn_in['bias']}

def reference(x, src, dst, edge_weight, L0_gnn_W0, L0_gnn_b0, L0_gnn_W1, L0_gnn_b1, L0_gnn_W2, L0_gnn_b2, L1_gnn_weight, L1_gnn_bias):
    import jax
    import jax.numpy as jnp

    def _L0_gnn_ref(x, W0, b0, W1, b1, W2, b2, edge_index):
        import jax, jax.numpy as jnp
        import numpy as np
        N_NODES = 20000
        N_EDGES = 5000
        IN_CH = 64
        GROWTH = 64
        N_BLOCKS = 3

        def _edge_conv(x, src, dst, W, b, n_nodes):
            xi = x[dst]
            xj = x[src]
            feat = jnp.concatenate([xi, xj - xi], axis=-1)
            msg = jax.nn.relu(feat @ W + b)
            agg = jax.ops.segment_max(msg, dst, num_segments=n_nodes)
            return jnp.where(jnp.isfinite(agg), agg, 0.0)
        src, dst = (edge_index[0], edge_index[1])
        n = x.shape[0]
        for W, b in ((W0, b0), (W1, b1), (W2, b2)):
            out = _edge_conv(x, src, dst, W, b, n)
            x = jnp.concatenate([x, out], axis=-1)
        x = x.reshape(n, GROWTH, N_BLOCKS + 1)
        return jnp.max(x, axis=-1)

    def _L1_gnn_ref(x, edge_index, edge_attr, weight, bias):
        import jax, jax.numpy as jnp
        import numpy as np
        import math
        N_NODES = 100000
        N_EDGES = 25000
        IN_CH = 64
        OUT_CH = 64
        EPS = 1e-12
        row, col = (edge_index[0], edge_index[1])
        msgs = edge_attr[:, None] * x[col]
        agg = jax.ops.segment_sum(msgs, row, num_segments=x.shape[0])
        out = agg @ weight + bias
        norm = jnp.linalg.norm(out, axis=-1, keepdims=True)
        out = out / jnp.maximum(norm, EPS)
        return out
    edge_index = jnp.stack([src, dst])
    x = _layernorm(x + _L0_gnn_ref(x, L0_gnn_W0, L0_gnn_b0, L0_gnn_W1, L0_gnn_b1, L0_gnn_W2, L0_gnn_b2, edge_index), axis=-1)
    x = _layernorm(x + _L1_gnn_ref(x, edge_index, edge_weight, L1_gnn_weight, L1_gnn_bias), axis=-1)
    return x

_drawn_inputs = setup_inputs


def setup_inputs(seed=0):
    import zlib

    import numpy as np

    out = dict(_drawn_inputs(seed))
    spreads = {'L0_gnn_b0': (0.0, 0.311), 'L0_gnn_b1': (0.0, 0.322), 'L0_gnn_b2': (0.0, 0.385)}
    factors = {}
    for name, (base, spread) in spreads.items():
        noise = np.random.default_rng([zlib.crc32(name.encode()), seed]).standard_normal(out[name].shape)
        drawn = base * np.exp(spread * noise) if base else spread * noise
        out[name] = jnp.asarray(drawn.astype(out[name].dtype))
    for name, factor in factors.items():
        out[name] = (out[name] * factor).astype(out[name].dtype)
    return out
```

```python
from contextlib import ExitStack

import numpy as np

import concourse.bass as bass
from concourse import mybir

FP32, BF16, FP16, I32 = mybir.dt.float32, mybir.dt.bfloat16, mybir.dt.float16, mybir.dt.int32
ALU = mybir.AluOpType
ACT = mybir.ActivationFunctionType
X = mybir.AxisListType.X

P = 128
N = 100000
E = 50000
F = 64
TPC = 4
CH = TPC * P
NCH = -(-E // CH)
NCH += NCH % 2
NT = NCH * TPC
EP = NCH * CH
LAST_ROW = E - (NCH - 1) * CH
HI = -(-N // P)
HB = HI // 2
NB = -(-HI // P)
NFILL = 1024
NTAB = NFILL * NCH
Z_LATE = 3
DUMMY = N + 1
ZROW = EP
ROW = F + 2
NPP = 16
GR = P * NPP
NG = N // GR
A_SPLIT = NCH // 4
A_FIRST = NG + 1 - A_SPLIT
RP = (N - NG * GR) // NPP
EPS_LN = 1e-5
EPS_NORM = 1e-12
H_STEPS = 12
assert HI % 2 == 0 and RP * NPP == N - NG * GR and NTAB >= DUMMY + P and 0 < LAST_ROW < CH


def stepped(eng, stages, total, depth=2):
    skew = max(late for _, late in stages)
    lead = -(-(skew + depth) // depth) * depth
    whole = total - total % depth

    def at(s):
        for fn, late in stages:
            n = s - late
            if 0 <= n < total:
                fn(n, n // depth, n % depth)

    for s in range(lead):
        at(s)
    with eng.Fori(lead // depth, whole // depth) as i:
        for v in range(depth):
            for fn, late in stages:
                fn(depth * i + (v - late), i + (v - late) // depth, (v - late) % depth)
    for s in range(whole, total + skew):
        at(s)


def again(n, depth=2):
    return not isinstance(n, int) or n >= depth


def freed(eng, semaphore, n, per=1, depth=2):
    if again(n, depth):
        eng.wait_ge(semaphore, per * (n - depth + 1))


def stored(eng, semaphore, n, k, amount=16, depth=2):
    if again(n, depth):
        eng.wait_ge(semaphore, amount * k)


def build(nc, x, src, dst, edge_weight, w0, b0, w1, b1, w2, b2, w_l1, b_l1, out):
    with ExitStack() as ctx:
        def sb(name, shape, dt=FP32):
            return ctx.enter_context(nc.sbuf_tensor(name, shape, dt))

        def sem(name):
            return ctx.enter_context(nc.semaphore(name))

        def dram(name, shape, dt=FP32):
            return nc.dram_tensor(name, shape, dt).ap()

        xpos = dram("xpos", (N, ROW))
        pos_d = dram("pos_d", (HI * P, 2))
        same_d = dram("same_d", (EP + CH,))
        srcf_d = dram("srcf_d", (EP,))
        part_d = dram("part_d", (P, EP))
        tables = [dram("table0", (EP + 1, F)), dram("table1", (EP + 1, F))]
        o2_d = dram("o2_d", (F, EP))
        y1_d = dram("y1_d", (NTAB, F))
        agg_d = [dram("agg0", (NTAB, F)), dram("agg1", (NTAB, F))]

        xl = sb("xl", [P, NT * F])
        dst_g = sb("dst_g", [P, NT], I32)
        dst_s = sb("dst_s", [P, NT], I32)
        src_g = sb("src_g", [P, NT], I32)
        src_f = sb("src_f", [P, NT])
        ew = sb("ew", [P, NT])
        pos_g = [sb("last_g", [P, NT], I32), sb("first_g", [P, NT], I32)]
        ident = sb("ident", [P, P])
        w_x = sb("w_x", [P, 3 * F])
        w_o = [sb("w_o0", [P, 2 * F]), sb("w_o1", [P, F])]
        w_p = sb("w_p", [F, F])
        bias0 = sb("bias0", [F, 1])
        bias12 = sb("bias12", [P, 1])
        fill = [sb("fill0", [P, NFILL // P * F]), sb("fill1", [P, NFILL // P * F])]
        eps_ln = sb("eps_ln", [P, 1])
        zero = sb("zero", [P, 1])
        mask = sb("mask", [P, TPC, P])
        dummy_f = sb("dummy_f", [P, 1])
        idx_w = sb("idx_w", [P, 4, TPC], I32)

        work_words = 18432
        work = sb("work", [P, work_words])
        place = [0]

        def carve(words):
            place[0] += words
            assert place[0] <= work_words, place[0]
            return work[:, place[0] - words:place[0]]

        psum = ctx.enter_context(nc.psum_tensor("psum", [P, 8, 512], FP32))
        p_t = [psum[:, 0, :], psum[:, 1, :]]
        p_m = [psum[:, 2, :], psum[:, 3, :]]
        p_p = [psum[:, 4, :], psum[:, 5, :]]
        p_b = [psum[:, 6, :], psum[:, 7, :]]

        phase_done = sem("phase_done")

        def phase_end(eng, n):
            eng.drain().then_inc(phase_done, 1)
            eng.wait_ge(phase_done, 5 * n)
            eng.nop(nofuse=True)

        n_dst, n_prev, n_next, n_src = (carve(CH)[0:NCH, :].bitcast(I32) for _ in range(4))
        n_ew, n_same, n_last, n_dummy, n_dstf, n_srcf, n_dsts = (carve(CH)[0:NCH, :] for _ in range(7))
        end_natural = place[0]
        w_b = carve(6 * F)[0:F, :]
        b_row = carve(F)
        hi_i = carve(NT).bitcast(I32)
        hi_f = carve(NT)
        lo_f = carve(NT)
        iota_h = carve(HB).bitcast(FP16)
        iota_l = carve(F).bitcast(FP16)
        oh_h = [carve(HB).bitcast(BF16) for _ in range(2)]
        oh_l = [carve(F).bitcast(BF16) for _ in range(2)]
        upper = carve(P)
        ones = carve(P)
        pos_n = carve(NB * P * 2)
        def a_buffers(copies):
            return [[carve(width) for _ in range(copies)] for width in (NPP * F, NPP * F, NPP * 16, NPP * 4)]

        a_first = a_buffers(2)
        a_first.insert(0, a_first[0])
        xs = [carve(NPP * ROW) for _ in range(2)]
        xi = [carve(TPC * F) for _ in range(2)]
        place[0] = 0
        cnt, tot, run, last_c, first_c = (carve(HI) for _ in range(5))
        assert place[0] <= end_natural
        place[0] = 0
        xb = [carve(NPP * F) for _ in range(4)]
        ps = [carve(NPP * 2) for _ in range(4)]
        assert place[0] <= end_natural

        place[0] = 0
        fx = [carve(TPC * (P + 2)) for _ in range(4)]
        xt = [carve(CH) for _ in range(2)]
        ms = [carve(CH) for _ in range(2)]
        fs = [carve(CH) for _ in range(2)]
        sn = [carve(CH) for _ in range(4)]
        pl = [carve(CH) for _ in range(4)]
        ts = [carve(TPC * F) for _ in range(2)]
        gm = [carve(TPC * 16) for _ in range(2)]
        before_p3 = place[0]
        yy = [carve(TPC * F) for _ in range(4)]
        st3 = [carve(TPC * 4) for _ in range(2)]
        zs = [carve(TPC * F) for _ in range(2)]
        ga = [m[:, q * TPC * F:(q + 1) * TPC * F] for m in ms for q in range(2)]
        sq3 = ts
        eq = [carve(CH) for _ in range(2)]
        sr = [carve(CH) for _ in range(4)]
        eqm = carve(CH)
        dup = carve(TPC)
        off = carve(TPC)
        add_i = [carve(TPC).bitcast(I32) for _ in range(4)]
        place[0] = before_p3
        a_second = a_buffers(1)
        a_second.insert(0, [carve(NPP * F)])

        DD = 4
        dz = [[xl[:, (4 * u + q) * NPP * F:(4 * u + q + 1) * NPP * F] for q in range(4)] for u in range(DD)]
        dst_d = [xl[:, 4 * DD * NPP * F + u * 8 * NPP:4 * DD * NPP * F + (u + 1) * 8 * NPP] for u in range(DD)]

        def fx3(u):
            return fx[u].rearrange("p (j f) -> p j f", f=P + 2)

        def byf(a, f=F):
            return a.rearrange("p (j f) -> p j f", f=f)

        def spread(a, width):
            return a.unsqueeze(2).to_broadcast([a.shape[0], a.shape[1], width])

        def at_chunk(l, n):
            return n if l in (0, 2) else (NCH - 1) - n

        def e0(l, n):
            return at_chunk(l, n) * CH

        def cols(a, l, n):
            return a[:, bass.ds(at_chunk(l, n) * TPC, TPC)]

        def xl_at(l, n, a=0, b=F):
            return byf(xl[:, bass.ds(at_chunk(l, n) * (TPC * F), TPC * F)])[:, :, a:b]

        def rows(t, l, n):
            return t[bass.ds(e0(l, n), CH), :].rearrange("(j p) f -> p j f", p=P)

        def parts_of(n):
            return RP if isinstance(n, int) and n == NG else P

        def group(t, n):
            return t[bass.ds(n * GR, parts_of(n) * NPP), :].rearrange("(p k) f -> p (k f)", k=NPP)

        def first_group(k):
            return A_SPLIT + k

        def second_group(k):
            return k

        def in_fours(what):
            def stage(n, k, u):
                for fn, late in what.get(u, ()):
                    if not isinstance(k, int) or 0 <= k + late < A_SPLIT:
                        fn(k + late, k + late, 0)
            return stage

        def back(a, l):
            return a[:, ::-1] if l in (1, 3) else a

        def end_col(a, l):
            return a[:, 0:1] if l in (1, 3) else a[:, CH - 1:CH]

        c_memset, c_zero, c_nat, c_wts, c_pool = sem("c_memset"), sem("c_zero"), sem("c_nat"), sem("c_wts"), sem("c_pool")
        c_v, c_same, c_rows, c_out, c_tr, c_dst = sem("c_v"), sem("c_same"), sem("c_rows"), sem("c_out"), sem("c_tr"), sem("c_dst")
        window_ready = sem("window_ready")
        x_got, x_put = [sem("x_got0"), sem("x_got1")], [sem("x_put0"), sem("x_put1")]
        h_free, h_made, h_v, h_pe, h_tr, h_pos, h_out = (sem(f"h_{t}") for t in ("free", "made", "v", "pe", "tr", "pos", "out"))
        b_in, b_out = [sem(f"b_in{u}") for u in range(4)], [sem("b_out0"), sem("b_out1")]
        b_row_made = sem("b_row_made")
        a_in, a_out = ([sem(f"a_{t}{u}") for u in range(2)] for t in ("in", "out"))
        a_v, a_sub, a_sq, a_var, a_std, a_rec, a_y = (sem(f"a_{t}") for t in ("v", "sub", "sq", "var", "std", "rec", "y"))

        def sems(tag, plain, dmas2, dmas4):
            made = {t: sem(f"{tag}_{t}") for t in plain.split()}
            made.update({t: [sem(f"{tag}_{t}{u}") for u in range(2)] for t in dmas2.split()})
            made.update({t: [sem(f"{tag}_{t}{u}") for u in range(4)] for t in dmas4.split()})
            return made

        q0 = sems("q0", "xi t_ready xt_ready m_ready ms_ready p_ready part_ready scan taken b_ready ts_ready",
                  "d_part d_table", "d_in d_got")
        q12 = {l: sems(f"q{l}", "t_ready g_ready o_ready p_ready s_ready scan gb_ready gmax d_fill",
                       "d_table", "d_in d_got") for l in (1, 2)}
        q12[1].update(sems("q1", "fb_ready ts_ready", "d_part", ""))
        q3 = sems("q3", "scan gb_ready gmax xl ln sub sq var std rec y_ready yt_ready yts z_ready zs eq eqc "
                  "add_i sum_ready ga_ready", "d_add", "d_in d_y")
        f_in, f_out = ([sem(f"f_{t}{u}") for u in range(DD)] for t in ("in", "out"))
        f_sum, f_sq1, f_nrm, f_std1, f_v, f_sub, f_sq2, f_var, f_std2, f_rec, f_y = (
            sem(f"f_{t}") for t in ("sum", "sq1", "nrm", "std1", "v", "sub", "sq2", "var", "std2", "rec", "y"))

        block = ctx.enter_context(nc.Block())

        @block.sync
        def _(sp):
            full = (NCH - 1) * CH

            def row(a):
                return a.rearrange("(c k) -> c k", c=1)

            sp.wait_ge(c_memset, 1)
            for tile, array in ((n_dst, dst), (n_src, src), (n_ew, edge_weight)):
                sp.dma_start(tile[0:NCH - 1, :], array[0:full].rearrange("(c k) -> c k", k=CH)).then_inc(c_nat, 16)
                sp.dma_start(tile[NCH - 1:NCH, 0:LAST_ROW], row(array[full:E])).then_inc(c_nat, 16)
            sp.dma_start(n_prev[0:1, 1:CH], row(dst[0:CH - 1])).then_inc(c_nat, 16)
            sp.dma_start(n_prev[1:NCH - 1, :], dst[CH - 1:full - 1].rearrange("(c k) -> c k", k=CH)).then_inc(c_nat, 16)
            sp.dma_start(n_prev[NCH - 1:NCH, 0:LAST_ROW + 1], row(dst[full - 1:E])).then_inc(c_nat, 16)
            sp.dma_start(n_next[0:NCH - 1, :], dst[1:full + 1].rearrange("(c k) -> c k", k=CH)).then_inc(c_nat, 16)
            sp.dma_start(n_next[NCH - 1:NCH, 0:LAST_ROW - 1], row(dst[full + 1:E])).then_inc(c_nat, 16)
            blocks = ((w0, 0, F, w_x, 0), (w1, 0, 2 * F, w_x, 1), (w2, 0, 3 * F, w_x, 2),
                      (w1, F, 3 * F, w_o[0], 0), (w2, F, 4 * F, w_o[0], 1), (w2, 2 * F, 5 * F, w_o[1], 0))
            for q, (w, a, b, tile, at) in enumerate(blocks):
                sp.dma_start(tile[0:F, at * F:(at + 1) * F], w[a:a + F, :]).then_inc(c_wts, 16)
                sp.dma_start(tile[F:P, at * F:(at + 1) * F], w[b:b + F, :]).then_inc(c_wts, 16)
                sp.dma_start(w_b[:, q * F:(q + 1) * F], w[b:b + F, :]).then_inc(c_wts, 16)
            sp.dma_start(w_p[:, :], w_l1[:, :]).then_inc(c_wts, 16)
            sp.dma_start(bias0[:, :], b0.rearrange("(p a) -> p a", a=1)).then_inc(c_wts, 16)
            sp.dma_start(bias12[0:F, :], b1.rearrange("(p a) -> p a", a=1)).then_inc(c_wts, 16)
            sp.dma_start(bias12[F:P, :], b2.rearrange("(p a) -> p a", a=1)).then_inc(c_wts, 16)
            sp.dma_start(b_row, b_l1.partition_broadcast(P)).then_inc(c_wts, 16)
            sp.wait_ge(c_zero, 1)
            for t in tables:
                sp.dma_start(t[ZROW:ZROW + 1, :], fill[1][0:1, 0:F]).then_inc(c_out, 16)
            sp.dma_start(row(same_d[EP:EP + CH]), fill[1][0:1, 0:CH]).then_inc(c_out, 16)
            sp.wait_ge(c_same, 2)
            sp.dma_start(same_d[0:EP].rearrange("(c k) -> c k", k=CH), n_same).then_inc(c_out, 16)
            sp.dma_start(srcf_d.rearrange("(c k) -> c k", k=CH), n_srcf).then_inc(c_out, 16)

            def put(n, k, u):
                sp.wait_ge(x_got[u], 64 * k + 64)
                sp.nop(nofuse=True)
                sp.dma_start(xl[:, bass.ds(n * (TPC * F), TPC * F)], xi[u]).then_inc(x_put[u], 16)

            stepped(sp, [(put, 0)], NCH)
            sp.wait_ge(c_out, 16 * 5)
            for u in range(2):
                sp.wait_ge(x_put[u], 16 * (NCH // 2))
            phase_end(sp, 1)

            def load0(n, k, u):
                freed(sp, q0["scan"], n, depth=4)
                sp.nop(nofuse=True)
                sp.dma_start(sn[u][0:F, :], same_d[bass.ds(e0(0, n), CH)].partition_broadcast(F)).then_inc(q0["d_in"][u], 16)

            stepped(sp, [(load0, 0)], NCH, 4)
            phase_end(sp, 2)

            for l in (1, 2):
                s = q12[l]

                def load(n, k, u):
                    freed(sp, s["scan"], n, depth=4)
                    freed(sp, s["t_ready"], n, depth=4)
                    sp.nop(nofuse=True)
                    sp.dma_start(fx3(u)[:, :, 0:F], rows(tables[l - 1], l, n)).then_inc(s["d_in"][u], 16)
                    ahead = 1 if l == 1 else 0
                    sp.dma_start(sn[u][0:F, :], same_d[bass.ds(e0(l, n) + ahead, CH)].partition_broadcast(F)).then_inc(s["d_in"][u], 16)
                    part = part_d[:, bass.ds(e0(l, n), CH)] if l == 1 else part_d[F:P, bass.ds(e0(l, n), CH)]
                    sp.dma_start(pl[u] if l == 1 else pl[u][0:F, :], part).then_inc(s["d_in"][u], 16)
                    sp.dma_start(agg_d[l - 1][bass.ds(n * NFILL, NFILL), :].rearrange("(p k) f -> p (k f)", p=P),
                                 fill[l - 1][:, :]).then_inc(s["d_fill"], 16)

                stepped(sp, [(load, 0)], NCH, 4)
                sp.wait_ge(s["d_fill"], 16 * NCH)
                phase_end(sp, l + 2)

            def load3(n, k, u):
                freed(sp, q3["scan"], n, depth=4)
                sp.nop(nofuse=True)
                sp.dma_start(sn[u][0:F, :], same_d[bass.ds(e0(3, n) + 1, CH)].partition_broadcast(F)).then_inc(q3["d_in"][u], 16)
                sp.dma_start(pl[u][0:F, :], o2_d[:, bass.ds(e0(3, n), CH)]).then_inc(q3["d_in"][u], 16)
                freed(sp, q3["eq"], n, depth=4)
                sp.nop(nofuse=True)
                sp.dma_start(sr[u], srcf_d[bass.ds(e0(3, n), CH)].partition_broadcast(P)).then_inc(q3["d_in"][u], 16)

            stepped(sp, [(load3, 0)], NCH, 4)
            phase_end(sp, 5)

            def load_f(n, k, u):
                stored(sp, f_out[u], n, k, depth=DD)
                sp.nop(nofuse=True)
                for q, t in enumerate((y1_d, agg_d[0], agg_d[1])):
                    sp.dma_start(dz[u][q][0:parts_of(n), :], group(t, n)).then_inc(f_in[u], 16)

            stepped(sp, [(load_f, 0)], NG + 1, DD)
            phase_end(sp, 6)

        @block.gpsimd
        def _(gp):
            def iota(out_, pattern, base, channel):
                gp.iota(out_, pattern=pattern, base=base, channel_multiplier=channel,
                        allow_small_or_imprecise_dtypes=True).then_inc(c_pool, 1)

            gp.memset(ident[:, :], 0.0).then_inc(c_pool, 1)
            gp.memset(mask[:, :, :], 1.0).then_inc(c_pool, 1)
            gp.memset(upper, 1.0).then_inc(c_pool, 1)
            iota(n_dummy.rearrange("p (j k) -> p j k", k=P), [[0, TPC], [1, P]], DUMMY, 0)
            gp.wait_ge(c_pool, 3)
            gp.affine_select(out=ident[:, :], in_=ident[:, :], compare_op=ALU.not_equal, fill=1.0, base=0,
                             pattern=[[-1, P]], channel_multiplier=1).then_inc(c_pool, 1)
            iota(iota_h, [[1, HI]], 0, 0)
            iota(iota_l, [[1, P]], 0, 0)
            iota(dummy_f[:, :], [[0, 1]], DUMMY, 1)
            gp.affine_select(out=mask[:, :, :], in_=mask[:, :, :], compare_op=ALU.is_gt, fill=0.0, base=0,
                             pattern=[[0, TPC], [-1, P]], channel_multiplier=1).then_inc(c_pool, 1)
            gp.affine_select(out=upper, in_=upper, compare_op=ALU.is_ge, fill=0.0, base=0,
                             pattern=[[1, P]], channel_multiplier=-1).then_inc(c_pool, 1)

            gp.wait_ge(c_dst, 1)
            gp.nop(nofuse=True)

            def window(column, l, n, u, use):
                gp.tensor_copy(idx_w[:, u, :], cols(column, l, n)).then_inc(window_ready, 1)
                gp.wait_ge(window_ready, use * NCH + n + 1)
                gp.nop(nofuse=True)

            def fetch(out_, table, u, j, done):
                gp.indirect_dma_start(out_, None, table[:, :],
                                      bass.IndirectOffsetOnAxis(ap=idx_w[:, u, j:j + 1], axis=0)).then_inc(done, 16)

            def gather_x(n, k, u):
                stored(gp, x_put[u], n, k)
                gp.nop(nofuse=True)
                window(dst_g, 0, n, u, 0)
                for j in range(TPC):
                    fetch(xi[u][:, j * F:(j + 1) * F], x, u, j, x_got[u])

            stepped(gp, [(gather_x, 0)], NCH)
            phase_end(gp, 1)

            def gather0(n, k, u):
                freed(gp, q0["t_ready"], n, depth=4)
                freed(gp, q0["taken"], n, depth=4)
                gp.nop(nofuse=True)
                window(src_g, 0, n, u, 1)
                for j in range(TPC):
                    fetch(fx3(u)[:, j, F:P + 2], xpos, u, j, q0["d_got"][u])

            stepped(gp, [(gather0, 0)], NCH, 4)
            phase_end(gp, 2)

            for l in (1, 2):
                s = q12[l]

                def gather(n, k, u):
                    freed(gp, s["t_ready"], n, depth=4)
                    gp.nop(nofuse=True)
                    window(pos_g[l - 1], l, n, u, l + 1)
                    for j in range(TPC):
                        fetch(fx3(u)[:, j, F:P], tables[l - 1], u, j, s["d_got"][u])

                stepped(gp, [(gather, 0)], NCH, 4)
                phase_end(gp, l + 2)

            def add(m, w, j):
                if j >= 2 or not isinstance(m, int) or m > 0:
                    gp.wait_ge(q3["d_add"][j % 2], 16 * (2 * m + j // 2))
                    gp.nop(nofuse=True)
                gp.indirect_dma_start(agg_d[j % 2][:, :], bass.IndirectOffsetOnAxis(ap=add_i[w][:, j:j + 1], axis=0),
                                      ga[w][:, j * F:(j + 1) * F], None, compute_op=ALU.add).then_inc(q3["d_add"][j % 2], 16)

            def scatter(n, k, u):
                z = (u - Z_LATE) % 4
                some_y = not isinstance(n, int) or n < NCH
                some_z = not isinstance(n, int) or n >= Z_LATE
                if some_y:
                    gp.wait_ge(q3["y_ready"], n + 1)
                    stored(gp, q3["d_y"][u], n, k, 64, 4)
                    gp.nop(nofuse=True)
                    window(dst_s, 3, n, u, 4)
                if some_z:
                    gp.wait_ge(q3["ga_ready"], n - Z_LATE + 1)
                    gp.wait_ge(q3["add_i"], n - Z_LATE + 1)
                    gp.nop(nofuse=True)
                for j in (0, 2):
                    if some_z:
                        add(n - Z_LATE, z, j)
                        add(n - Z_LATE, z, j + 1)
                    if some_y:
                        for q in (j, j + 1):
                            gp.indirect_dma_start(y1_d[:, :], bass.IndirectOffsetOnAxis(ap=idx_w[:, u, q:q + 1], axis=0),
                                                  yy[u][:, q * F:(q + 1) * F], None, bounds_check=N - 1,
                                                  oob_is_err=False).then_inc(q3["d_y"][u], 16)

            stepped(gp, [(scatter, 0)], NCH, 4)
            for n in range(NCH, NCH + Z_LATE):
                scatter(n, n // 4, n % 4)
            for u in range(4):
                gp.wait_ge(q3["d_y"][u], 64 * ((NCH + 3 - u) // 4))
            for q in range(2):
                gp.wait_ge(q3["d_add"][q], 32 * NCH)
            phase_end(gp, 5)
            phase_end(gp, 6)

        @block.scalar
        def _(act):
            for b in range(NB):
                w = min(P, HI - b * P)
                act.wait_ge(h_pos, b + 1)
                act.dma_start(pos_d[b * P * P:(b * P + w) * P, :].rearrange("(h l) q -> h (l q)", l=P),
                              pos_n[0:w, b * 2 * P:(b + 1) * 2 * P]).then_inc(h_out, 16)
            act.wait_ge(h_out, 16 * NB)

            def groups_b(k, s_):
                for q in range(2):
                    if not isinstance(k, int) or 2 * k + q <= NG:
                        yield q, 2 * k + q, 2 * s_ + q

            def load_b(k, kk, s_):
                for q, g, b in groups_b(k, s_):
                    m = parts_of(g)
                    if again(k):
                        act.wait_ge(b_row_made, 2 * g - 6)
                    act.nop(nofuse=True)
                    act.dma_start(xb[b][0:m, :], group(x, g)).then_inc(b_in[b], 16)
                    act.dma_start(ps[b][0:m, :], group(pos_d, g)).then_inc(b_in[b], 16)

            def row_b(k, kk, s_):
                for q, g, b in groups_b(k, s_):
                    m = parts_of(g)
                    act.wait_ge(b_in[b], 32 * kk + 32)
                    if again(k, 1):
                        act.wait_ge(b_out[q], 16 * k)
                    act.nop(nofuse=True)
                    act.activation(byf(xs[q], ROW)[0:m, :, 0:F], byf(xb[b])[0:m], ACT.Copy).then_inc(b_row_made, 1)
                    act.activation(byf(xs[q], ROW)[0:m, :, F:ROW], byf(ps[b], 2)[0:m], ACT.Copy).then_inc(b_row_made, 1)
                    act.wait_ge(b_row_made, 2 * g + 2)
                    act.nop(nofuse=True)
                    act.dma_start(group(xpos, g), xs[q][0:m, :]).then_inc(b_out[q], 16)

            def nodes_act(buffers, c0, g_of):
                hx, hh, sq, _, st = buffers

                def load_a(k, kk, s_):
                    m = parts_of(g_of(k))
                    if c0:
                        act.wait_ge(a_sub, c0 + k)
                    elif again(k):
                        act.wait_ge(a_out[s_], 16 * kk)
                    act.nop(nofuse=True)
                    act.dma_start(hx[s_][0:m, :], group(x, g_of(k))).then_inc(a_in[s_], 16)

                def square_a(k, kk, s_):
                    m = parts_of(g_of(k))
                    act.wait_ge(a_sub, c0 + k + 1)
                    act.nop(nofuse=True)
                    act.activation(sq[s_][0:m, :], hh[s_][0:m, :], ACT.Square).then_inc(a_sq, 1)

                def root_a(k, kk, s_):
                    m = parts_of(g_of(k))
                    act.wait_ge(a_var, c0 + k + 1)
                    act.nop(nofuse=True)
                    act.activation(st[s_][0:m, 2 * NPP:3 * NPP], st[s_][0:m, NPP:2 * NPP], ACT.Sqrt,
                                   bias=eps_ln[0:m, :], scale=1.0 / F).then_inc(a_std, 1)

                def store_a(k, kk, s_):
                    m = parts_of(g_of(k))
                    act.wait_ge(a_y, c0 + k + 1)
                    act.nop(nofuse=True)
                    act.dma_start(group(y1_d, g_of(k)), hh[s_][0:m, :]).then_inc(a_out[s_], 16)

                return load_a, square_a, root_a, store_a

            load_a, square_a, root_a, store_a = nodes_act(a_first, 0, first_group)
            stepped(act, [(load_b, 0), (store_a, 2), (load_a, 0), (row_b, 1), (square_a, 1), (root_a, 1)], A_FIRST)
            for q in range(2):
                act.wait_ge(b_out[q], 16 * (NG // 2 + 1 - q))
                act.wait_ge(a_out[q], 16 * ((A_FIRST + 1 - q) // 2))
            phase_end(act, 1)

            def xi0(n, k, u):
                freed(act, q0["t_ready"], n, depth=4)
                freed(act, q0["taken"], n, depth=4)
                act.nop(nofuse=True)
                act.activation(fx3(u)[:, :, 0:F], xl_at(0, n), ACT.Copy).then_inc(q0["xi"], 1)

            def front0(n, k, u):
                w = u % 2
                act.wait_ge(q0["t_ready"], n + 1)
                freed(act, q0["p_ready"], n)
                act.nop(nofuse=True)
                act.activation(xt[w], p_t[w], ACT.Copy).then_inc(q0["xt_ready"], 1)

            def mid0(n, k, u):
                w = u % 2
                act.wait_ge(q0["m_ready"], n + 1)
                freed(act, q0["scan"], n)
                act.nop(nofuse=True)
                act.activation(ms[w][0:F, :], p_m[w][0:F, :], ACT.Identity, bias=bias0[:, :]).then_inc(q0["ms_ready"], 1)
                act.wait_ge(q0["p_ready"], n + 1)
                stored(act, q0["d_part"][w], n, 2 * k + u // 2)
                act.nop(nofuse=True)
                act.activation(pl[w], p_p[w], ACT.Identity, bias=bias12[:, :]).then_inc(q0["part_ready"], 1)

            def back0(n, k, u):
                w = u % 2
                act.wait_ge(q0["part_ready"], n + 1)
                act.nop(nofuse=True)
                act.dma_start(part_d[:, bass.ds(e0(0, n), CH)], pl[w]).then_inc(q0["d_part"][w], 16)
                act.wait_ge(q0["b_ready"], n + 1)
                stored(act, q0["d_table"][w], n, 2 * k + u // 2)
                act.nop(nofuse=True)
                act.activation(ts[w], p_b[w][:, 0:TPC * F], ACT.Copy).then_inc(q0["ts_ready"], 1)

            def out0(n, k, u):
                w = u % 2
                act.wait_ge(q0["ts_ready"], n + 1)
                act.nop(nofuse=True)
                act.dma_start(rows(tables[0], 0, n), byf(ts[w])).then_inc(q0["d_table"][w], 16)

            load_a, square_a, root_a, store_a = nodes_act(a_second, A_FIRST, second_group)
            nodes0 = in_fours({0: [(load_a, 0)], 1: [(store_a, -1)], 2: [(square_a, 0)], 3: [(root_a, 0)]})
            stepped(act, [(xi0, 0), (front0, 1), (mid0, 2), (out0, 4), (back0, 3), (nodes0, 0)], NCH, 4)
            for w in range(2):
                act.wait_ge(q0["d_part"][w], 16 * (NCH // 2))
                act.wait_ge(q0["d_table"][w], 16 * (NCH // 2))
            act.wait_ge(a_out[0], 16 * ((A_FIRST + 1) // 2 + A_SPLIT))
            phase_end(act, 2)

            for l in (1, 2):
                s = q12[l]

                def front(n, k, u):
                    w = u % 2
                    act.wait_ge(s["t_ready"], n + 1)
                    freed(act, s["p_ready"], n)
                    act.nop(nofuse=True)
                    act.activation(xt[w][F:P, :], p_t[w][F:P, :], ACT.Copy).then_inc(s["o_ready"], 1)

                def back1(n, k, u):
                    w = u % 2
                    act.wait_ge(s["fb_ready"], n + 1)
                    stored(act, s["d_table"][w], n, 2 * k + u // 2)
                    act.nop(nofuse=True)
                    act.activation(ts[w], p_m[w][:, 0:TPC * F], ACT.Copy).then_inc(s["ts_ready"], 1)

                def store_part(n, k, u):
                    w = u % 2
                    act.wait_ge(s["s_ready"], n + 1)
                    act.nop(nofuse=True)
                    act.dma_start(part_d[F:P, bass.ds(e0(l, n), CH)], ms[w][F:P, :]).then_inc(s["d_part"][w], 16)

                def store_out(n, k, u):
                    w = u % 2
                    if l == 1:
                        act.wait_ge(s["ts_ready"], n + 1)
                        act.nop(nofuse=True)
                        act.dma_start(rows(tables[1], l, n), byf(ts[w])).then_inc(s["d_table"][w], 16)
                    else:
                        act.wait_ge(s["scan"], n + 1)
                        act.nop(nofuse=True)
                        act.dma_start(o2_d[:, bass.ds(e0(l, n), CH)], fs[w][0:F, :]).then_inc(s["d_table"][w], 16)

                if l == 1:
                    stages = [(front, 0), (store_out, 3), (store_part, 2), (back1, 2)]
                else:
                    stages = [(front, 0), (store_out, 2)]
                stepped(act, stages, NCH, 4)
                for w in range(2):
                    if l == 1:
                        act.wait_ge(s["d_part"][w], 16 * (NCH // 2))
                    act.wait_ge(s["d_table"][w], 16 * (NCH // 2))
                phase_end(act, l + 2)

            def square3(n, k, u):
                w = u % 2
                act.wait_ge(q3["sub"], n + 1)
                freed(act, q3["var"], n)
                act.nop(nofuse=True)
                act.activation(sq3[w], yy[u], ACT.Square).then_inc(q3["sq"], 1)

            def root3(n, k, u):
                w = u % 2
                act.wait_ge(q3["var"], n + 1)
                act.nop(nofuse=True)
                act.activation(st3[w][:, 2 * TPC:3 * TPC], st3[w][:, TPC:2 * TPC], ACT.Sqrt,
                               bias=eps_ln[:, :], scale=1.0 / F).then_inc(q3["std"], 1)

            def project3(n, k, u):
                w = u % 2
                act.wait_ge(q3["yt_ready"], n + 1)
                freed(act, q3["z_ready"], n)
                act.nop(nofuse=True)
                act.activation(xt[w][0:F, :], p_t[w][0:F, :], ACT.Copy).then_inc(q3["yts"], 1)

            def sum3(n, k, u):
                w = u % 2
                act.wait_ge(q3["sum_ready"], n + 1)
                for q in range(2):
                    freed(act, q3["d_add"][q], n, 32, 4)
                act.nop(nofuse=True)
                act.activation(ga[u], p_p[w][:, 0:TPC * F], ACT.Copy).then_inc(q3["ga_ready"], 1)

            stepped(act, [(project3, 2), (sum3, 4), (square3, 1), (root3, 1)], NCH, 4)
            phase_end(act, 5)

            def norm_f(n, k, u):
                m = parts_of(n)
                act.wait_ge(f_sum, n + 1)
                act.nop(nofuse=True)
                act.activation(dz[u][3][0:m, :], dz[u][1][0:m, :], ACT.Square).then_inc(f_sq1, 1)

            def root1_f(n, k, u):
                m = parts_of(n)
                act.wait_ge(f_nrm, n + 1)
                act.nop(nofuse=True)
                act.activation(dst_d[u][0:m, NPP:2 * NPP], dst_d[u][0:m, 0:NPP], ACT.Sqrt).then_inc(f_std1, 1)

            def square_f(n, k, u):
                m = parts_of(n)
                act.wait_ge(f_sub, n + 1)
                act.nop(nofuse=True)
                act.activation(dz[u][3][0:m, :], dz[u][1][0:m, :], ACT.Square).then_inc(f_sq2, 1)

            def root2_f(n, k, u):
                m = parts_of(n)
                act.wait_ge(f_var, n + 1)
                act.nop(nofuse=True)
                act.activation(dst_d[u][0:m, 5 * NPP:6 * NPP], dst_d[u][0:m, 4 * NPP:5 * NPP], ACT.Sqrt,
                               bias=eps_ln[0:m, :], scale=1.0 / F).then_inc(f_std2, 1)

            def store_f(n, k, u):
                act.wait_ge(f_y, n + 1)
                act.dma_start(group(out, n), dz[u][1][0:parts_of(n), :]).then_inc(f_out[u], 16)

            stepped(act, [(norm_f, 0), (root1_f, 0), (square_f, 1), (root2_f, 2), (store_f, 2)], NG + 1, DD)
            for u in range(DD):
                act.wait_ge(f_out[u], 16 * ((NG + 1 - u + DD - 1) // DD))
            phase_end(act, 6)

        @block.tensor
        def _(pe):
            pe.wait_ge(c_pool, 5)
            pe.wait_ge(c_rows, 1)
            pe.wait_ge(c_nat, 16 * 11)
            for q, tile in enumerate((n_dstf, n_dsts, n_srcf, n_ew)):
                for j in range(TPC):
                    last = nc.tensor.transpose(psum[:, q, j * NCH:(j + 1) * NCH], tile[:, j * P:(j + 1) * P],
                                               ident[0:NCH, 0:NCH])
                last.then_inc(c_tr, 1)

            def count(lo, hi, start=False, stop=False):
                for b in range(2):
                    last = nc.tensor.matmul(psum[:, 4 + b, 0:HB], lo, hi[:, b * HB:(b + 1) * HB],
                                            start=start, stop=stop)
                last.then_inc(h_free, 1)

            pe.wait_ge(h_made, 1)
            count(oh_l[0], oh_h[0], start=True)

            def count_tile(n, k, u):
                pe.wait_ge(h_made, n + 2)
                count(oh_l[u], oh_h[u], stop=isinstance(n, int) and n == NT - 1)

            stepped(pe, [(count_tile, 0)], NT - 2)
            count_tile(NT - 2, NT // 2 - 1, 0)
            count_tile(NT - 1, NT // 2 - 1, 1)
            pe.wait_ge(h_v, 1)
            pe.wait_ge(c_pool, 10)
            for b in range(2):
                nc.tensor.matmul(psum[:, b, 0:HB], upper, cnt[:, b * HB:(b + 1) * HB], start=True, stop=True)
                last = nc.tensor.matmul(psum[:, 2 + b, 0:HB], ones, cnt[:, b * HB:(b + 1) * HB], start=True, stop=True)
            last.then_inc(h_pe, 1)
            pe.wait_ge(h_v, H_STEPS)
            for b in range(NB):
                w = min(P, HI - b * P)
                if b >= 4:
                    pe.wait_ge(h_pos, b - 3)
                for q, t in enumerate((last_c, first_c)):
                    last = nc.tensor.transpose(psum[0:w, 4 + b % 4, q * P:(q + 1) * P], t[:, b * P:b * P + w],
                                               ident[:, :])
                last.then_inc(h_tr, 1)
            phase_end(pe, 1)

            def front0(n, k, u):
                w = u % 2
                pe.wait_ge(q0["xi"], n + 1)
                pe.wait_ge(q0["d_got"][u], 64 * k + 64)
                freed(pe, q0["xt_ready"], n)
                pe.nop(nofuse=True)
                for j in range(TPC):
                    last = nc.tensor.transpose(p_t[w][:, j * P:(j + 1) * P], fx3(u)[:, j, 0:P], ident[:, :])
                last.then_inc(q0["t_ready"], 1)

            def mid0(n, k, u):
                w = u % 2
                pe.wait_ge(q0["xt_ready"], n + 1)
                freed(pe, q0["ms_ready"], n)
                pe.nop(nofuse=True)
                nc.tensor.matmul(p_m[w][0:F, :], w_x[:, 0:F], xt[w], start=True, stop=True).then_inc(q0["m_ready"], 1)
                freed(pe, q0["part_ready"], n)
                pe.nop(nofuse=True)
                nc.tensor.matmul(p_p[w], w_x[:, F:3 * F], xt[w], start=True, stop=True).then_inc(q0["p_ready"], 1)

            def by_edge(bank, rows_t, done):
                for j in range(TPC):
                    last = nc.tensor.transpose(bank[:, j * F:(j + 1) * F], rows_t[0:F, j * P:(j + 1) * P],
                                               ident[0:F, 0:F])
                last.then_inc(done, 1)

            def back0(n, k, u):
                w = u % 2
                pe.wait_ge(q0["scan"], n + 1)
                freed(pe, q0["ts_ready"], n)
                pe.nop(nofuse=True)
                by_edge(p_b[w], fs[w], q0["b_ready"])

            stepped(pe, [(front0, 0), (mid0, 1), (back0, 2)], NCH, 4)
            phase_end(pe, 2)

            for l in (1, 2):
                s = q12[l]
                width = P if l == 1 else F

                def front(n, k, u):
                    w = u % 2
                    pe.wait_ge(s["d_in"][u], 48 * k + 48)
                    pe.wait_ge(s["d_got"][u], 64 * k + 64)
                    freed(pe, s["g_ready"], n)
                    freed(pe, s["o_ready"], n)
                    pe.nop(nofuse=True)
                    for j in range(TPC):
                        last = nc.tensor.transpose(p_t[w][:, j * P:(j + 1) * P], fx3(u)[:, j, 0:P], ident[:, :])
                    last.then_inc(s["t_ready"], 1)

                def mid(n, k, u):
                    w = u % 2
                    pe.wait_ge(s["g_ready"], n + 1)
                    pe.wait_ge(s["o_ready"], n + 1)
                    freed(pe, s["s_ready"], n)
                    pe.nop(nofuse=True)
                    nc.tensor.matmul(p_p[w][0:width, :], w_o[l - 1][:, :], xt[w], start=True, stop=True).then_inc(s["p_ready"], 1)
                    freed(pe, s["gmax"], n)
                    pe.nop(nofuse=True)
                    by_edge(p_b[w], xt[w], s["gb_ready"])

                def back1(n, k, u):
                    w = u % 2
                    pe.wait_ge(s["scan"], n + 1)
                    freed(pe, s["ts_ready"], n)
                    pe.nop(nofuse=True)
                    by_edge(p_m[w], fs[w], s["fb_ready"])

                stepped(pe, [(front, 0), (mid, 1)] + ([(back1, 2)] if l == 1 else []), NCH, 4)
                phase_end(pe, l + 2)

            def by_edge3(n, k, u):
                w = u % 2
                pe.wait_ge(q3["scan"], n + 1)
                freed(pe, q3["gmax"], n)
                pe.nop(nofuse=True)
                by_edge(p_b[w], fs[w], q3["gb_ready"])

            def transpose3(n, k, u):
                w = u % 2
                pe.wait_ge(q3["y_ready"], n + 1)
                freed(pe, q3["yts"], n)
                pe.nop(nofuse=True)
                for j in range(TPC):
                    last = nc.tensor.transpose(p_t[w][0:F, j * P:(j + 1) * P], yy[u][:, j * F:(j + 1) * F], ident[:, :])
                last.then_inc(q3["yt_ready"], 1)

            def project3(n, k, u):
                w = u % 2
                pe.wait_ge(q3["yts"], n + 1)
                freed(pe, q3["zs"], n)
                pe.nop(nofuse=True)
                for j in range(TPC):
                    last = nc.tensor.matmul(p_m[w][:, j * F:(j + 1) * F], xt[w][0:F, j * P:(j + 1) * P], w_p[:, :],
                                            start=True, stop=True)
                last.then_inc(q3["z_ready"], 1)

            def sum3(n, k, u):
                w = u % 2
                pe.wait_ge(q3["zs"], n + 1)
                pe.wait_ge(q3["eq"], n + 1)
                freed(pe, q3["ga_ready"], n)
                pe.nop(nofuse=True)
                for j in range(TPC):
                    last = nc.tensor.matmul(p_p[w][:, j * F:(j + 1) * F], eq[w][:, j * P:(j + 1) * P],
                                            zs[w][:, j * F:(j + 1) * F], start=True, stop=True)
                last.then_inc(q3["sum_ready"], 1)

            stepped(pe, [(by_edge3, 0), (transpose3, 2), (project3, 2), (sum3, 4)], NCH, 4)
            phase_end(pe, 5)
            phase_end(pe, 6)

        @block.vector
        def _(ve):
            v = nc.vector
            chained = {}

            def link(ins, counter):
                chained[counter.name] = chained.get(counter.name, 0) + 1
                ins.then_inc(counter, 1)
                ve.wait_ge(counter, chained[counter.name])

            v.memset(n_dst, N)
            v.memset(n_src, N)
            v.memset(n_next, N)
            v.memset(n_ew, 0.0)
            link(v.memset(n_prev, N), c_v)
            v.memset(n_prev[0:1, 0:1], -1).then_inc(c_memset, 1)
            v.memset(ones, 1.0)
            v.memset(eps_ln[:, :], EPS_LN)
            v.memset(zero[:, :], 0.0)
            v.memset(fill[1][:, :], 0.0).then_inc(c_zero, 1)
            v.memset(oh_l[0], 0.0)
            v.memset(oh_h[0], 0.0).then_inc(h_made, 1)
            ve.wait_ge(c_nat, 16 * 11)
            ve.wait_ge(c_memset, 1)
            ve.wait_ge(c_pool, 4)
            v.tensor_tensor(n_same, n_dst, n_prev, ALU.is_equal).then_inc(c_same, 1)
            v.tensor_tensor(n_last, n_dst, n_next, ALU.not_equal)
            v.tensor_copy(n_srcf, n_src).then_inc(c_same, 1)
            link(v.tensor_copy(n_dstf, n_dst), c_v)
            link(v.tensor_tensor(n_dsts, n_dstf, n_dummy, ALU.subtract), c_v)
            link(v.tensor_tensor(n_dsts, n_dsts, n_last, ALU.mult), c_v)
            v.tensor_tensor(n_dsts, n_dsts, n_dummy, ALU.add).then_inc(c_rows, 1)
            ve.wait_ge(c_wts, 16 * 23)
            v.tensor_tensor(w_x[0:F, :], w_x[0:F, :], w_b[:, 0:3 * F], ALU.subtract)
            v.tensor_tensor(w_o[0][0:F, :], w_o[0][0:F, :], w_b[:, 3 * F:5 * F], ALU.subtract)
            v.tensor_tensor(w_o[1][0:F, :], w_o[1][0:F, :], w_b[:, 5 * F:6 * F], ALU.subtract)
            v.tensor_copy(byf(fill[0][:, :]), b_row.unsqueeze(1).to_broadcast([P, NFILL // P, F]))

            def column(q):
                return psum[:, q, 0:NT].rearrange("p (j c) -> p j c", c=NCH)

            def by_j(a):
                return a.rearrange("p (c j) -> p j c", j=TPC)

            ve.wait_ge(c_tr, 1)
            v.tensor_scalar(by_j(dst_g[:, :]), column(0), float(N - 1), None, ALU.min).then_inc(c_dst, 1)
            v.tensor_copy(by_j(lo_f), column(0))
            link(v.tensor_copy(by_j(hi_i), column(0)), c_v)
            link(v.tensor_scalar(hi_i, hi_i, 7, None, ALU.arith_shift_right), c_v)
            link(v.tensor_copy(hi_f, hi_i), c_v)
            link(v.scalar_tensor_tensor(out=lo_f, in0=hi_f, scalar=-float(P), in1=lo_f, op0=ALU.mult, op1=ALU.add), c_v)
            ve.wait_ge(c_tr, 4)
            v.tensor_copy(by_j(dst_s[:, :]), column(1))
            v.tensor_scalar(by_j(src_g[:, :]), column(2), float(N - 1), None, ALU.min)
            v.tensor_copy(by_j(src_f[:, :]), column(2))
            link(v.tensor_copy(by_j(ew[:, :]), column(3)), c_v)
            ve.wait_ge(c_out, 16 * 5)
            ve.wait_ge(c_pool, 10)

            def one_hot(n, k, u):
                ve.wait_ge(h_free, n if again(n, 1) else 1)
                v.tensor_scalar(oh_h[u], iota_h, hi_f[:, bass.ds(n, 1)], None, ALU.is_equal)
                v.tensor_scalar(oh_l[u], iota_l, lo_f[:, bass.ds(n, 1)], None, ALU.is_equal).then_inc(h_made, 1)

            stepped(ve, [(one_hot, 0)], NT)
            ve.wait_ge(h_free, NT + 1)

            def halves(a):
                return a.rearrange("p (b h) -> p b h", b=2)

            link(v.tensor_copy(halves(cnt), psum[:, 4:6, 0:HB]), h_v)
            link(v.memset(last_c, 0.0), h_v)
            ve.wait_ge(h_pe, 1)
            link(v.tensor_copy(halves(tot), psum[:, 2:4, 0:HB]), h_v)
            link(v.tensor_tensor_scan(run, last_c, tot, 0.0, ALU.add, ALU.add), h_v)
            link(v.tensor_tensor(run, run, tot, ALU.subtract), h_v)
            link(v.tensor_tensor(halves(run), halves(run), psum[:, 0:2, 0:HB], ALU.add), h_v)
            link(v.tensor_scalar(tot, cnt, 0.0, None, ALU.is_gt), h_v)
            link(v.scalar_tensor_tensor(out=last_c, in0=run, scalar=-1.0 - ZROW, in1=tot, op0=ALU.add, op1=ALU.mult), h_v)
            link(v.tensor_scalar(last_c, last_c, float(ZROW), None, ALU.add), h_v)
            link(v.tensor_tensor(first_c, run, cnt, ALU.subtract), h_v)
            link(v.scalar_tensor_tensor(out=first_c, in0=first_c, scalar=-float(ZROW), in1=tot, op0=ALU.add, op1=ALU.mult), h_v)
            link(v.tensor_scalar(first_c, first_c, float(ZROW), None, ALU.add), h_v)
            assert chained[h_v.name] == H_STEPS
            for b in range(NB):
                w = min(P, HI - b * P)
                ve.wait_ge(h_tr, b + 1)
                v.tensor_copy(pos_n[0:w, b * 2 * P:(b + 1) * 2 * P].rearrange("p (l q) -> p q l", q=2),
                              psum[0:w, 4 + b % 4, 0:2 * P].rearrange("p (q l) -> p q l", q=2)).then_inc(h_pos, 1)

            def nodes_ve(buffers, c0, g_of):
                hx, hh, sq, gm_a, st = buffers
                first0 = (A_FIRST + 1) // 2

                def center_a(k, kk, s_):
                    m = parts_of(g_of(k))
                    hv, c = byf(hx[s_])[0:m], c0 + k
                    ve.wait_ge(a_in[s_], 16 * (first0 + k) + 16 if c0 else 16 * kk + 16)
                    v.tensor_reduce(byf(gm_a[s_], 16)[0:m], hv.rearrange("p k (g q) -> p k g q", q=4), X, ALU.max).then_inc(a_v, 1)
                    ve.wait_ge(a_v, 3 * c + 1)
                    v.tensor_tensor(hv[:, :, 0:16], hv[:, :, 0:16], byf(gm_a[s_], 16)[0:m], ALU.add).then_inc(a_v, 1)
                    ve.wait_ge(a_v, 3 * c + 2)
                    v.tensor_reduce(st[s_][0:m, 0:NPP], hv, X, ALU.add).then_inc(a_v, 1)
                    ve.wait_ge(a_v, 3 * c + 3)
                    if c0:
                        ve.wait_ge(a_out[s_], 16 * (first0 + k))
                    v.scalar_tensor_tensor(out=byf(hh[s_])[0:m], in0=spread(st[s_][0:m, 0:NPP], F), scalar=-1.0 / F,
                                           in1=hv, op0=ALU.mult, op1=ALU.add).then_inc(a_sub, 1)

                def variance_a(k, kk, s_):
                    m = parts_of(g_of(k))
                    ve.wait_ge(a_sq, c0 + k + 1)
                    v.tensor_reduce(st[s_][0:m, NPP:2 * NPP], byf(sq[s_])[0:m], X, ALU.add).then_inc(a_var, 1)

                def scale_a(k, kk, s_):
                    m = parts_of(g_of(k))
                    ve.wait_ge(a_std, c0 + k + 1)
                    v.reciprocal(st[s_][0:m, 3 * NPP:4 * NPP], st[s_][0:m, 2 * NPP:3 * NPP]).then_inc(a_rec, 1)
                    ve.wait_ge(a_rec, c0 + k + 1)
                    v.tensor_tensor(byf(hh[s_])[0:m], byf(hh[s_])[0:m], spread(st[s_][0:m, 3 * NPP:4 * NPP], F),
                                    ALU.mult).then_inc(a_y, 1)

                return center_a, variance_a, scale_a

            center_a, variance_a, scale_a = nodes_ve(a_first, 0, first_group)
            stepped(ve, [(variance_a, 1), (center_a, 0), (scale_a, 1)], A_FIRST)
            phase_end(ve, 1)

            def scan(l, out_, before, data, flags, n, done):
                if isinstance(n, int) and n == 0:
                    start = zero[0:F, :]
                else:
                    ve.wait_ge(done, n)
                    start = end_col(before[0:F, :], l)
                ve.nop(nofuse=True)
                v.tensor_tensor_scan(back(out_[0:F, :], l), back(flags[0:F, :], l), back(data[0:F, :], l), start,
                                     ALU.mult, ALU.max).then_inc(done, 1)

            def add_max(l, n, u, src_rows, first, maxed, added):
                v.tensor_reduce(byf(gm[u], 16), src_rows.rearrange("p j (g q) -> p j g q", q=4), X, ALU.max).then_inc(maxed, 1)
                ve.wait_ge(maxed, n + 1)
                ve.nop(nofuse=True)
                ins = v.tensor_tensor(xl_at(l, n, first, first + 16), xl_at(l, n, first, first + 16), byf(gm[u], 16), ALU.add)
                if added is not None:
                    ins.then_inc(added, 1)

            def take0(n, k, u):
                w = u % 2
                ve.wait_ge(q0["d_got"][u], 64 * k + 64)
                ve.wait_ge(q0["xi"], n + 1)
                ve.nop(nofuse=True)
                for q in range(2):
                    v.tensor_copy(cols(pos_g[q], 0, n), fx3(u)[:, :, P + q])
                add_max(0, n, w, fx3(u)[:, :, 0:F], 0, q0["taken"], None)

            def scan0(n, k, u):
                w = u % 2
                ve.wait_ge(q0["d_in"][u], 16 * k + 16)
                ve.wait_ge(q0["ms_ready"], n + 1)
                freed(ve, q0["b_ready"], n)
                scan(0, fs[w], fs[1 - w], ms[w], sn[u], n, q0["scan"])

            center_a, variance_a, scale_a = nodes_ve(a_second, A_FIRST, second_group)
            nodes0 = in_fours({0: [(scale_a, -1)], 2: [(center_a, 0)], 3: [(variance_a, 0)]})
            stepped(ve, [(take0, 0), (scan0, 2), (nodes0, 0)], NCH, 4)
            phase_end(ve, 2)

            for l in (1, 2):
                s = q12[l]
                width = P if l == 1 else F

                def complete(n, k, u):
                    w = u % 2
                    ve.wait_ge(s["t_ready"], n + 1)
                    ve.wait_ge(s["d_in"][u], 48 * k + 48)
                    freed(ve, s["gb_ready"], n)
                    scan(l, xt[w], xt[1 - w], p_t[w], sn[u], n, s["g_ready"])

                def message(n, k, u):
                    w = u % 2
                    ve.wait_ge(s["p_ready"], n + 1)
                    if l == 1:
                        stored(ve, s["d_part"][w], n, 2 * k + u // 2)
                    v.tensor_tensor(ms[w][0:width, :], p_p[w][0:width, :], pl[u][0:width, :], ALU.add).then_inc(s["s_ready"], 1)
                    ve.wait_ge(s["s_ready"], n + 1)
                    if l == 1:
                        freed(ve, s["fb_ready"], n)
                    else:
                        stored(ve, s["d_table"][w], n, 2 * k + u // 2)
                    scan(l, fs[w], fs[1 - w], ms[w], sn[u], n, s["scan"])

                def maxima(n, k, u):
                    w = u % 2
                    ve.wait_ge(s["gb_ready"], n + 1)
                    add_max(l, n, w, byf(p_b[w][:, 0:TPC * F]), 16 * l, s["gmax"], None)

                stepped(ve, [(complete, 0), (message, 1), (maxima, 1)], NCH, 4)
                phase_end(ve, l + 2)

            def scan3(n, k, u):
                w = u % 2
                ve.wait_ge(q3["d_in"][u], 48 * k + 48)
                freed(ve, q3["gb_ready"], n)
                scan(3, fs[w], fs[1 - w], pl[u], sn[u], n, q3["scan"])

            def center3(n, k, u):
                w = u % 2
                ve.wait_ge(q3["gb_ready"], n + 1)
                add_max(3, n, w, byf(p_b[w][:, 0:TPC * F]), 48, q3["gmax"], q3["xl"])
                ve.wait_ge(q3["xl"], n + 1)
                ve.nop(nofuse=True)
                v.tensor_reduce(st3[w][:, 0:TPC], xl_at(3, n), X, ALU.add).then_inc(q3["ln"], 1)
                ve.wait_ge(q3["ln"], n + 1)
                stored(ve, q3["d_y"][u], n, k, 64, 4)
                freed(ve, q3["yt_ready"], n, depth=4)
                ve.nop(nofuse=True)
                v.scalar_tensor_tensor(out=byf(yy[u]), in0=spread(st3[w][:, 0:TPC], F), scalar=-1.0 / F,
                                       in1=xl_at(3, n), op0=ALU.mult, op1=ALU.add).then_inc(q3["sub"], 1)

            def same_src3(n, k, u):
                w = u % 2
                freed(ve, q3["sum_ready"], n)
                ve.nop(nofuse=True)
                eq3 = byf(eq[w], P)
                v.tensor_tensor(eq3, byf(sr[u], P), spread(cols(src_f, 3, n), P), ALU.is_equal).then_inc(q3["eq"], 1)
                ve.wait_ge(q3["eq"], n + 1)
                v.tensor_tensor(byf(eqm, P), eq3, mask[:, :, :], ALU.mult).then_inc(q3["eqc"], 1)
                ve.wait_ge(q3["eqc"], 3 * n + 1)
                v.tensor_reduce(dup, byf(eqm, P), X, ALU.max).then_inc(q3["eqc"], 1)
                ve.wait_ge(q3["eqc"], 3 * n + 2)
                ve.nop(nofuse=True)
                v.scalar_tensor_tensor(out=off, in0=cols(src_f, 3, n), scalar=dummy_f[:, :], in1=dup,
                                       op0=ALU.subtract, op1=ALU.mult).then_inc(q3["eqc"], 1)
                ve.wait_ge(q3["eqc"], 3 * n + 3)
                for q in range(2):
                    freed(ve, q3["d_add"][q], n, 32, 4)
                ve.nop(nofuse=True)
                v.tensor_tensor(add_i[u], cols(src_f, 3, n), off, ALU.subtract).then_inc(q3["add_i"], 1)

            def variance3(n, k, u):
                w = u % 2
                ve.wait_ge(q3["sq"], n + 1)
                v.tensor_reduce(st3[w][:, TPC:2 * TPC], byf(sq3[w]), X, ALU.add).then_inc(q3["var"], 1)

            def scale3(n, k, u):
                w = u % 2
                ve.wait_ge(q3["std"], n + 1)
                v.reciprocal(st3[w][:, 3 * TPC:4 * TPC], st3[w][:, 2 * TPC:3 * TPC]).then_inc(q3["rec"], 1)
                ve.wait_ge(q3["rec"], n + 1)
                v.tensor_tensor(byf(yy[u]), byf(yy[u]), spread(st3[w][:, 3 * TPC:4 * TPC], F), ALU.mult).then_inc(q3["y_ready"], 1)

            def weigh3(n, k, u):
                w = u % 2
                ve.wait_ge(q3["z_ready"], n + 1)
                freed(ve, q3["sum_ready"], n)
                ve.nop(nofuse=True)
                v.tensor_tensor(byf(zs[w]), byf(p_m[w][:, 0:TPC * F]), spread(cols(ew, 3, n), F), ALU.mult).then_inc(q3["zs"], 1)

            stepped(ve, [(scan3, 0), (center3, 1), (same_src3, 3), (variance3, 1), (weigh3, 3), (scale3, 1)], NCH, 4)
            phase_end(ve, 5)

            def sum_f(n, k, u):
                m = parts_of(n)
                ve.wait_ge(f_in[u], 48 * k + 48)
                v.tensor_tensor(dz[u][1][0:m, :], dz[u][1][0:m, :], dz[u][2][0:m, :], ALU.add).then_inc(f_sum, 1)

            def norm_f(n, k, u):
                m = parts_of(n)
                ve.wait_ge(f_sq1, n + 1)
                v.tensor_reduce(dst_d[u][0:m, 0:NPP], byf(dz[u][3])[0:m], X, ALU.add).then_inc(f_nrm, 1)

            def center_f(n, k, u):
                m = parts_of(n)
                st, hv = dst_d[u], byf(dz[u][1])[0:m]
                ve.wait_ge(f_std1, n + 1)
                v.tensor_scalar(st[0:m, 2 * NPP:3 * NPP], st[0:m, NPP:2 * NPP], EPS_NORM, None, ALU.max).then_inc(f_v, 1)
                ve.wait_ge(f_v, 5 * n + 1)
                v.reciprocal(st[0:m, 3 * NPP:4 * NPP], st[0:m, 2 * NPP:3 * NPP]).then_inc(f_v, 1)
                ve.wait_ge(f_v, 5 * n + 2)
                v.tensor_tensor(hv, hv, spread(st[0:m, 3 * NPP:4 * NPP], F), ALU.mult).then_inc(f_v, 1)
                ve.wait_ge(f_v, 5 * n + 3)
                v.tensor_tensor(hv, hv, byf(dz[u][0])[0:m], ALU.add).then_inc(f_v, 1)
                ve.wait_ge(f_v, 5 * n + 4)
                v.tensor_reduce(st[0:m, 6 * NPP:7 * NPP], hv, X, ALU.add).then_inc(f_v, 1)
                ve.wait_ge(f_v, 5 * n + 5)
                v.scalar_tensor_tensor(out=hv, in0=spread(st[0:m, 6 * NPP:7 * NPP], F), scalar=-1.0 / F, in1=hv,
                                       op0=ALU.mult, op1=ALU.add).then_inc(f_sub, 1)

            def variance_f(n, k, u):
                m = parts_of(n)
                ve.wait_ge(f_sq2, n + 1)
                v.tensor_reduce(dst_d[u][0:m, 4 * NPP:5 * NPP], byf(dz[u][3])[0:m], X, ALU.add).then_inc(f_var, 1)

            def scale_f(n, k, u):
                m = parts_of(n)
                ve.wait_ge(f_std2, n + 1)
                v.reciprocal(dst_d[u][0:m, 7 * NPP:8 * NPP], dst_d[u][0:m, 5 * NPP:6 * NPP]).then_inc(f_rec, 1)
                ve.wait_ge(f_rec, n + 1)
                v.tensor_tensor(byf(dz[u][1])[0:m], byf(dz[u][1])[0:m], spread(dst_d[u][0:m, 7 * NPP:8 * NPP], F),
                                ALU.mult).then_inc(f_y, 1)

            stepped(ve, [(sum_f, 0), (variance_f, 2), (norm_f, 0), (center_f, 1), (scale_f, 2)], NG + 1, DD)
            phase_end(ve, 6)


_INS = ["x", "src", "dst", "edge_weight", "L0_gnn_W0", "L0_gnn_b0", "L0_gnn_W1", "L0_gnn_b1", "L0_gnn_W2",
        "L0_gnn_b2", "L1_gnn_weight", "L1_gnn_bias"]
_OUTS = [((N, F), "float32")]


def kernel(**inputs):
    import numpy as _np
    import concourse.bacc as _bacc
    from concourse import mybir as _mybir
    from concourse.bass_utils import run_bass_kernel_spmd as _run

    nc = _bacc.Bacc("TRN2", target_bir_lowering=False, num_devices=1)
    arrays, args = {}, []
    for name in _INS:
        a = _np.ascontiguousarray(inputs[name])
        arrays[f"in_{name}_dram"] = a
        args.append(nc.dram_tensor(f"in_{name}_dram", a.shape, _mybir.dt.from_np(a.dtype), kind="ExternalInput").ap())
    for i, (shape, dtype) in enumerate(_OUTS):
        dt = _mybir.dt.from_np(_np.dtype(dtype))
        args.append(nc.dram_tensor(f"out_{i}_dram", shape, dt, kind="ExternalOutput").ap())
    build(nc, *args)
    r = _run(nc, [arrays], core_ids=[0])
    return r.results[0]["out_0_dram"]
```

```python
from contextlib import ExitStack

import numpy as np

import concourse.bass as bass
from concourse import mybir

FP32, BF16, FP16, I32 = mybir.dt.float32, mybir.dt.bfloat16, mybir.dt.float16, mybir.dt.int32
ALU = mybir.AluOpType
ACT = mybir.ActivationFunctionType
X = mybir.AxisListType.X

P = 128
N = 100000
E = 50000
F = 64
TPC = 4
CH = TPC * P
NCH = -(-E // CH)
NCH += NCH % 2
NT = NCH * TPC
EP = NCH * CH
LAST_ROW = E - (NCH - 1) * CH
HI = -(-N // P)
HB = HI // 2
NB = -(-HI // P)
NFILL = 1024
NTAB = NFILL * NCH
Z_REP = 2
Z_LATE = 3
DUMMY = N + 1
ZROW = EP
ROW = F + 2
NPP = 16
GR = P * NPP
NG = N // GR
A_STEPS = NCH // 4
RP = (N - NG * GR) // NPP
EPS_LN = 1e-5
EPS_NORM = 1e-12
H_STEPS = 12
assert NG == 2 * A_STEPS and HI % 2 == 0 and RP * NPP == N - NG * GR and NTAB >= DUMMY + P and 0 < LAST_ROW < CH


def stepped(eng, stages, total, depth=2):
    skew = max(late for _, late in stages)
    lead = -(-(skew + depth) // depth) * depth
    whole = total - total % depth

    def at(s):
        for fn, late in stages:
            n = s - late
            if 0 <= n < total:
                fn(n, n // depth, n % depth)

    for s in range(lead):
        at(s)
    with eng.Fori(lead // depth, whole // depth) as i:
        for v in range(depth):
            for fn, late in stages:
                fn(depth * i + (v - late), i + (v - late) // depth, (v - late) % depth)
    for s in range(whole, total + skew):
        at(s)


def again(n, depth=2):
    return not isinstance(n, int) or n >= depth


def freed(eng, semaphore, n, per=1, depth=2):
    if again(n, depth):
        eng.wait_ge(semaphore, per * (n - depth + 1))


def stored(eng, semaphore, n, k, amount=16, depth=2):
    if again(n, depth):
        eng.wait_ge(semaphore, amount * k)


def build(nc, x, src, dst, edge_weight, w0, b0, w1, b1, w2, b2, w_l1, b_l1, out):
    with ExitStack() as ctx:
        def sb(name, shape, dt=FP32):
            return ctx.enter_context(nc.sbuf_tensor(name, shape, dt))

        def sem(name):
            return ctx.enter_context(nc.semaphore(name))

        def dram(name, shape, dt=FP32):
            return nc.dram_tensor(name, shape, dt).ap()

        xpos = dram("xpos", (N, ROW))
        pos_d = dram("pos_d", (HI * P, 2))
        same_d = dram("same_d", (EP + CH,))
        srcf_d = dram("srcf_d", (EP,))
        part_d = dram("part_d", (P, EP))
        tables = [dram("table0", (EP + 1, F)), dram("table1", (EP + 1, F))]
        o2_d = dram("o2_d", (F, EP))
        y1_d = dram("y1_d", (NTAB, F))
        agg_d = [dram("agg0", (NTAB, F)), dram("agg1", (NTAB, F))]

        xl = sb("xl", [P, NT * F])
        dst_g = sb("dst_g", [P, NT], I32)
        dst_s = sb("dst_s", [P, NT], I32)
        src_g = sb("src_g", [P, NT], I32)
        src_f = sb("src_f", [P, NT])
        ew = sb("ew", [P, NT])
        pos_g = [sb("last_g", [P, NT], I32), sb("first_g", [P, NT], I32)]
        ident = sb("ident", [P, P])
        w_x = sb("w_x", [P, 3 * F])
        w_o = [sb("w_o0", [P, 2 * F]), sb("w_o1", [P, F])]
        w_p = sb("w_p", [F, F])
        bias0 = sb("bias0", [F, 1])
        bias12 = sb("bias12", [P, 1])
        fill = [sb("fill0", [P, NFILL // P * F]), sb("fill1", [P, NFILL // P * F])]
        eps_ln = sb("eps_ln", [P, 1])
        zero = sb("zero", [P, 1])
        mask = sb("mask", [P, TPC, P])
        dummy_f = sb("dummy_f", [P, 1])
        idx_w = sb("idx_w", [P, 4, TPC], I32)

        work_words = 18432
        work = sb("work", [P, work_words])
        place = [0]

        def carve(words):
            place[0] += words
            assert place[0] <= work_words, place[0]
            return work[:, place[0] - words:place[0]]

        psum = ctx.enter_context(nc.psum_tensor("psum", [P, 8, 512], FP32))
        p_t = [psum[:, 0, :], psum[:, 1, :]]
        p_m = [psum[:, 2, :], psum[:, 3, :]]
        p_p = [psum[:, 4, :], psum[:, 5, :]]
        p_b = [psum[:, 6, :], psum[:, 7, :]]

        phase_done = sem("phase_done")

        def phase_end(eng, n):
            eng.drain().then_inc(phase_done, 1)
            eng.wait_ge(phase_done, 5 * n)
            eng.nop(nofuse=True)

        n_dst, n_prev, n_next, n_src = (carve(CH)[0:NCH, :].bitcast(I32) for _ in range(4))
        n_ew, n_same, n_last, n_dummy, n_dstf, n_srcf, n_dsts = (carve(CH)[0:NCH, :] for _ in range(7))
        end_natural = place[0]
        w_b = carve(6 * F)[0:F, :]
        b_row = carve(F)
        hi_i = carve(NT).bitcast(I32)
        hi_f = carve(NT)
        lo_f = carve(NT)
        iota_h = carve(HB).bitcast(FP16)
        iota_l = carve(F).bitcast(FP16)
        at_onehots = place[0]
        oh_h = [carve(HB).bitcast(BF16) for _ in range(8)]
        oh_l = [carve(F).bitcast(BF16) for _ in range(8)]
        end_onehots = place[0]
        place[0] = at_onehots
        xs = [carve(NPP * ROW) for _ in range(2)]
        place[0] = max(place[0], end_onehots)
        upper = carve(P)
        ones = carve(P)
        pos_n = carve(NB * P * 2)
        def a_buffers():
            return [carve(width) for width in (NPP * F, NPP * F, NPP * F, NPP * 16, NPP * 4)]

        xi = [carve(TPC * F) for _ in range(4)]
        place[0] = 0
        cnt, tot, run, last_c, first_c = (carve(HI) for _ in range(5))
        assert place[0] <= end_natural
        place[0] = 0
        xb = [carve(NPP * F) for _ in range(4)]
        ps = [carve(NPP * 2) for _ in range(4)]
        assert place[0] <= end_natural

        place[0] = 0
        fx = [carve(TPC * (P + 2)) for _ in range(4)]
        xt = [carve(CH) for _ in range(2)]
        ms = [carve(CH) for _ in range(2)]
        fs = [carve(CH) for _ in range(2)]
        sn = [carve(CH) for _ in range(4)]
        pl = [carve(CH) for _ in range(4)]
        ts = [carve(TPC * F) for _ in range(2)]
        gm = [carve(TPC * 16) for _ in range(2)]
        before_p3 = place[0]
        yy = [carve(TPC * F) for _ in range(4)]
        st3 = [carve(TPC * 4) for _ in range(2)]
        zs = [carve(TPC * F) for _ in range(2)]
        ga = [m[:, q * TPC * F:(q + 1) * TPC * F] for m in ms for q in range(2)]
        sq3 = ts
        eq = [carve(CH) for _ in range(2)]
        sr = [carve(CH) for _ in range(4)]
        eqm = carve(CH)
        dup = carve(TPC)
        off = carve(TPC)
        add_i = [carve(TPC).bitcast(I32) for _ in range(4)]
        place[0] = before_p3
        a_passes = a_buffers()

        DD = 8
        dz = [[xl[:, (3 * u + q) * NPP * F:(3 * u + q + 1) * NPP * F] for q in range(3)] for u in range(DD)]
        dst_d = [work[:, u * 8 * NPP:(u + 1) * 8 * NPP] for u in range(DD)]

        def fx3(u):
            return fx[u].rearrange("p (j f) -> p j f", f=P + 2)

        def byf(a, f=F):
            return a.rearrange("p (j f) -> p j f", f=f)

        def spread(a, width):
            return a.unsqueeze(2).to_broadcast([a.shape[0], a.shape[1], width])

        def at_chunk(l, n):
            return n if l in (0, 2) else (NCH - 1) - n

        def e0(l, n):
            return at_chunk(l, n) * CH

        def cols(a, l, n):
            return a[:, bass.ds(at_chunk(l, n) * TPC, TPC)]

        def xl_at(l, n, a=0, b=F):
            return byf(xl[:, bass.ds(at_chunk(l, n) * (TPC * F), TPC * F)])[:, :, a:b]

        def rows(t, l, n):
            return t[bass.ds(e0(l, n), CH), :].rearrange("(j p) f -> p j f", p=P)

        def parts_of(n):
            return RP if isinstance(n, int) and n == NG else P

        def group(t, n):
            return t[bass.ds(n * GR, parts_of(n) * NPP), :].rearrange("(p k) f -> p (k f)", k=NPP)

        def nodes_of(phase, k):
            if phase == 1:
                return NG * GR, NPP, RP, 0
            if phase == 2:
                return k * GR, NPP, P, 1
            return A_STEPS * GR + ((phase - 3) * A_STEPS + k) * (GR // 2), NPP // 2, P, 1 + (phase - 2) * A_STEPS + k

        def before(phase, k):
            return 0 if phase == 1 else 1 + (phase - 2) * A_STEPS + k

        def node_rows(t, phase, k):
            first, per, m, _ = nodes_of(phase, k)
            return t[bass.ds(first, m * per), :].rearrange("(p k) f -> p (k f)", k=per)

        def in_fours(phase, what):
            def stage(n, k, u):
                for fn, late in what.get(u, ()):
                    if not isinstance(k, int) or 0 <= k + late < A_STEPS:
                        fn(phase, k + late)
            return stage

        def uses(u):
            return (NCH + 3 - u) // 4

        def back(a, l):
            return a[:, ::-1] if l in (1, 3) else a

        def end_col(a, l):
            return a[:, 0:1] if l in (1, 3) else a[:, CH - 1:CH]

        c_memset, c_zero, c_nat, c_wts, c_pool = sem("c_memset"), sem("c_zero"), sem("c_nat"), sem("c_wts"), sem("c_pool")
        c_v, c_same, c_rows, c_out, c_tr, c_dst = sem("c_v"), sem("c_same"), sem("c_rows"), sem("c_out"), sem("c_tr"), sem("c_dst")
        window_ready = sem("window_ready")
        x_got, x_put = [sem(f"x_got{u}") for u in range(4)], [sem(f"x_put{u}") for u in range(4)]
        h_free, h_made, h_v, h_pe, h_tr, h_pos, h_out = (sem(f"h_{t}") for t in ("free", "made", "v", "pe", "tr", "pos", "out"))
        b_in, b_out = [sem(f"b_in{u}") for u in range(4)], [sem("b_out0"), sem("b_out1")]
        b_row_made = sem("b_row_made")
        z_fill = sem("z_fill")
        a_in, a_out = sem("a_in"), sem("a_out")
        a_v, a_sub, a_sq, a_var, a_std, a_rec, a_y = (sem(f"a_{t}") for t in ("v", "sub", "sq", "var", "std", "rec", "y"))

        def sems(tag, plain, dmas2, dmas4):
            made = {t: sem(f"{tag}_{t}") for t in plain.split()}
            made.update({t: [sem(f"{tag}_{t}{u}") for u in range(2)] for t in dmas2.split()})
            made.update({t: [sem(f"{tag}_{t}{u}") for u in range(4)] for t in dmas4.split()})
            return made

        q0 = sems("q0", "xi t_ready xt_ready m_ready ms_ready p_ready part_ready scan taken b_ready ts_ready",
                  "d_part d_table", "d_in d_got")
        q12 = {l: sems(f"q{l}", "t_ready g_ready o_ready p_ready s_ready scan gb_ready gmax",
                       "d_table", "d_got") for l in (1, 2)}
        q12_in = [sem(f"q12_in{u}") for u in range(4)]
        q12[1].update(sems("q1", "fb_ready ts_ready", "d_part", ""))
        q3 = sems("q3", "scan gb_ready gmax sub sq var std y_ready yt_ready yts z_ready zs eq eqc "
                  "add_i sum_ready ga_ready", "d_add", "d_in d_y")
        f_in, f_out = ([sem(f"f_{t}{u}") for u in range(DD)] for t in ("in", "out"))
        f_sum, f_nrm, f_std1, f_unit, f_h, f_sub, f_sq2, f_var, f_std2, f_y = (
            sem(f"f_{t}") for t in ("sum", "nrm", "std1", "unit", "h", "sub", "sq2", "var", "std2", "y"))

        block = ctx.enter_context(nc.Block())

        @block.sync
        def _(sp):
            full = (NCH - 1) * CH

            def row(a):
                return a.rearrange("(c k) -> c k", c=1)

            sp.wait_ge(c_memset, 1)
            for tile, array in ((n_dst, dst), (n_src, src), (n_ew, edge_weight)):
                sp.dma_start(tile[0:NCH - 1, :], array[0:full].rearrange("(c k) -> c k", k=CH)).then_inc(c_nat, 16)
                sp.dma_start(tile[NCH - 1:NCH, 0:LAST_ROW], row(array[full:E])).then_inc(c_nat, 16)
            sp.dma_start(n_prev[0:1, 1:CH], row(dst[0:CH - 1])).then_inc(c_nat, 16)
            sp.dma_start(n_prev[1:NCH - 1, :], dst[CH - 1:full - 1].rearrange("(c k) -> c k", k=CH)).then_inc(c_nat, 16)
            sp.dma_start(n_prev[NCH - 1:NCH, 0:LAST_ROW + 1], row(dst[full - 1:E])).then_inc(c_nat, 16)
            sp.dma_start(n_next[0:NCH - 1, :], dst[1:full + 1].rearrange("(c k) -> c k", k=CH)).then_inc(c_nat, 16)
            sp.dma_start(n_next[NCH - 1:NCH, 0:LAST_ROW - 1], row(dst[full + 1:E])).then_inc(c_nat, 16)
            blocks = ((w0, 0, F, w_x, 0), (w1, 0, 2 * F, w_x, 1), (w2, 0, 3 * F, w_x, 2),
                      (w1, F, 3 * F, w_o[0], 0), (w2, F, 4 * F, w_o[0], 1), (w2, 2 * F, 5 * F, w_o[1], 0))
            for q, (w, a, b, tile, at) in enumerate(blocks):
                sp.dma_start(tile[0:F, at * F:(at + 1) * F], w[a:a + F, :]).then_inc(c_wts, 16)
                sp.dma_start(tile[F:P, at * F:(at + 1) * F], w[b:b + F, :]).then_inc(c_wts, 16)
                sp.dma_start(w_b[:, q * F:(q + 1) * F], w[b:b + F, :]).then_inc(c_wts, 16)
            sp.dma_start(w_p[:, :], w_l1[:, :]).then_inc(c_wts, 16)
            sp.dma_start(bias0[:, :], b0.rearrange("(p a) -> p a", a=1)).then_inc(c_wts, 16)
            sp.dma_start(bias12[0:F, :], b1.rearrange("(p a) -> p a", a=1)).then_inc(c_wts, 16)
            sp.dma_start(bias12[F:P, :], b2.rearrange("(p a) -> p a", a=1)).then_inc(c_wts, 16)
            sp.dma_start(b_row, b_l1.partition_broadcast(P)).then_inc(c_wts, 16)
            sp.wait_ge(c_zero, 1)
            for t in tables:
                sp.dma_start(t[ZROW:ZROW + 1, :], fill[1][0:1, 0:F]).then_inc(c_out, 16)
            sp.dma_start(row(same_d[EP:EP + CH]), fill[1][0:1, 0:CH]).then_inc(c_out, 16)
            sp.wait_ge(c_same, 2)
            sp.dma_start(same_d[0:EP].rearrange("(c k) -> c k", k=CH), n_same).then_inc(c_out, 16)
            sp.dma_start(srcf_d.rearrange("(c k) -> c k", k=CH), n_srcf).then_inc(c_out, 16)

            def put(n, k, u):
                sp.wait_ge(x_got[u], 64 * k + 64)
                sp.nop(nofuse=True)
                sp.dma_start(xl[:, bass.ds(n * (TPC * F), TPC * F)], xi[u]).then_inc(x_put[u], 16)

            stepped(sp, [(put, 0)], NCH, 4)
            sp.wait_ge(c_out, 16 * 5)
            for u in range(4):
                sp.wait_ge(x_put[u], 16 * uses(u))
            phase_end(sp, 1)

            def load0(n, k, u):
                freed(sp, q0["scan"], n, depth=4)
                sp.nop(nofuse=True)
                sp.dma_start(sn[u][0:F, :], same_d[bass.ds(e0(0, n), CH)].partition_broadcast(F)).then_inc(q0["d_in"][u], 16)

            stepped(sp, [(load0, 0)], NCH, 4)
            phase_end(sp, 2)

            for l in (1, 2):
                s = q12[l]

                def load(n, k, u):
                    freed(sp, s["scan"], n, depth=4)
                    freed(sp, s["t_ready"], n, depth=4)
                    sp.nop(nofuse=True)
                    sp.dma_start(fx3(u)[:, :, 0:F], rows(tables[l - 1], l, n)).then_inc(q12_in[u], 16)
                    ahead = 1 if l == 1 else 0
                    sp.dma_start(sn[u][0:F, :], same_d[bass.ds(e0(l, n) + ahead, CH)].partition_broadcast(F)).then_inc(q12_in[u], 16)
                    part = part_d[:, bass.ds(e0(l, n), CH)] if l == 1 else part_d[F:P, bass.ds(e0(l, n), CH)]
                    sp.dma_start(pl[u] if l == 1 else pl[u][0:F, :], part).then_inc(q12_in[u], 16)

                stepped(sp, [(load, 0)], NCH, 4)
                phase_end(sp, l + 2)

            def load3(n, k, u):
                freed(sp, q3["scan"], n, depth=4)
                sp.nop(nofuse=True)
                sp.dma_start(sn[u][0:F, :], same_d[bass.ds(e0(3, n) + 1, CH)].partition_broadcast(F)).then_inc(q3["d_in"][u], 16)
                sp.dma_start(pl[u][0:F, :], o2_d[:, bass.ds(e0(3, n), CH)]).then_inc(q3["d_in"][u], 16)
                freed(sp, q3["eq"], n, depth=4)
                sp.nop(nofuse=True)
                sp.dma_start(sr[u], srcf_d[bass.ds(e0(3, n), CH)].partition_broadcast(P)).then_inc(q3["d_in"][u], 16)

            stepped(sp, [(load3, 0)], NCH, 4)
            phase_end(sp, 5)

            def load_f(n, k, u):
                stored(sp, f_out[u], n, k, depth=DD)
                sp.nop(nofuse=True)
                for q, t in enumerate((y1_d, agg_d[0], agg_d[1])):
                    sp.dma_start(dz[u][q][0:parts_of(n), :], group(t, n)).then_inc(f_in[u], 16)

            stepped(sp, [(load_f, 0)], NG + 1, DD)
            phase_end(sp, 6)

        @block.gpsimd
        def _(gp):
            def iota(out_, pattern, base, channel):
                gp.iota(out_, pattern=pattern, base=base, channel_multiplier=channel,
                        allow_small_or_imprecise_dtypes=True).then_inc(c_pool, 1)

            gp.memset(ident[:, :], 0.0).then_inc(c_pool, 1)
            gp.memset(mask[:, :, :], 1.0).then_inc(c_pool, 1)
            gp.memset(upper, 1.0).then_inc(c_pool, 1)
            iota(n_dummy.rearrange("p (j k) -> p j k", k=P), [[0, TPC], [1, P]], DUMMY, 0)
            gp.wait_ge(c_pool, 3)
            gp.affine_select(out=ident[:, :], in_=ident[:, :], compare_op=ALU.not_equal, fill=1.0, base=0,
                             pattern=[[-1, P]], channel_multiplier=1).then_inc(c_pool, 1)
            iota(iota_h, [[1, HI]], 0, 0)
            iota(iota_l, [[1, P]], 0, 0)
            iota(dummy_f[:, :], [[0, 1]], DUMMY, 1)
            gp.affine_select(out=mask[:, :, :], in_=mask[:, :, :], compare_op=ALU.is_gt, fill=0.0, base=0,
                             pattern=[[0, TPC], [-1, P]], channel_multiplier=1).then_inc(c_pool, 1)
            gp.affine_select(out=upper, in_=upper, compare_op=ALU.is_ge, fill=0.0, base=0,
                             pattern=[[1, P]], channel_multiplier=-1).then_inc(c_pool, 1)

            gp.wait_ge(c_dst, 1)
            gp.nop(nofuse=True)

            def window(column, l, n, u, use):
                gp.tensor_copy(idx_w[:, u, :], cols(column, l, n)).then_inc(window_ready, 1)
                gp.wait_ge(window_ready, use * NCH + n + 1)
                gp.nop(nofuse=True)

            def fetch(out_, table, u, j, done):
                gp.indirect_dma_start(out_, None, table[:, :],
                                      bass.IndirectOffsetOnAxis(ap=idx_w[:, u, j:j + 1], axis=0)).then_inc(done, 16)

            def gather_x(n, k, u):
                stored(gp, x_put[u], n, k, depth=4)
                gp.nop(nofuse=True)
                window(dst_g, 0, n, u, 0)
                for j in range(TPC):
                    fetch(xi[u][:, j * F:(j + 1) * F], x, u, j, x_got[u])

            stepped(gp, [(gather_x, 0)], NCH, 4)
            phase_end(gp, 1)

            def gather0(n, k, u):
                freed(gp, q0["t_ready"], n, depth=4)
                freed(gp, q0["taken"], n, depth=4)
                gp.nop(nofuse=True)
                window(src_g, 0, n, u, 1)
                for j in range(TPC):
                    fetch(fx3(u)[:, j, F:P + 2], xpos, u, j, q0["d_got"][u])

            stepped(gp, [(gather0, 0)], NCH, 4)
            phase_end(gp, 2)

            for l in (1, 2):
                s = q12[l]

                def gather(n, k, u):
                    freed(gp, s["t_ready"], n, depth=4)
                    gp.nop(nofuse=True)
                    window(pos_g[l - 1], l, n, u, l + 1)
                    for j in range(TPC):
                        fetch(fx3(u)[:, j, F:P], tables[l - 1], u, j, s["d_got"][u])

                stepped(gp, [(gather, 0)], NCH, 4)
                phase_end(gp, l + 2)

            def add(m, w, j):
                if j >= 2 or not isinstance(m, int) or m > 0:
                    gp.wait_ge(q3["d_add"][j % 2], 16 * (2 * m + j // 2))
                    gp.nop(nofuse=True)
                gp.indirect_dma_start(agg_d[j % 2][:, :], bass.IndirectOffsetOnAxis(ap=add_i[w][:, j:j + 1], axis=0),
                                      ga[w][:, j * F:(j + 1) * F], None, compute_op=ALU.add).then_inc(q3["d_add"][j % 2], 16)

            def scatter(n, k, u):
                z = (u - Z_LATE) % 4
                some_y = not isinstance(n, int) or n < NCH
                some_z = not isinstance(n, int) or n >= Z_LATE
                if some_y:
                    gp.wait_ge(q3["y_ready"], 2 * n + 2)
                    stored(gp, q3["d_y"][u], n, k, 64, 4)
                    gp.nop(nofuse=True)
                    window(dst_s, 3, n, u, 4)
                if some_z:
                    gp.wait_ge(q3["ga_ready"], n - Z_LATE + 1)
                    gp.wait_ge(q3["add_i"], n - Z_LATE + 1)
                    gp.nop(nofuse=True)
                for j in (0, 2):
                    if some_z:
                        add(n - Z_LATE, z, j)
                        add(n - Z_LATE, z, j + 1)
                    if some_y:
                        for q in (j, j + 1):
                            gp.indirect_dma_start(y1_d[:, :], bass.IndirectOffsetOnAxis(ap=idx_w[:, u, q:q + 1], axis=0),
                                                  yy[u][:, q * F:(q + 1) * F], None, bounds_check=N - 1,
                                                  oob_is_err=False).then_inc(q3["d_y"][u], 16)

            stepped(gp, [(scatter, 0)], NCH, 4)
            for n in range(NCH, NCH + Z_LATE):
                scatter(n, n // 4, n % 4)
            for u in range(4):
                gp.wait_ge(q3["d_y"][u], 64 * ((NCH + 3 - u) // 4))
            for q in range(2):
                gp.wait_ge(q3["d_add"][q], 32 * NCH)
            phase_end(gp, 5)

            def sum_f(n, k, u):
                m = parts_of(n)
                gp.wait_ge(f_in[u], 48 * k + 48)
                gp.nop(nofuse=True)
                gp.tensor_tensor(dz[u][1][0:m, :], dz[u][1][0:m, :], dz[u][2][0:m, :], ALU.add).then_inc(f_sum, 1)

            def residual_f(n, k, u):
                m = parts_of(n)
                gp.wait_ge(f_unit, 3 * n + 3)
                gp.nop(nofuse=True)
                gp.tensor_tensor(dz[u][1][0:m, :], dz[u][1][0:m, :], dz[u][0][0:m, :], ALU.add).then_inc(f_h, 1)

            stepped(gp, [(sum_f, 0), (residual_f, 1)], NG + 1, DD)
            phase_end(gp, 6)

        @block.scalar
        def _(act):
            act.wait_ge(c_zero, 2)

            def clear(q, fills, before_):
                def stage(n, k, u):
                    if again(n, 1):
                        act.wait_ge(z_fill, 16 * (before_ + n))
                    act.nop(nofuse=True)
                    rows_n = agg_d[q][bass.ds(n * fills * NFILL, fills * NFILL), :]
                    act.dma_start(rows_n.rearrange("(r p k) f -> p r (k f)", r=fills, p=P),
                                  fill[q][:, :].unsqueeze(1).to_broadcast([P, fills, NFILL // P * F])).then_inc(z_fill, 16)
                return stage

            stepped(act, [(clear(0, Z_REP, 0), 0)], NCH // Z_REP)

            for b in range(NB):
                w = min(P, HI - b * P)
                act.wait_ge(h_pos, b + 1)
                act.dma_start(pos_d[b * P * P:(b * P + w) * P, :].rearrange("(h l) q -> h (l q)", l=P),
                              pos_n[0:w, b * 2 * P:(b + 1) * 2 * P]).then_inc(h_out, 16)
            act.wait_ge(h_out, 16 * NB)

            def groups_b(k, s_):
                for q in range(2):
                    if not isinstance(k, int) or 2 * k + q <= NG:
                        yield q, 2 * k + q, 2 * s_ + q

            def load_b(k, kk, s_):
                for q, g, b in groups_b(k, s_):
                    m = parts_of(g)
                    if again(k):
                        act.wait_ge(b_row_made, 2 * g - 6)
                    act.nop(nofuse=True)
                    act.dma_start(xb[b][0:m, :], group(x, g)).then_inc(b_in[b], 16)
                    act.dma_start(ps[b][0:m, :], group(pos_d, g)).then_inc(b_in[b], 16)

            def row_b(k, kk, s_):
                for q, g, b in groups_b(k, s_):
                    m = parts_of(g)
                    act.wait_ge(b_in[b], 32 * kk + 32)
                    if again(k, 1):
                        act.wait_ge(b_out[q], 16 * k)
                    act.nop(nofuse=True)
                    act.activation(byf(xs[q], ROW)[0:m, :, 0:F], byf(xb[b])[0:m], ACT.Copy).then_inc(b_row_made, 1)
                    act.activation(byf(xs[q], ROW)[0:m, :, F:ROW], byf(ps[b], 2)[0:m], ACT.Copy).then_inc(b_row_made, 1)
                    act.wait_ge(b_row_made, 2 * g + 2)
                    act.nop(nofuse=True)
                    act.dma_start(group(xpos, g), xs[q][0:m, :]).then_inc(b_out[q], 16)

            def node_steps(buffers):
                hx, hh, sq, _, st = buffers

                def load_a(phase, k):
                    _, per, m, _ = nodes_of(phase, k)
                    if phase > 1:
                        act.wait_ge(a_sub, before(phase, k))
                        act.nop(nofuse=True)
                    act.dma_start(hx[0:m, 0:per * F], node_rows(x, phase, k)).then_inc(a_in, 16)

                def square_a(phase, k):
                    _, per, m, _ = nodes_of(phase, k)
                    act.wait_ge(a_sub, before(phase, k) + 1)
                    act.nop(nofuse=True)
                    act.activation(sq[0:m, 0:per * F], hh[0:m, 0:per * F], ACT.Square).then_inc(a_sq, 1)

                def root_a(phase, k):
                    _, per, m, _ = nodes_of(phase, k)
                    act.wait_ge(a_var, before(phase, k) + 1)
                    act.nop(nofuse=True)
                    act.activation(st[0:m, 2 * NPP:2 * NPP + per], st[0:m, NPP:NPP + per], ACT.Sqrt,
                                   bias=eps_ln[0:m, :], scale=1.0 / F).then_inc(a_std, 1)

                def store_a(phase, k):
                    _, per, m, _ = nodes_of(phase, k)
                    act.wait_ge(a_y, before(phase, k) + 1)
                    act.nop(nofuse=True)
                    act.dma_start(node_rows(y1_d, phase, k), hh[0:m, 0:per * F]).then_inc(a_out, 16)

                return load_a, square_a, root_a, store_a

            def nodes_stage(phase):
                load_a, square_a, root_a, store_a = node_steps(a_passes)
                return in_fours(phase, {0: [(load_a, 0)], 1: [(store_a, -1)], 2: [(square_a, 0)], 3: [(root_a, 0)]})

            stepped(act, [(load_b, 0), (row_b, 1)], (NG + 2) // 2)
            for q in range(2):
                act.wait_ge(b_out[q], 16 * (NG // 2 + 1 - q))
            act.wait_ge(z_fill, 16 * (NCH // Z_REP))
            phase_end(act, 1)

            def xi0(n, k, u):
                freed(act, q0["t_ready"], n, depth=4)
                freed(act, q0["taken"], n, depth=4)
                act.nop(nofuse=True)
                act.activation(fx3(u)[:, :, 0:F], xl_at(0, n), ACT.Copy).then_inc(q0["xi"], 1)

            def front0(n, k, u):
                w = u % 2
                act.wait_ge(q0["t_ready"], n + 1)
                freed(act, q0["p_ready"], n)
                act.nop(nofuse=True)
                act.activation(xt[w], p_t[w], ACT.Copy).then_inc(q0["xt_ready"], 1)

            def mid0(n, k, u):
                w = u % 2
                act.wait_ge(q0["m_ready"], n + 1)
                freed(act, q0["scan"], n)
                act.nop(nofuse=True)
                act.activation(ms[w][0:F, :], p_m[w][0:F, :], ACT.Identity, bias=bias0[:, :]).then_inc(q0["ms_ready"], 1)
                act.wait_ge(q0["p_ready"], n + 1)
                stored(act, q0["d_part"][w], n, 2 * k + u // 2)
                act.nop(nofuse=True)
                act.activation(pl[w], p_p[w], ACT.Identity, bias=bias12[:, :]).then_inc(q0["part_ready"], 1)

            def back0(n, k, u):
                w = u % 2
                act.wait_ge(q0["part_ready"], n + 1)
                act.nop(nofuse=True)
                act.dma_start(part_d[:, bass.ds(e0(0, n), CH)], pl[w]).then_inc(q0["d_part"][w], 16)
                act.wait_ge(q0["b_ready"], n + 1)
                stored(act, q0["d_table"][w], n, 2 * k + u // 2)
                act.nop(nofuse=True)
                act.activation(ts[w], p_b[w][:, 0:TPC * F], ACT.Copy).then_inc(q0["ts_ready"], 1)

            def out0(n, k, u):
                w = u % 2
                act.wait_ge(q0["ts_ready"], n + 1)
                act.nop(nofuse=True)
                act.dma_start(rows(tables[0], 0, n), byf(ts[w])).then_inc(q0["d_table"][w], 16)

            for fn in node_steps(a_passes):
                fn(1, 0)
            stepped(act, [(xi0, 0), (front0, 1), (mid0, 2), (out0, 4), (back0, 3), (nodes_stage(2), 0)], NCH, 4)
            for w in range(2):
                act.wait_ge(q0["d_part"][w], 16 * (NCH // 2))
                act.wait_ge(q0["d_table"][w], 16 * (NCH // 2))
            act.wait_ge(a_out, 16 * before(3, 0))
            phase_end(act, 2)

            for l in (1, 2):
                s = q12[l]

                def front(n, k, u):
                    w = u % 2
                    act.wait_ge(s["t_ready"], n + 1)
                    freed(act, s["p_ready"], n)
                    act.nop(nofuse=True)
                    act.activation(xt[w][F:P, :], p_t[w][F:P, :], ACT.Copy).then_inc(s["o_ready"], 1)

                def back1(n, k, u):
                    w = u % 2
                    act.wait_ge(s["fb_ready"], n + 1)
                    stored(act, s["d_table"][w], n, 2 * k + u // 2)
                    act.nop(nofuse=True)
                    act.activation(ts[w], p_m[w][:, 0:TPC * F], ACT.Copy).then_inc(s["ts_ready"], 1)

                def store_part(n, k, u):
                    w = u % 2
                    act.wait_ge(s["s_ready"], n + 1)
                    act.nop(nofuse=True)
                    act.dma_start(part_d[F:P, bass.ds(e0(l, n), CH)], ms[w][F:P, :]).then_inc(s["d_part"][w], 16)

                def store_out(n, k, u):
                    w = u % 2
                    if l == 1:
                        act.wait_ge(s["ts_ready"], n + 1)
                        act.nop(nofuse=True)
                        act.dma_start(rows(tables[1], l, n), byf(ts[w])).then_inc(s["d_table"][w], 16)
                    else:
                        act.wait_ge(s["scan"], n + 1)
                        act.nop(nofuse=True)
                        act.dma_start(o2_d[:, bass.ds(e0(l, n), CH)], fs[w][0:F, :]).then_inc(s["d_table"][w], 16)

                if l == 1:
                    stages = [(front, 0), (store_out, 3), (store_part, 2), (back1, 2)]
                else:
                    stages = [(front, 0), (store_out, 2)]
                    stages.append((clear(1, 1, NCH // Z_REP), 0))
                stepped(act, stages + [(nodes_stage(l + 2), 0)], NCH, 4)
                act.wait_ge(a_out, 16 * before(l + 3, 0))
                if l == 2:
                    act.wait_ge(z_fill, 16 * (NCH // Z_REP + NCH))
                for w in range(2):
                    if l == 1:
                        act.wait_ge(s["d_part"][w], 16 * (NCH // 2))
                    act.wait_ge(s["d_table"][w], 16 * (NCH // 2))
                phase_end(act, l + 2)

            def square3(n, k, u):
                w = u % 2
                act.wait_ge(q3["sub"], 3 * n + 3)
                freed(act, q3["var"], n)
                act.nop(nofuse=True)
                act.activation(sq3[w], yy[u], ACT.Square).then_inc(q3["sq"], 1)

            def root3(n, k, u):
                w = u % 2
                act.wait_ge(q3["var"], n + 1)
                act.nop(nofuse=True)
                act.activation(st3[w][:, 2 * TPC:3 * TPC], st3[w][:, TPC:2 * TPC], ACT.Sqrt,
                               bias=eps_ln[:, :], scale=1.0 / F).then_inc(q3["std"], 1)

            def project3(n, k, u):
                w = u % 2
                act.wait_ge(q3["yt_ready"], n + 1)
                freed(act, q3["z_ready"], n)
                act.nop(nofuse=True)
                act.activation(xt[w][0:F, :], p_t[w][0:F, :], ACT.Copy).then_inc(q3["yts"], 1)

            def sum3(n, k, u):
                w = u % 2
                act.wait_ge(q3["sum_ready"], n + 1)
                for q in range(2):
                    freed(act, q3["d_add"][q], n, 32, 4)
                act.nop(nofuse=True)
                act.activation(ga[u], p_p[w][:, 0:TPC * F], ACT.Copy).then_inc(q3["ga_ready"], 1)

            stepped(act, [(project3, 2), (sum3, 4), (square3, 1), (root3, 1)], NCH, 4)
            phase_end(act, 5)

            def norm_f(n, k, u):
                m = parts_of(n)
                act.wait_ge(f_sum, n + 1)
                act.nop(nofuse=True)
                for q in range(NPP):
                    last = act.activation(dz[u][2][0:m, q * F:(q + 1) * F], dz[u][1][0:m, q * F:(q + 1) * F], ACT.Square,
                                          accum_out=dst_d[u][0:m, q:q + 1])
                last.then_inc(f_nrm, 1)

            def root1_f(n, k, u):
                m = parts_of(n)
                act.wait_ge(f_nrm, n + 1)
                act.nop(nofuse=True)
                act.activation(dst_d[u][0:m, NPP:2 * NPP], dst_d[u][0:m, 0:NPP], ACT.Sqrt).then_inc(f_std1, 1)

            def square_f(n, k, u):
                m = parts_of(n)
                act.wait_ge(f_sub, 2 * n + 2)
                act.nop(nofuse=True)
                act.activation(dz[u][2][0:m, :], dz[u][1][0:m, :], ACT.Square).then_inc(f_sq2, 1)

            def root2_f(n, k, u):
                m = parts_of(n)
                act.wait_ge(f_var, n + 1)
                act.nop(nofuse=True)
                act.activation(dst_d[u][0:m, 5 * NPP:6 * NPP], dst_d[u][0:m, 4 * NPP:5 * NPP], ACT.Sqrt,
                               bias=eps_ln[0:m, :], scale=1.0 / F).then_inc(f_std2, 1)

            def store_f(n, k, u):
                act.wait_ge(f_y, 2 * n + 2)
                act.dma_start(group(out, n), dz[u][1][0:parts_of(n), :]).then_inc(f_out[u], 16)

            stepped(act, [(norm_f, 0), (root2_f, 3), (root1_f, 0), (square_f, 2), (store_f, 3)], NG + 1, DD)
            for u in range(DD):
                act.wait_ge(f_out[u], 16 * ((NG + 1 - u + DD - 1) // DD))
            phase_end(act, 6)

        @block.tensor
        def _(pe):
            pe.wait_ge(c_pool, 5)
            pe.wait_ge(c_rows, 1)
            pe.wait_ge(c_nat, 16 * 11)
            for q, tile in enumerate((n_dstf, n_dsts, n_srcf, n_ew)):
                for j in range(TPC):
                    last = nc.tensor.transpose(psum[:, q, j * NCH:(j + 1) * NCH], tile[:, j * P:(j + 1) * P],
                                               ident[0:NCH, 0:NCH])
                last.then_inc(c_tr, 1)

            def count(lo, hi, start=False, stop=False):
                for b in range(2):
                    last = nc.tensor.matmul(psum[:, 4 + b, 0:HB], lo, hi[:, b * HB:(b + 1) * HB],
                                            start=start, stop=stop)
                last.then_inc(h_free, 1)

            pe.wait_ge(h_made, 1)
            count(oh_l[0], oh_h[0], start=True)

            def count_tile(n, k, u):
                pe.wait_ge(h_made, n + 2)
                count(oh_l[u], oh_h[u], stop=isinstance(n, int) and n == NT - 1)

            stepped(pe, [(count_tile, 0)], NT - 8, 8)
            for u in range(8):
                count_tile(NT - 8 + u, NT // 8 - 1, u)
            pe.wait_ge(h_v, 1)
            pe.wait_ge(c_pool, 10)
            for b in range(2):
                nc.tensor.matmul(psum[:, b, 0:HB], upper, cnt[:, b * HB:(b + 1) * HB], start=True, stop=True)
                last = nc.tensor.matmul(psum[:, 2 + b, 0:HB], ones, cnt[:, b * HB:(b + 1) * HB], start=True, stop=True)
            last.then_inc(h_pe, 1)
            pe.wait_ge(h_v, H_STEPS)
            for b in range(NB):
                w = min(P, HI - b * P)
                if b >= 4:
                    pe.wait_ge(h_pos, b - 3)
                for q, t in enumerate((last_c, first_c)):
                    last = nc.tensor.transpose(psum[0:w, 4 + b % 4, q * P:(q + 1) * P], t[:, b * P:b * P + w],
                                               ident[:, :])
                last.then_inc(h_tr, 1)
            phase_end(pe, 1)

            def front0(n, k, u):
                w = u % 2
                pe.wait_ge(q0["xi"], n + 1)
                pe.wait_ge(q0["d_got"][u], 64 * k + 64)
                freed(pe, q0["xt_ready"], n)
                pe.nop(nofuse=True)
                for j in range(TPC):
                    last = nc.tensor.transpose(p_t[w][:, j * P:(j + 1) * P], fx3(u)[:, j, 0:P], ident[:, :])
                last.then_inc(q0["t_ready"], 1)

            def mid0(n, k, u):
                w = u % 2
                pe.wait_ge(q0["xt_ready"], n + 1)
                freed(pe, q0["ms_ready"], n)
                pe.nop(nofuse=True)
                nc.tensor.matmul(p_m[w][0:F, :], w_x[:, 0:F], xt[w], start=True, stop=True).then_inc(q0["m_ready"], 1)
                freed(pe, q0["part_ready"], n)
                pe.nop(nofuse=True)
                nc.tensor.matmul(p_p[w], w_x[:, F:3 * F], xt[w], start=True, stop=True).then_inc(q0["p_ready"], 1)

            def by_edge(bank, rows_t, done):
                for j in range(TPC):
                    last = nc.tensor.transpose(bank[:, j * F:(j + 1) * F], rows_t[0:F, j * P:(j + 1) * P],
                                               ident[0:F, 0:F])
                last.then_inc(done, 1)

            def back0(n, k, u):
                w = u % 2
                pe.wait_ge(q0["scan"], n + 1)
                freed(pe, q0["ts_ready"], n)
                pe.nop(nofuse=True)
                by_edge(p_b[w], fs[w], q0["b_ready"])

            stepped(pe, [(front0, 0), (mid0, 1), (back0, 2)], NCH, 4)
            phase_end(pe, 2)

            for l in (1, 2):
                s = q12[l]
                width = P if l == 1 else F

                def front(n, k, u):
                    w = u % 2
                    pe.wait_ge(q12_in[u], 48 * (l - 1) * uses(u) + 48 * k + 48)
                    pe.wait_ge(s["d_got"][u], 64 * k + 64)
                    freed(pe, s["g_ready"], n)
                    freed(pe, s["o_ready"], n)
                    pe.nop(nofuse=True)
                    for j in range(TPC):
                        last = nc.tensor.transpose(p_t[w][:, j * P:(j + 1) * P], fx3(u)[:, j, 0:P], ident[:, :])
                    last.then_inc(s["t_ready"], 1)

                def mid(n, k, u):
                    w = u % 2
                    pe.wait_ge(s["g_ready"], n + 1)
                    pe.wait_ge(s["o_ready"], n + 1)
                    freed(pe, s["s_ready"], n)
                    pe.nop(nofuse=True)
                    nc.tensor.matmul(p_p[w][0:width, :], w_o[l - 1][:, :], xt[w], start=True, stop=True).then_inc(s["p_ready"], 1)
                    freed(pe, s["gmax"], n)
                    pe.nop(nofuse=True)
                    by_edge(p_b[w], xt[w], s["gb_ready"])

                def back1(n, k, u):
                    w = u % 2
                    pe.wait_ge(s["scan"], n + 1)
                    freed(pe, s["ts_ready"], n)
                    pe.nop(nofuse=True)
                    by_edge(p_m[w], fs[w], s["fb_ready"])

                stepped(pe, [(front, 0), (mid, 1)] + ([(back1, 2)] if l == 1 else []), NCH, 4)
                phase_end(pe, l + 2)

            def by_edge3(n, k, u):
                w = u % 2
                pe.wait_ge(q3["scan"], n + 1)
                freed(pe, q3["gmax"], n)
                pe.nop(nofuse=True)
                by_edge(p_b[w], fs[w], q3["gb_ready"])

            def transpose3(n, k, u):
                w = u % 2
                pe.wait_ge(q3["y_ready"], 2 * n + 2)
                freed(pe, q3["yts"], n)
                pe.nop(nofuse=True)
                for j in range(TPC):
                    last = nc.tensor.transpose(p_t[w][0:F, j * P:(j + 1) * P], yy[u][:, j * F:(j + 1) * F], ident[:, :])
                last.then_inc(q3["yt_ready"], 1)

            def project3(n, k, u):
                w = u % 2
                pe.wait_ge(q3["yts"], n + 1)
                freed(pe, q3["zs"], n)
                pe.nop(nofuse=True)
                for j in range(TPC):
                    last = nc.tensor.matmul(p_m[w][:, j * F:(j + 1) * F], xt[w][0:F, j * P:(j + 1) * P], w_p[:, :],
                                            start=True, stop=True)
                last.then_inc(q3["z_ready"], 1)

            def sum3(n, k, u):
                w = u % 2
                pe.wait_ge(q3["zs"], n + 1)
                pe.wait_ge(q3["eq"], n + 1)
                freed(pe, q3["ga_ready"], n)
                pe.nop(nofuse=True)
                for j in range(TPC):
                    last = nc.tensor.matmul(p_p[w][:, j * F:(j + 1) * F], eq[w][:, j * P:(j + 1) * P],
                                            zs[w][:, j * F:(j + 1) * F], start=True, stop=True)
                last.then_inc(q3["sum_ready"], 1)

            stepped(pe, [(transpose3, 2), (sum3, 4), (by_edge3, 0), (project3, 2)], NCH, 4)
            phase_end(pe, 5)
            phase_end(pe, 6)

        @block.vector
        def _(ve):
            v = nc.vector
            chained = {}

            def link(ins, counter):
                chained[counter.name] = chained.get(counter.name, 0) + 1
                ins.then_inc(counter, 1)
                ve.wait_ge(counter, chained[counter.name])

            v.memset(n_dst, N)
            v.memset(n_src, N)
            v.memset(n_next, N)
            v.memset(n_ew, 0.0)
            link(v.memset(n_prev, N), c_v)
            v.memset(n_prev[0:1, 0:1], -1).then_inc(c_memset, 1)
            v.memset(ones, 1.0)
            v.memset(eps_ln[:, :], EPS_LN)
            v.memset(zero[:, :], 0.0)
            v.memset(fill[1][:, :], 0.0).then_inc(c_zero, 1)
            v.memset(oh_l[0], 0.0)
            v.memset(oh_h[0], 0.0).then_inc(h_made, 1)
            ve.wait_ge(c_nat, 16 * 11)
            ve.wait_ge(c_memset, 1)
            ve.wait_ge(c_pool, 4)
            v.tensor_tensor(n_same, n_dst, n_prev, ALU.is_equal).then_inc(c_same, 1)
            v.tensor_tensor(n_last, n_dst, n_next, ALU.not_equal)
            v.tensor_copy(n_srcf, n_src).then_inc(c_same, 1)
            link(v.tensor_copy(n_dstf, n_dst), c_v)
            link(v.tensor_tensor(n_dsts, n_dstf, n_dummy, ALU.subtract), c_v)
            link(v.tensor_tensor(n_dsts, n_dsts, n_last, ALU.mult), c_v)
            v.tensor_tensor(n_dsts, n_dsts, n_dummy, ALU.add).then_inc(c_rows, 1)
            ve.wait_ge(c_wts, 16 * 23)
            v.tensor_tensor(w_x[0:F, :], w_x[0:F, :], w_b[:, 0:3 * F], ALU.subtract)
            v.tensor_tensor(w_o[0][0:F, :], w_o[0][0:F, :], w_b[:, 3 * F:5 * F], ALU.subtract)
            v.tensor_tensor(w_o[1][0:F, :], w_o[1][0:F, :], w_b[:, 5 * F:6 * F], ALU.subtract)
            v.tensor_copy(byf(fill[0][:, :]), b_row.unsqueeze(1).to_broadcast([P, NFILL // P, F])).then_inc(c_zero, 1)

            def column(q):
                return psum[:, q, 0:NT].rearrange("p (j c) -> p j c", c=NCH)

            def by_j(a):
                return a.rearrange("p (c j) -> p j c", j=TPC)

            ve.wait_ge(c_tr, 1)
            v.tensor_scalar(by_j(dst_g[:, :]), column(0), float(N - 1), None, ALU.min).then_inc(c_dst, 1)
            v.tensor_copy(by_j(lo_f), column(0))
            link(v.tensor_copy(by_j(hi_i), column(0)), c_v)
            link(v.tensor_scalar(hi_i, hi_i, 7, None, ALU.arith_shift_right), c_v)
            link(v.tensor_copy(hi_f, hi_i), c_v)
            link(v.scalar_tensor_tensor(out=lo_f, in0=hi_f, scalar=-float(P), in1=lo_f, op0=ALU.mult, op1=ALU.add), c_v)
            ve.wait_ge(c_tr, 4)
            v.tensor_copy(by_j(dst_s[:, :]), column(1))
            v.tensor_scalar(by_j(src_g[:, :]), column(2), float(N - 1), None, ALU.min)
            v.tensor_copy(by_j(src_f[:, :]), column(2))
            link(v.tensor_copy(by_j(ew[:, :]), column(3)), c_v)
            ve.wait_ge(c_out, 16 * 5)
            ve.wait_ge(c_pool, 10)

            def one_hot(n, k, u):
                if u == 0:
                    ve.wait_ge(h_free, n - 3 if again(n, 8) else 1)
                if u == 4 and again(n, 8):
                    ve.wait_ge(h_free, n - 3)
                v.tensor_scalar(oh_h[u], iota_h, hi_f[:, bass.ds(n, 1)], None, ALU.is_equal)
                v.tensor_scalar(oh_l[u], iota_l, lo_f[:, bass.ds(n, 1)], None, ALU.is_equal).then_inc(h_made, 1)

            stepped(ve, [(one_hot, 0)], NT, 8)
            ve.wait_ge(h_free, NT + 1)

            def halves(a):
                return a.rearrange("p (b h) -> p b h", b=2)

            link(v.tensor_copy(halves(cnt), psum[:, 4:6, 0:HB]), h_v)
            link(v.memset(last_c, 0.0), h_v)
            ve.wait_ge(h_pe, 1)
            link(v.tensor_copy(halves(tot), psum[:, 2:4, 0:HB]), h_v)
            link(v.tensor_tensor_scan(run, last_c, tot, 0.0, ALU.add, ALU.add), h_v)
            link(v.tensor_tensor(run, run, tot, ALU.subtract), h_v)
            link(v.tensor_tensor(halves(run), halves(run), psum[:, 0:2, 0:HB], ALU.add), h_v)
            link(v.tensor_scalar(tot, cnt, 0.0, None, ALU.is_gt), h_v)
            link(v.scalar_tensor_tensor(out=last_c, in0=run, scalar=-1.0 - ZROW, in1=tot, op0=ALU.add, op1=ALU.mult), h_v)
            link(v.tensor_scalar(last_c, last_c, float(ZROW), None, ALU.add), h_v)
            link(v.tensor_tensor(first_c, run, cnt, ALU.subtract), h_v)
            link(v.scalar_tensor_tensor(out=first_c, in0=first_c, scalar=-float(ZROW), in1=tot, op0=ALU.add, op1=ALU.mult), h_v)
            link(v.tensor_scalar(first_c, first_c, float(ZROW), None, ALU.add), h_v)
            assert chained[h_v.name] == H_STEPS
            for b in range(NB):
                w = min(P, HI - b * P)
                ve.wait_ge(h_tr, b + 1)
                v.tensor_copy(pos_n[0:w, b * 2 * P:(b + 1) * 2 * P].rearrange("p (l q) -> p q l", q=2),
                              psum[0:w, 4 + b % 4, 0:2 * P].rearrange("p (q l) -> p q l", q=2)).then_inc(h_pos, 1)

            def node_steps(buffers):
                hx, hh, sq, gm_a, st = buffers

                def center_a(phase, k):
                    _, per, m, _ = nodes_of(phase, k)
                    c = before(phase, k)
                    hv, gv, sv = byf(hx[0:m, 0:per * F]), byf(gm_a[0:m, 0:per * 16], 16), st[0:m, 0:per]
                    ve.wait_ge(a_in, 16 * c + 16)
                    v.tensor_reduce(gv, hv.rearrange("p k (g q) -> p k g q", q=4), X, ALU.max).then_inc(a_v, 1)
                    ve.wait_ge(a_v, 3 * c + 1)
                    v.tensor_tensor(hv[:, :, 0:16], hv[:, :, 0:16], gv, ALU.add).then_inc(a_v, 1)
                    ve.wait_ge(a_v, 3 * c + 2)
                    v.tensor_reduce(sv, hv, X, ALU.add).then_inc(a_v, 1)
                    ve.wait_ge(a_v, 3 * c + 3)
                    if phase > 1:
                        ve.wait_ge(a_out, 16 * c)
                    v.scalar_tensor_tensor(out=byf(hh[0:m, 0:per * F]), in0=spread(sv, F), scalar=-1.0 / F,
                                           in1=hv, op0=ALU.mult, op1=ALU.add).then_inc(a_sub, 1)

                def variance_a(phase, k):
                    _, per, m, _ = nodes_of(phase, k)
                    ve.wait_ge(a_sq, before(phase, k) + 1)
                    v.tensor_reduce(st[0:m, NPP:NPP + per], byf(sq[0:m, 0:per * F]), X, ALU.add).then_inc(a_var, 1)

                def scale_a(phase, k):
                    _, per, m, _ = nodes_of(phase, k)
                    hv, rv = byf(hh[0:m, 0:per * F]), st[0:m, 3 * NPP:3 * NPP + per]
                    ve.wait_ge(a_std, before(phase, k) + 1)
                    v.reciprocal(rv, st[0:m, 2 * NPP:2 * NPP + per]).then_inc(a_rec, 1)
                    ve.wait_ge(a_rec, before(phase, k) + 1)
                    v.tensor_tensor(hv, hv, spread(rv, F), ALU.mult).then_inc(a_y, 1)

                return center_a, variance_a, scale_a

            def nodes_stage(phase):
                center_a, variance_a, scale_a = node_steps(a_passes)
                return in_fours(phase, {0: [(scale_a, -1)], 2: [(center_a, 0)], 3: [(variance_a, 0)]})

            phase_end(ve, 1)

            def scan(l, out_, before, data, flags, n, done):
                if isinstance(n, int) and n == 0:
                    start = zero[0:F, :]
                else:
                    ve.wait_ge(done, n)
                    start = end_col(before[0:F, :], l)
                ve.nop(nofuse=True)
                v.tensor_tensor_scan(back(out_[0:F, :], l), back(flags[0:F, :], l), back(data[0:F, :], l), start,
                                     ALU.mult, ALU.max).then_inc(done, 1)

            def add_max(l, n, u, src_rows, first, maxed, added):
                v.tensor_reduce(byf(gm[u], 16), src_rows.rearrange("p j (g q) -> p j g q", q=4), X, ALU.max).then_inc(maxed, 1)
                ve.wait_ge(maxed, n + 1)
                ve.nop(nofuse=True)
                ins = v.tensor_tensor(xl_at(l, n, first, first + 16), xl_at(l, n, first, first + 16), byf(gm[u], 16), ALU.add)
                if added is not None:
                    ins.then_inc(added, 1)

            def take0(n, k, u):
                w = u % 2
                ve.wait_ge(q0["d_got"][u], 64 * k + 64)
                ve.wait_ge(q0["xi"], n + 1)
                ve.nop(nofuse=True)
                for q in range(2):
                    v.tensor_copy(cols(pos_g[q], 0, n), fx3(u)[:, :, P + q])
                add_max(0, n, w, fx3(u)[:, :, 0:F], 0, q0["taken"], None)

            def scan0(n, k, u):
                w = u % 2
                ve.wait_ge(q0["d_in"][u], 16 * k + 16)
                ve.wait_ge(q0["ms_ready"], n + 1)
                freed(ve, q0["b_ready"], n)
                scan(0, fs[w], fs[1 - w], ms[w], sn[u], n, q0["scan"])

            for fn in node_steps(a_passes):
                fn(1, 0)
            stepped(ve, [(take0, 0), (scan0, 2), (nodes_stage(2), 0)], NCH, 4)
            phase_end(ve, 2)

            for l in (1, 2):
                s = q12[l]
                width = P if l == 1 else F

                def complete(n, k, u):
                    w = u % 2
                    ve.wait_ge(s["t_ready"], n + 1)
                    ve.wait_ge(q12_in[u], 48 * (l - 1) * uses(u) + 48 * k + 48)
                    freed(ve, s["gb_ready"], n)
                    scan(l, xt[w], xt[1 - w], p_t[w], sn[u], n, s["g_ready"])

                def message(n, k, u):
                    w = u % 2
                    ve.wait_ge(s["p_ready"], n + 1)
                    if l == 1:
                        stored(ve, s["d_part"][w], n, 2 * k + u // 2)
                    v.tensor_tensor(ms[w][0:width, :], p_p[w][0:width, :], pl[u][0:width, :], ALU.add).then_inc(s["s_ready"], 1)
                    ve.wait_ge(s["s_ready"], n + 1)
                    if l == 1:
                        freed(ve, s["fb_ready"], n)
                    else:
                        stored(ve, s["d_table"][w], n, 2 * k + u // 2)
                    scan(l, fs[w], fs[1 - w], ms[w], sn[u], n, s["scan"])

                def maxima(n, k, u):
                    w = u % 2
                    ve.wait_ge(s["gb_ready"], n + 1)
                    add_max(l, n, w, byf(p_b[w][:, 0:TPC * F]), 16 * l, s["gmax"], None)

                stepped(ve, [(complete, 0), (message, 1), (maxima, 1), (nodes_stage(l + 2), 0)], NCH, 4)
                phase_end(ve, l + 2)

            def scan3(n, k, u):
                w = u % 2
                ve.wait_ge(q3["d_in"][u], 48 * k + 48)
                freed(ve, q3["gb_ready"], n)
                scan(3, fs[w], fs[1 - w], pl[u], sn[u], n, q3["scan"])

            def center3(n, k, u):
                w = u % 2
                ve.wait_ge(q3["gb_ready"], n + 1)
                add_max(3, n, w, byf(p_b[w][:, 0:TPC * F]), 48, q3["gmax"], q3["sub"])
                ve.wait_ge(q3["sub"], 3 * n + 1)
                ve.nop(nofuse=True)
                v.tensor_reduce(st3[w][:, 0:TPC], xl_at(3, n), X, ALU.add).then_inc(q3["sub"], 1)
                ve.wait_ge(q3["sub"], 3 * n + 2)
                stored(ve, q3["d_y"][u], n, k, 64, 4)
                freed(ve, q3["yt_ready"], n, depth=4)
                ve.nop(nofuse=True)
                v.scalar_tensor_tensor(out=byf(yy[u]), in0=spread(st3[w][:, 0:TPC], F), scalar=-1.0 / F,
                                       in1=xl_at(3, n), op0=ALU.mult, op1=ALU.add).then_inc(q3["sub"], 1)

            def same_src3(n, k, u):
                w = u % 2
                freed(ve, q3["sum_ready"], n)
                ve.nop(nofuse=True)
                eq3 = byf(eq[w], P)
                v.tensor_tensor(eq3, byf(sr[u], P), spread(cols(src_f, 3, n), P), ALU.is_equal).then_inc(q3["eq"], 1)
                ve.wait_ge(q3["eq"], n + 1)
                v.tensor_tensor(byf(eqm, P), eq3, mask[:, :, :], ALU.mult).then_inc(q3["eqc"], 1)
                ve.wait_ge(q3["eqc"], 3 * n + 1)
                v.tensor_reduce(dup, byf(eqm, P), X, ALU.max).then_inc(q3["eqc"], 1)
                ve.wait_ge(q3["eqc"], 3 * n + 2)
                ve.nop(nofuse=True)
                v.scalar_tensor_tensor(out=off, in0=cols(src_f, 3, n), scalar=dummy_f[:, :], in1=dup,
                                       op0=ALU.subtract, op1=ALU.mult).then_inc(q3["eqc"], 1)
                ve.wait_ge(q3["eqc"], 3 * n + 3)
                for q in range(2):
                    freed(ve, q3["d_add"][q], n, 32, 4)
                ve.nop(nofuse=True)
                v.tensor_tensor(add_i[u], cols(src_f, 3, n), off, ALU.subtract).then_inc(q3["add_i"], 1)

            def variance3(n, k, u):
                w = u % 2
                ve.wait_ge(q3["sq"], n + 1)
                v.tensor_reduce(st3[w][:, TPC:2 * TPC], byf(sq3[w]), X, ALU.add).then_inc(q3["var"], 1)

            def scale3(n, k, u):
                w = u % 2
                ve.wait_ge(q3["std"], n + 1)
                v.reciprocal(st3[w][:, 3 * TPC:4 * TPC], st3[w][:, 2 * TPC:3 * TPC]).then_inc(q3["y_ready"], 1)
                ve.wait_ge(q3["y_ready"], 2 * n + 1)
                v.tensor_tensor(byf(yy[u]), byf(yy[u]), spread(st3[w][:, 3 * TPC:4 * TPC], F), ALU.mult).then_inc(q3["y_ready"], 1)

            def weigh3(n, k, u):
                w = u % 2
                ve.wait_ge(q3["z_ready"], n + 1)
                freed(ve, q3["sum_ready"], n)
                ve.nop(nofuse=True)
                v.tensor_tensor(byf(zs[w]), byf(p_m[w][:, 0:TPC * F]), spread(cols(ew, 3, n), F), ALU.mult).then_inc(q3["zs"], 1)

            stepped(ve, [(center3, 1), (scan3, 0), (variance3, 1), (weigh3, 3), (scale3, 1), (same_src3, 3)], NCH, 4)
            phase_end(ve, 5)

            def unit_f(n, k, u):
                m = parts_of(n)
                st = dst_d[u]
                ve.wait_ge(f_std1, n + 1)
                v.tensor_scalar(st[0:m, 2 * NPP:3 * NPP], st[0:m, NPP:2 * NPP], EPS_NORM, None, ALU.max).then_inc(f_unit, 1)
                ve.wait_ge(f_unit, 3 * n + 1)
                v.reciprocal(st[0:m, 3 * NPP:4 * NPP], st[0:m, 2 * NPP:3 * NPP]).then_inc(f_unit, 1)
                ve.wait_ge(f_unit, 3 * n + 2)
                hv = byf(dz[u][1])[0:m]
                v.tensor_tensor(hv, hv, spread(st[0:m, 3 * NPP:4 * NPP], F), ALU.mult).then_inc(f_unit, 1)

            def center_f(n, k, u):
                m = parts_of(n)
                st, hv = dst_d[u], byf(dz[u][1])[0:m]
                ve.wait_ge(f_h, n + 1)
                v.tensor_reduce(st[0:m, 6 * NPP:7 * NPP], hv, X, ALU.add).then_inc(f_sub, 1)
                ve.wait_ge(f_sub, 2 * n + 1)
                v.scalar_tensor_tensor(out=hv, in0=spread(st[0:m, 6 * NPP:7 * NPP], F), scalar=-1.0 / F, in1=hv,
                                       op0=ALU.mult, op1=ALU.add).then_inc(f_sub, 1)

            def variance_f(n, k, u):
                m = parts_of(n)
                ve.wait_ge(f_sq2, n + 1)
                v.tensor_reduce(dst_d[u][0:m, 4 * NPP:5 * NPP], byf(dz[u][2])[0:m], X, ALU.add).then_inc(f_var, 1)

            def scale_f(n, k, u):
                m = parts_of(n)
                ve.wait_ge(f_std2, n + 1)
                v.reciprocal(dst_d[u][0:m, 7 * NPP:8 * NPP], dst_d[u][0:m, 5 * NPP:6 * NPP]).then_inc(f_y, 1)
                ve.wait_ge(f_y, 2 * n + 1)
                v.tensor_tensor(byf(dz[u][1])[0:m], byf(dz[u][1])[0:m], spread(dst_d[u][0:m, 7 * NPP:8 * NPP], F),
                                ALU.mult).then_inc(f_y, 1)

            stepped(ve, [(unit_f, 1), (center_f, 2), (scale_f, 3), (variance_f, 2)], NG + 1, DD)
            phase_end(ve, 6)


_INS = ["x", "src", "dst", "edge_weight", "L0_gnn_W0", "L0_gnn_b0", "L0_gnn_W1", "L0_gnn_b1", "L0_gnn_W2",
        "L0_gnn_b2", "L1_gnn_weight", "L1_gnn_bias"]
_OUTS = [((N, F), "float32")]


def kernel(**inputs):
    import numpy as _np
    import concourse.bacc as _bacc
    from concourse import mybir as _mybir
    from concourse.bass_utils import run_bass_kernel_spmd as _run

    nc = _bacc.Bacc("TRN2", target_bir_lowering=False, num_devices=1)
    arrays, args = {}, []
    for name in _INS:
        a = _np.ascontiguousarray(inputs[name])
        arrays[f"in_{name}_dram"] = a
        args.append(nc.dram_tensor(f"in_{name}_dram", a.shape, _mybir.dt.from_np(a.dtype), kind="ExternalInput").ap())
    for i, (shape, dtype) in enumerate(_OUTS):
        dt = _mybir.dt.from_np(_np.dtype(dtype))
        args.append(nc.dram_tensor(f"out_{i}_dram", shape, dt, kind="ExternalOutput").ap())
    build(nc, *args)
    r = _run(nc, [arrays], core_ids=[0])
    return r.results[0]["out_0_dram"]
```

```python
from contextlib import ExitStack

import numpy as np

import concourse.bass as bass
from concourse import mybir

FP32, BF16, FP16, I32 = mybir.dt.float32, mybir.dt.bfloat16, mybir.dt.float16, mybir.dt.int32
ALU = mybir.AluOpType
ACT = mybir.ActivationFunctionType
X = mybir.AxisListType.X

P = 128
N = 100000
E = 50000
F = 64
TPC = 4
CH = TPC * P
NCH = -(-E // CH)
NCH += NCH % 2
NT = NCH * TPC
EP = NCH * CH
LAST_ROW = E - (NCH - 1) * CH
HI = -(-N // P)
HB = HI // 2
NB = -(-HI // P)
NFILL = 1024
NTAB = NFILL * NCH
WINDOWS = -(-NCH // 4)
Z_REP = 2
Z_LATE = 3
DUMMY = N + 1
ZROW = EP
ROW = F + 2
NPP = 16
V_NODES = 10
GR = P * NPP
NG = N // GR
A_STEPS = NCH // 4
RP = (N - NG * GR) // NPP
EPS_LN = 1e-5
EPS_NORM = 1e-12
H_STEPS = 12
assert NG == 2 * A_STEPS and HI % 2 == 0 and RP * NPP == N - NG * GR and NTAB >= DUMMY + P and 0 < LAST_ROW < CH


def stepped(eng, stages, total, depth=2):
    skew = max(late for _, late in stages)
    lead = -(-(skew + depth) // depth) * depth
    whole = total - total % depth

    def at(s):
        for fn, late in stages:
            n = s - late
            if 0 <= n < total:
                fn(n, n // depth, n % depth)

    for s in range(lead):
        at(s)
    with eng.Fori(lead // depth, whole // depth) as i:
        for v in range(depth):
            for fn, late in stages:
                fn(depth * i + (v - late), i + (v - late) // depth, (v - late) % depth)
    for s in range(whole, total + skew):
        at(s)


def again(n, depth=2):
    return not isinstance(n, int) or n >= depth


def freed(eng, semaphore, n, per=1, depth=2):
    if again(n, depth):
        eng.wait_ge(semaphore, per * (n - depth + 1))


def stored(eng, semaphore, n, k, amount=16, depth=2):
    if again(n, depth):
        eng.wait_ge(semaphore, amount * k)


def build(nc, x, src, dst, edge_weight, w0, b0, w1, b1, w2, b2, w_l1, b_l1, out):
    with ExitStack() as ctx:
        def sb(name, shape, dt=FP32):
            return ctx.enter_context(nc.sbuf_tensor(name, shape, dt))

        def sem(name):
            return ctx.enter_context(nc.semaphore(name))

        def dram(name, shape, dt=FP32):
            return nc.dram_tensor(name, shape, dt).ap()

        xpos = dram("xpos", (N, ROW))
        pos_d = dram("pos_d", (HI * P, 2))
        same_d = dram("same_d", (EP + CH,))
        srcf_d = dram("srcf_d", (EP,))
        part_d = dram("part_d", (P, EP))
        tables = [dram("table0", (EP + 1, F)), dram("table1", (EP + 1, F))]
        o2_d = dram("o2_d", (F, EP))
        y1_d = dram("y1_d", (NTAB, F))
        agg_d = [dram("agg0", (NTAB, F)), dram("agg1", (NTAB, F))]

        xl = sb("xl", [P, NT * F])
        dst_g = sb("dst_g", [P, NT], I32)
        dst_s = sb("dst_s", [P, NT], I32)
        src_g = sb("src_g", [P, NT], I32)
        src_f = sb("src_f", [P, NT])
        ew = sb("ew", [P, NT])
        pos_g = [sb("last_g", [P, NT], I32), sb("first_g", [P, NT], I32)]
        ident = sb("ident", [P, P])
        w_x = sb("w_x", [P, 3 * F])
        w_o = [sb("w_o0", [P, 2 * F]), sb("w_o1", [P, F])]
        w_p = sb("w_p", [F, F])
        bias0 = sb("bias0", [F, 1])
        bias12 = sb("bias12", [P, 1])
        fill = [sb("fill0", [P, NFILL // P * F]), sb("fill1", [P, NFILL // P * F])]
        eps_ln = sb("eps_ln", [P, 1])
        zero = sb("zero", [P, 1])
        mask = sb("mask", [P, TPC, P])
        dummy_f = sb("dummy_f", [P, 1])
        idx_w = sb("idx_w", [P, 2, 4 * TPC], I32)

        work_words = 18432
        work = sb("work", [P, work_words])
        place = [0]

        def carve(words):
            place[0] += words
            assert place[0] <= work_words, place[0]
            return work[:, place[0] - words:place[0]]

        psum = ctx.enter_context(nc.psum_tensor("psum", [P, 8, 512], FP32))
        p_t = [psum[:, 0, :], psum[:, 1, :]]
        p_m = [psum[:, 2, :], psum[:, 3, :]]
        p_p = [psum[:, 4, :], psum[:, 5, :]]
        p_b = [psum[:, 6, :], psum[:, 7, :]]

        phase_done = sem("phase_done")

        def phase_end(eng, n):
            eng.drain().then_inc(phase_done, 1)
            eng.wait_ge(phase_done, 5 * n)
            eng.nop(nofuse=True)

        n_dst, n_prev, n_next, n_src = (carve(CH)[0:NCH, :].bitcast(I32) for _ in range(4))
        n_ew, n_same, n_last, n_dummy, n_dstf, n_srcf, n_dsts = (carve(CH)[0:NCH, :] for _ in range(7))
        end_natural = place[0]
        w_b = carve(6 * F)[0:F, :]
        b_row = carve(F)
        hi_i = carve(NT).bitcast(I32)
        hi_f = carve(NT)
        lo_f = carve(NT)
        iota_h = carve(HB).bitcast(FP16)
        iota_l = carve(F).bitcast(FP16)
        at_onehots = place[0]
        oh_h = [carve(HB).bitcast(BF16) for _ in range(8)]
        oh_l = [carve(F).bitcast(BF16) for _ in range(8)]
        end_onehots = place[0]
        place[0] = at_onehots
        xs = [carve(NPP * ROW) for _ in range(2)]
        place[0] = max(place[0], end_onehots)
        upper = carve(P)
        ones = carve(P)
        pos_n = carve(NB * P * 2)
        xi = [carve(TPC * F) for _ in range(4)]
        place[0] = 0
        cnt, tot, run, last_c, first_c = (carve(HI) for _ in range(5))
        assert place[0] <= end_natural
        place[0] = 0
        xb = [carve(NPP * F) for _ in range(4)]
        ps = [carve(NPP * 2) for _ in range(4)]
        assert place[0] <= end_natural

        place[0] = 0
        fx = [carve(TPC * (P + 2)) for _ in range(4)]
        xt = [carve(CH) for _ in range(2)]
        ms = [carve(CH) for _ in range(2)]
        fs = [carve(CH) for _ in range(2)]
        sn = [carve(CH) for _ in range(4)]
        pl = [carve(CH) for _ in range(4)]
        ts = [carve(TPC * F) for _ in range(2)]
        gm = [carve(TPC * 16) for _ in range(2)]
        before_p3 = place[0]
        yy = [carve(TPC * F) for _ in range(4)]
        st3 = [carve(TPC * 4) for _ in range(2)]
        zs = [carve(TPC * F) for _ in range(2)]
        ga = [m[:, q * TPC * F:(q + 1) * TPC * F] for m in ms for q in range(2)]
        sq3 = ts
        eq = [carve(CH) for _ in range(2)]
        sr = [carve(CH) for _ in range(4)]
        eqm = carve(CH)
        dup = carve(TPC)
        off = carve(TPC)
        add_i = [carve(TPC).bitcast(I32) for _ in range(4)]
        place[0] = before_p3
        a_h, a_c, a_s, a_gm, a_st = (carve(width) for width in (NPP * F, NPP * F, NPP * F, NPP * 16, NPP * 4))

        F_DEEP = 8
        grp = [[xl[:, (3 * u + q) * NPP * F:(3 * u + q + 1) * NPP * F] for q in range(3)] for u in range(F_DEEP)]
        stats = [work[:, u * 8 * NPP:(u + 1) * 8 * NPP] for u in range(F_DEEP)]

        def fx3(u):
            return fx[u].rearrange("p (j f) -> p j f", f=P + 2)

        def byf(a, f=F):
            return a.rearrange("p (j f) -> p j f", f=f)

        def spread(a, width):
            return a.unsqueeze(2).to_broadcast([a.shape[0], a.shape[1], width])

        def at_chunk(l, n):
            return n if l in (0, 2) else (NCH - 1) - n

        def e0(l, n):
            return at_chunk(l, n) * CH

        def cols(a, l, n):
            return a[:, bass.ds(at_chunk(l, n) * TPC, TPC)]

        def xl_at(l, n, a=0, b=F):
            return byf(xl[:, bass.ds(at_chunk(l, n) * (TPC * F), TPC * F)])[:, :, a:b]

        def rows(t, l, n):
            return t[bass.ds(e0(l, n), CH), :].rearrange("(j p) f -> p j f", p=P)

        def parts_of(n):
            return RP if isinstance(n, int) and n == NG else P

        def group(t, n):
            return t[bass.ds(n * GR, parts_of(n) * NPP), :].rearrange("(p k) f -> p (k f)", k=NPP)

        def nodes_of(phase, k):
            if phase == 1:
                return NG * GR, NPP, RP
            if phase == 2:
                return k * GR, NPP, P
            return A_STEPS * GR + ((phase - 3) * A_STEPS + k) * (GR // 2), NPP // 2, P

        def before(phase, k):
            return 0 if phase == 1 else 1 + (phase - 2) * A_STEPS + k

        def node_rows(t, phase, k):
            first, per, m = nodes_of(phase, k)
            return t[bass.ds(first, m * per), :].rearrange("(p k) f -> p (k f)", k=per)

        def in_fours(phase, what):
            def stage(n, k, u):
                for fn, late in what.get(u, ()):
                    if not isinstance(k, int) or 0 <= k + late < A_STEPS:
                        fn(phase, k + late)
            return stage

        def scale_rows(eng, n, u, a, b):
            m = parts_of(n)
            r = byf(grp[u][1])[0:m, a:b]
            return eng.tensor_tensor(r, r, spread(stats[u][0:m, 3 * NPP + a:3 * NPP + b], F), ALU.mult)

        def uses(u):
            return (NCH + 3 - u) // 4

        def back(a, l):
            return a[:, ::-1] if l in (1, 3) else a

        def end_col(a, l):
            return a[:, 0:1] if l in (1, 3) else a[:, CH - 1:CH]

        c_memset, c_zero, c_nat, c_wts, c_pool = sem("c_memset"), sem("c_zero"), sem("c_nat"), sem("c_wts"), sem("c_pool")
        c_din = sem("c_din")
        c_v, c_same, c_rows, c_out, c_tr, c_dst = sem("c_v"), sem("c_same"), sem("c_rows"), sem("c_out"), sem("c_tr"), sem("c_dst")
        window_ready = sem("window_ready")
        x_got, x_put = [sem(f"x_got{u}") for u in range(4)], [sem(f"x_put{u}") for u in range(4)]
        h_free, h_made, h_v, h_pe, h_tr, h_pos, h_out = (sem(f"h_{t}") for t in ("free", "made", "v", "pe", "tr", "pos", "out"))
        b_in, b_out = [sem(f"b_in{u}") for u in range(4)], [sem("b_out0"), sem("b_out1")]
        b_row_made = sem("b_row_made")
        z_fill = sem("z_fill")
        a_in, a_out = sem("a_in"), sem("a_out")
        a_v, a_sub, a_sq, a_var, a_std, a_y = (sem(f"a_{t}") for t in ("v", "sub", "sq", "var", "std", "y"))

        def sems(tag, plain, dmas2, dmas4):
            made = {t: sem(f"{tag}_{t}") for t in plain.split()}
            made.update({t: [sem(f"{tag}_{t}{u}") for u in range(2)] for t in dmas2.split()})
            made.update({t: [sem(f"{tag}_{t}{u}") for u in range(4)] for t in dmas4.split()})
            return made

        q0 = sems("q0", "xi t_ready xt_ready m_ready ms_ready p_ready part_ready scan taken b_ready ts_ready",
                  "d_part d_table", "d_in d_got")
        q12 = {l: sems(f"q{l}", "t_ready g_ready o_ready p_ready s_ready scan gb_ready gmax",
                       "d_table", "d_got") for l in (1, 2)}
        q12_in = [sem(f"q12_in{u}") for u in range(4)]
        q12[1].update(sems("q1", "fb_ready ts_ready", "d_part", ""))
        q3 = sems("q3", "scan gb_ready gmax sub sq var std y_ready yt_ready yts z_ready zs eq eqc "
                  "add_i sum_ready ga_ready", "d_add", "d_in d_y")
        f_in, f_out = ([sem(f"f_{t}{u}") for u in range(F_DEEP)] for t in ("in", "out"))
        f_sum, f_nrm, f_std1, f_unit, f_h, f_sub, f_sq2, f_var, f_std2, f_y = (
            sem(f"f_{t}") for t in ("sum", "nrm", "std1", "unit", "h", "sub", "sq2", "var", "std2", "y"))

        block = ctx.enter_context(nc.Block())

        @block.sync
        def _(sp):
            full = (NCH - 1) * CH

            def row(a):
                return a.rearrange("(c k) -> c k", c=1)

            def load_rows(tile, array, done):
                sp.dma_start(tile[0:NCH - 1, :], array[0:full].rearrange("(c k) -> c k", k=CH)).then_inc(done, 16)
                sp.dma_start(tile[NCH - 1:NCH, 0:LAST_ROW], row(array[full:E])).then_inc(done, 16)

            sp.wait_ge(c_memset, 1)
            load_rows(n_dst, dst, c_din)
            sp.wait_ge(c_memset, 2)
            load_rows(n_src, src, c_nat)
            load_rows(n_ew, edge_weight, c_nat)
            sp.dma_start(n_prev[0:1, 1:CH], row(dst[0:CH - 1])).then_inc(c_nat, 16)
            sp.dma_start(n_prev[1:NCH - 1, :], dst[CH - 1:full - 1].rearrange("(c k) -> c k", k=CH)).then_inc(c_nat, 16)
            sp.dma_start(n_prev[NCH - 1:NCH, 0:LAST_ROW + 1], row(dst[full - 1:E])).then_inc(c_nat, 16)
            sp.dma_start(n_next[0:NCH - 1, :], dst[1:full + 1].rearrange("(c k) -> c k", k=CH)).then_inc(c_nat, 16)
            sp.dma_start(n_next[NCH - 1:NCH, 0:LAST_ROW - 1], row(dst[full + 1:E])).then_inc(c_nat, 16)
            sp.wait_ge(c_zero, 1)
            for t in tables:
                sp.dma_start(t[ZROW:ZROW + 1, :], fill[1][0:1, 0:F]).then_inc(c_out, 16)
            sp.dma_start(row(same_d[EP:EP + CH]), fill[1][0:1, 0:CH]).then_inc(c_out, 16)
            sp.wait_ge(c_same, 2)
            sp.dma_start(same_d[0:EP].rearrange("(c k) -> c k", k=CH), n_same).then_inc(c_out, 16)
            sp.dma_start(srcf_d.rearrange("(c k) -> c k", k=CH), n_srcf).then_inc(c_out, 16)

            def put(n, k, u):
                sp.wait_ge(x_got[u], 64 * k + 64)
                sp.nop(nofuse=True)
                sp.dma_start(xl[:, bass.ds(n * (TPC * F), TPC * F)], xi[u]).then_inc(x_put[u], 16)

            stepped(sp, [(put, 0)], NCH, 4)
            sp.wait_ge(c_out, 16 * 5)
            for u in range(4):
                sp.wait_ge(x_put[u], 16 * uses(u))
            phase_end(sp, 1)

            def load0(n, k, u):
                freed(sp, q0["scan"], n, depth=4)
                sp.nop(nofuse=True)
                sp.dma_start(sn[u][0:F, :], same_d[bass.ds(e0(0, n), CH)].partition_broadcast(F)).then_inc(q0["d_in"][u], 16)

            stepped(sp, [(load0, 0)], NCH, 4)
            phase_end(sp, 2)

            for l in (1, 2):
                s = q12[l]

                def load(n, k, u):
                    freed(sp, s["scan"], n, depth=4)
                    freed(sp, s["t_ready"], n, depth=4)
                    sp.nop(nofuse=True)
                    sp.dma_start(fx3(u)[:, :, 0:F], rows(tables[l - 1], l, n)).then_inc(q12_in[u], 16)
                    ahead = 1 if l == 1 else 0
                    sp.dma_start(sn[u][0:F, :], same_d[bass.ds(e0(l, n) + ahead, CH)].partition_broadcast(F)).then_inc(q12_in[u], 16)
                    part = part_d[:, bass.ds(e0(l, n), CH)] if l == 1 else part_d[F:P, bass.ds(e0(l, n), CH)]
                    sp.dma_start(pl[u] if l == 1 else pl[u][0:F, :], part).then_inc(q12_in[u], 16)

                stepped(sp, [(load, 0)], NCH, 4)
                phase_end(sp, l + 2)

            def load3(n, k, u):
                freed(sp, q3["scan"], n, depth=4)
                sp.nop(nofuse=True)
                sp.dma_start(sn[u][0:F, :], same_d[bass.ds(e0(3, n) + 1, CH)].partition_broadcast(F)).then_inc(q3["d_in"][u], 16)
                sp.dma_start(pl[u][0:F, :], o2_d[:, bass.ds(e0(3, n), CH)]).then_inc(q3["d_in"][u], 16)
                freed(sp, q3["eq"], n, depth=4)
                sp.nop(nofuse=True)
                sp.dma_start(sr[u], srcf_d[bass.ds(e0(3, n), CH)].partition_broadcast(P)).then_inc(q3["d_in"][u], 16)

            stepped(sp, [(load3, 0)], NCH, 4)
            phase_end(sp, 5)

            def load_f(n, k, u):
                stored(sp, f_out[u], n, k, depth=F_DEEP)
                sp.nop(nofuse=True)
                for q, t in enumerate((y1_d, agg_d[0], agg_d[1])):
                    sp.dma_start(grp[u][q][0:parts_of(n), :], group(t, n)).then_inc(f_in[u], 16)

            stepped(sp, [(load_f, 0)], NG + 1, F_DEEP)
            phase_end(sp, 6)

        @block.gpsimd
        def _(gp):
            def iota(out_, pattern, base, channel):
                gp.iota(out_, pattern=pattern, base=base, channel_multiplier=channel,
                        allow_small_or_imprecise_dtypes=True).then_inc(c_pool, 1)

            gp.memset(ident[:, :], 0.0).then_inc(c_pool, 1)
            gp.memset(mask[:, :, :], 1.0).then_inc(c_pool, 1)
            gp.memset(upper, 1.0).then_inc(c_pool, 1)
            iota(n_dummy.rearrange("p (j k) -> p j k", k=P), [[0, TPC], [1, P]], DUMMY, 0)
            gp.wait_ge(c_pool, 3)
            gp.affine_select(out=ident[:, :], in_=ident[:, :], compare_op=ALU.not_equal, fill=1.0, base=0,
                             pattern=[[-1, P]], channel_multiplier=1).then_inc(c_pool, 1)
            iota(iota_h, [[1, HI]], 0, 0)
            iota(iota_l, [[1, P]], 0, 0)
            iota(dummy_f[:, :], [[0, 1]], DUMMY, 1)
            gp.affine_select(out=mask[:, :, :], in_=mask[:, :, :], compare_op=ALU.is_gt, fill=0.0, base=0,
                             pattern=[[0, TPC], [-1, P]], channel_multiplier=1).then_inc(c_pool, 1)
            gp.affine_select(out=upper, in_=upper, compare_op=ALU.is_ge, fill=0.0, base=0,
                             pattern=[[1, P]], channel_multiplier=-1).then_inc(c_pool, 1)

            gp.wait_ge(c_dst, 1)
            gp.nop(nofuse=True)

            def window_chunks(n):
                return min(4, NCH - n // 4 * 4) if isinstance(n, int) else 4

            def window(column, l, n, k, v, use):
                if v % 4 == 0:
                    c = window_chunks(n)
                    first = n if l in (0, 2) else (NCH - c) - n
                    gp.tensor_copy(idx_w[:, v // 4, 0:c * TPC], column[:, bass.ds(first * TPC, c * TPC)]).then_inc(window_ready, 1)
                    gp.wait_ge(window_ready, use * WINDOWS + 2 * k + v // 4 + 1)
                    gp.nop(nofuse=True)

            def index(l, n, v, j):
                at = v % 4 if l in (0, 2) else window_chunks(n) - 1 - v % 4
                return bass.IndirectOffsetOnAxis(ap=idx_w[:, v // 4, at * TPC + j:at * TPC + j + 1], axis=0)

            def fetch(out_, table, rows_, done):
                gp.indirect_dma_start(out_, None, table[:, :], rows_).then_inc(done, 16)

            def gather_x(n, k8, v):
                u, k = v % 4, 2 * k8 + v // 4
                stored(gp, x_put[u], n, k, depth=4)
                gp.nop(nofuse=True)
                window(dst_g, 0, n, k8, v, 0)
                for j in range(TPC):
                    fetch(xi[u][:, j * F:(j + 1) * F], x, index(0, n, v, j), x_got[u])

            stepped(gp, [(gather_x, 0)], NCH, 8)
            phase_end(gp, 1)

            def gather0(n, k8, v):
                u = v % 4
                freed(gp, q0["t_ready"], n, depth=4)
                freed(gp, q0["taken"], n, depth=4)
                gp.nop(nofuse=True)
                window(src_g, 0, n, k8, v, 1)
                for j in range(TPC):
                    fetch(fx3(u)[:, j, F:P + 2], xpos, index(0, n, v, j), q0["d_got"][u])

            stepped(gp, [(gather0, 0)], NCH, 8)
            phase_end(gp, 2)

            for l in (1, 2):
                s = q12[l]

                def gather(n, k8, v):
                    u = v % 4
                    freed(gp, s["t_ready"], n, depth=4)
                    gp.nop(nofuse=True)
                    window(pos_g[l - 1], l, n, k8, v, l + 1)
                    for j in range(TPC):
                        fetch(fx3(u)[:, j, F:P], tables[l - 1], index(l, n, v, j), s["d_got"][u])

                stepped(gp, [(gather, 0)], NCH, 8)
                phase_end(gp, l + 2)

            def add(m, w, j):
                if j >= 2 or not isinstance(m, int) or m > 0:
                    gp.wait_ge(q3["d_add"][j % 2], 16 * (2 * m + j // 2))
                    gp.nop(nofuse=True)
                gp.indirect_dma_start(agg_d[j % 2][:, :], bass.IndirectOffsetOnAxis(ap=add_i[w][:, j:j + 1], axis=0),
                                      ga[w][:, j * F:(j + 1) * F], None, compute_op=ALU.add).then_inc(q3["d_add"][j % 2], 16)

            def scatter(n, k8, v):
                u, k = v % 4, 2 * k8 + v // 4
                z = (u - Z_LATE) % 4
                some_y = not isinstance(n, int) or n < NCH
                some_z = not isinstance(n, int) or n >= Z_LATE
                if some_y:
                    gp.wait_ge(q3["y_ready"], 2 * n + 2)
                    stored(gp, q3["d_y"][u], n, k, 64, 4)
                    gp.nop(nofuse=True)
                    window(dst_s, 3, n, k8, v, 4)
                if some_z:
                    gp.wait_ge(q3["ga_ready"], n - Z_LATE + 1)
                    gp.wait_ge(q3["add_i"], n - Z_LATE + 1)
                    gp.nop(nofuse=True)
                for j in (0, 2):
                    if some_z:
                        add(n - Z_LATE, z, j)
                        add(n - Z_LATE, z, j + 1)
                    if some_y:
                        for q in (j, j + 1):
                            gp.indirect_dma_start(y1_d[:, :], index(3, n, v, q),
                                                  yy[u][:, q * F:(q + 1) * F], None, bounds_check=N - 1,
                                                  oob_is_err=False).then_inc(q3["d_y"][u], 16)

            stepped(gp, [(scatter, 0)], NCH, 8)
            for n in range(NCH, NCH + Z_LATE):
                scatter(n, n // 8, n % 8)
            for u in range(4):
                gp.wait_ge(q3["d_y"][u], 64 * ((NCH + 3 - u) // 4))
            for q in range(2):
                gp.wait_ge(q3["d_add"][q], 32 * NCH)
            phase_end(gp, 5)

            def sum_f(n, k, u):
                m = parts_of(n)
                gp.wait_ge(f_in[u], 48 * k + 48)
                gp.nop(nofuse=True)
                gp.tensor_tensor(grp[u][1][0:m, :], grp[u][1][0:m, :], grp[u][2][0:m, :], ALU.add).then_inc(f_sum, 1)

            def residual_f(n, k, u):
                m = parts_of(n)
                gp.wait_ge(f_unit, 3 * n + 2)
                gp.nop(nofuse=True)
                scale_rows(gp, n, u, V_NODES, NPP).then_inc(f_h, 1)
                gp.wait_ge(f_h, 2 * n + 1)
                gp.wait_ge(f_unit, 3 * n + 3)
                gp.nop(nofuse=True)
                gp.tensor_tensor(grp[u][1][0:m, :], grp[u][1][0:m, :], grp[u][0][0:m, :], ALU.add).then_inc(f_h, 1)

            stepped(gp, [(sum_f, 0), (residual_f, 2)], NG + 1, F_DEEP)
            phase_end(gp, 6)

        @block.scalar
        def _(act):
            blocks = ((w0, 0, F, w_x, 0), (w1, 0, 2 * F, w_x, 1), (w2, 0, 3 * F, w_x, 2),
                      (w1, F, 3 * F, w_o[0], 0), (w2, F, 4 * F, w_o[0], 1), (w2, 2 * F, 5 * F, w_o[1], 0))
            for q, (w, a, b, tile, at) in enumerate(blocks):
                act.dma_start(tile[0:F, at * F:(at + 1) * F], w[a:a + F, :]).then_inc(c_wts, 16)
                act.dma_start(tile[F:P, at * F:(at + 1) * F], w[b:b + F, :]).then_inc(c_wts, 16)
                act.dma_start(w_b[:, q * F:(q + 1) * F], w[b:b + F, :]).then_inc(c_wts, 16)
            act.dma_start(w_p[:, :], w_l1[:, :]).then_inc(c_wts, 16)
            act.dma_start(bias0[:, :], b0.rearrange("(p a) -> p a", a=1)).then_inc(c_wts, 16)
            act.dma_start(bias12[0:F, :], b1.rearrange("(p a) -> p a", a=1)).then_inc(c_wts, 16)
            act.dma_start(bias12[F:P, :], b2.rearrange("(p a) -> p a", a=1)).then_inc(c_wts, 16)
            act.dma_start(b_row, b_l1.partition_broadcast(P)).then_inc(c_wts, 16)
            act.wait_ge(c_zero, 1)

            def clear(q, fills, before_):
                def stage(n, k, u):
                    if again(n, 1):
                        act.wait_ge(z_fill, 16 * (before_ + n))
                    act.nop(nofuse=True)
                    rows_n = agg_d[q][bass.ds(n * fills * NFILL, fills * NFILL), :]
                    act.dma_start(rows_n.rearrange("(r p k) f -> p r (k f)", r=fills, p=P),
                                  fill[q][:, :].unsqueeze(1).to_broadcast([P, fills, NFILL // P * F])).then_inc(z_fill, 16)
                return stage

            stepped(act, [(clear(1, Z_REP, 0), 0)], NCH // Z_REP)

            for b in range(NB):
                w = min(P, HI - b * P)
                act.wait_ge(h_pos, b + 1)
                act.dma_start(pos_d[b * P * P:(b * P + w) * P, :].rearrange("(h l) q -> h (l q)", l=P),
                              pos_n[0:w, b * 2 * P:(b + 1) * 2 * P]).then_inc(h_out, 16)
            act.wait_ge(h_out, 16 * NB)

            def groups_b(k, slot):
                for q in range(2):
                    if not isinstance(k, int) or 2 * k + q <= NG:
                        yield q, 2 * k + q, 2 * slot + q

            def load_b(k, uses_, slot):
                for q, g, b in groups_b(k, slot):
                    m = parts_of(g)
                    if again(k):
                        act.wait_ge(b_row_made, 2 * g - 6)
                    act.nop(nofuse=True)
                    act.dma_start(xb[b][0:m, :], group(x, g)).then_inc(b_in[b], 16)
                    act.dma_start(ps[b][0:m, :], group(pos_d, g)).then_inc(b_in[b], 16)

            def row_b(k, uses_, slot):
                for q, g, b in groups_b(k, slot):
                    m = parts_of(g)
                    act.wait_ge(b_in[b], 32 * uses_ + 32)
                    if again(k, 1):
                        act.wait_ge(b_out[q], 16 * k)
                    act.nop(nofuse=True)
                    act.activation(byf(xs[q], ROW)[0:m, :, 0:F], byf(xb[b])[0:m], ACT.Copy).then_inc(b_row_made, 1)
                    act.activation(byf(xs[q], ROW)[0:m, :, F:ROW], byf(ps[b], 2)[0:m], ACT.Copy).then_inc(b_row_made, 1)
                    act.wait_ge(b_row_made, 2 * g + 2)
                    act.nop(nofuse=True)
                    act.dma_start(group(xpos, g), xs[q][0:m, :]).then_inc(b_out[q], 16)

            def node_steps():
                def load_a(phase, k):
                    _, per, m = nodes_of(phase, k)
                    if phase > 1:
                        act.wait_ge(a_sub, before(phase, k))
                        act.nop(nofuse=True)
                    act.dma_start(a_h[0:m, 0:per * F], node_rows(x, phase, k)).then_inc(a_in, 16)

                def square_a(phase, k):
                    _, per, m = nodes_of(phase, k)
                    act.wait_ge(a_sub, before(phase, k) + 1)
                    act.nop(nofuse=True)
                    act.activation(a_s[0:m, 0:per * F], a_c[0:m, 0:per * F], ACT.Square).then_inc(a_sq, 1)

                def root_a(phase, k):
                    _, per, m = nodes_of(phase, k)
                    act.wait_ge(a_var, before(phase, k) + 1)
                    act.nop(nofuse=True)
                    act.activation(a_st[0:m, 2 * NPP:2 * NPP + per], a_st[0:m, NPP:NPP + per], ACT.Sqrt,
                                   bias=eps_ln[0:m, :], scale=1.0 / F).then_inc(a_std, 1)

                def store_a(phase, k):
                    _, per, m = nodes_of(phase, k)
                    act.wait_ge(a_y, 2 * before(phase, k) + 2)
                    act.nop(nofuse=True)
                    act.dma_start(node_rows(y1_d, phase, k), a_c[0:m, 0:per * F]).then_inc(a_out, 16)

                return load_a, square_a, root_a, store_a

            def nodes_stage(phase):
                load_a, square_a, root_a, store_a = node_steps()
                return in_fours(phase, {0: [(root_a, -1), (load_a, 0)], 1: [(store_a, -1)], 3: [(square_a, 0)]})

            stepped(act, [(load_b, 0), (row_b, 1)], (NG + 2) // 2)
            for q in range(2):
                act.wait_ge(b_out[q], 16 * (NG // 2 + 1 - q))
            act.wait_ge(z_fill, 16 * (NCH // Z_REP))
            phase_end(act, 1)

            def xi0(n, k, u):
                freed(act, q0["t_ready"], n, depth=4)
                freed(act, q0["taken"], n, depth=4)
                act.nop(nofuse=True)
                act.activation(fx3(u)[:, :, 0:F], xl_at(0, n), ACT.Copy).then_inc(q0["xi"], 1)

            def front0(n, k, u):
                w = u % 2
                act.wait_ge(q0["t_ready"], n + 1)
                freed(act, q0["p_ready"], n)
                act.nop(nofuse=True)
                act.activation(xt[w], p_t[w], ACT.Copy).then_inc(q0["xt_ready"], 1)

            def mid0(n, k, u):
                w = u % 2
                act.wait_ge(q0["m_ready"], n + 1)
                freed(act, q0["scan"], n)
                act.nop(nofuse=True)
                act.activation(ms[w][0:F, :], p_m[w][0:F, :], ACT.Identity, bias=bias0[:, :]).then_inc(q0["ms_ready"], 1)
                act.wait_ge(q0["p_ready"], n + 1)
                stored(act, q0["d_part"][w], n, 2 * k + u // 2)
                act.nop(nofuse=True)
                act.activation(pl[w], p_p[w], ACT.Identity, bias=bias12[:, :]).then_inc(q0["part_ready"], 1)

            def back0(n, k, u):
                w = u % 2
                act.wait_ge(q0["part_ready"], n + 1)
                act.nop(nofuse=True)
                act.dma_start(part_d[:, bass.ds(e0(0, n), CH)], pl[w]).then_inc(q0["d_part"][w], 16)
                act.wait_ge(q0["b_ready"], n + 1)
                stored(act, q0["d_table"][w], n, 2 * k + u // 2)
                act.nop(nofuse=True)
                act.activation(ts[w], p_b[w][:, 0:TPC * F], ACT.Copy).then_inc(q0["ts_ready"], 1)

            def out0(n, k, u):
                w = u % 2
                act.wait_ge(q0["ts_ready"], n + 1)
                act.nop(nofuse=True)
                act.dma_start(rows(tables[0], 0, n), byf(ts[w])).then_inc(q0["d_table"][w], 16)

            for fn in node_steps():
                fn(1, 0)
            stepped(act, [(xi0, 0), (front0, 1), (mid0, 2), (back0, 3), (out0, 3), (nodes_stage(2), 0)], NCH, 4)
            for w in range(2):
                act.wait_ge(q0["d_part"][w], 16 * (NCH // 2))
                act.wait_ge(q0["d_table"][w], 16 * (NCH // 2))
            act.wait_ge(a_out, 16 * before(3, 0))
            phase_end(act, 2)

            for l in (1, 2):
                s = q12[l]

                def front(n, k, u):
                    w = u % 2
                    act.wait_ge(s["t_ready"], n + 1)
                    freed(act, s["p_ready"], n)
                    act.nop(nofuse=True)
                    act.activation(xt[w][F:P, :], p_t[w][F:P, :], ACT.Copy).then_inc(s["o_ready"], 1)

                def back1(n, k, u):
                    w = u % 2
                    act.wait_ge(s["fb_ready"], n + 1)
                    stored(act, s["d_table"][w], n, 2 * k + u // 2)
                    act.nop(nofuse=True)
                    act.activation(ts[w], p_m[w][:, 0:TPC * F], ACT.Copy).then_inc(s["ts_ready"], 1)

                def store_part(n, k, u):
                    w = u % 2
                    act.wait_ge(s["s_ready"], n + 1)
                    act.nop(nofuse=True)
                    act.dma_start(part_d[F:P, bass.ds(e0(l, n), CH)], ms[w][F:P, :]).then_inc(s["d_part"][w], 16)

                def store_out(n, k, u):
                    w = u % 2
                    if l == 1:
                        act.wait_ge(s["ts_ready"], n + 1)
                        act.nop(nofuse=True)
                        act.dma_start(rows(tables[1], l, n), byf(ts[w])).then_inc(s["d_table"][w], 16)
                    else:
                        act.wait_ge(s["scan"], n + 1)
                        act.nop(nofuse=True)
                        act.dma_start(o2_d[:, bass.ds(e0(l, n), CH)], fs[w][0:F, :]).then_inc(s["d_table"][w], 16)

                if l == 1:
                    stages = [(front, 0), (store_part, 2), (back1, 2), (store_out, 2)]
                else:
                    stages = [(front, 0), (store_out, 2)]
                    stages.append((clear(0, 1, NCH // Z_REP), 0))
                stepped(act, stages + [(nodes_stage(l + 2), 0)], NCH, 4)
                act.wait_ge(a_out, 16 * before(l + 3, 0))
                if l == 2:
                    act.wait_ge(z_fill, 16 * (NCH // Z_REP + NCH))
                for w in range(2):
                    if l == 1:
                        act.wait_ge(s["d_part"][w], 16 * (NCH // 2))
                    act.wait_ge(s["d_table"][w], 16 * (NCH // 2))
                phase_end(act, l + 2)

            def square3(n, k, u):
                w = u % 2
                act.wait_ge(q3["sub"], 3 * n + 3)
                freed(act, q3["var"], n)
                act.nop(nofuse=True)
                act.activation(sq3[w], yy[u], ACT.Square).then_inc(q3["sq"], 1)

            def root3(n, k, u):
                w = u % 2
                act.wait_ge(q3["var"], n + 1)
                act.nop(nofuse=True)
                act.activation(st3[w][:, 2 * TPC:3 * TPC], st3[w][:, TPC:2 * TPC], ACT.Sqrt,
                               bias=eps_ln[:, :], scale=1.0 / F).then_inc(q3["std"], 1)

            def project3(n, k, u):
                w = u % 2
                act.wait_ge(q3["yt_ready"], n + 1)
                freed(act, q3["z_ready"], n)
                act.nop(nofuse=True)
                act.activation(xt[w][0:F, :], p_t[w][0:F, :], ACT.Copy).then_inc(q3["yts"], 1)

            def sum3(n, k, u):
                w = u % 2
                act.wait_ge(q3["sum_ready"], n + 1)
                for q in range(2):
                    freed(act, q3["d_add"][q], n, 32, 4)
                act.nop(nofuse=True)
                act.activation(ga[u], p_p[w][:, 0:TPC * F], ACT.Copy).then_inc(q3["ga_ready"], 1)

            stepped(act, [(project3, 2), (sum3, 4), (square3, 1), (root3, 1)], NCH, 4)
            phase_end(act, 5)

            def norm_f(n, k, u):
                m = parts_of(n)
                act.wait_ge(f_sum, n + 1)
                act.nop(nofuse=True)
                for q in range(NPP):
                    last = act.activation(grp[u][2][0:m, q * F:(q + 1) * F], grp[u][1][0:m, q * F:(q + 1) * F], ACT.Square,
                                          accum_out=stats[u][0:m, q:q + 1])
                last.then_inc(f_nrm, 1)

            def root1_f(n, k, u):
                m = parts_of(n)
                act.wait_ge(f_nrm, n + 1)
                act.nop(nofuse=True)
                act.activation(stats[u][0:m, NPP:2 * NPP], stats[u][0:m, 0:NPP], ACT.Sqrt).then_inc(f_std1, 1)

            def square_f(n, k, u):
                m = parts_of(n)
                act.wait_ge(f_sub, 2 * n + 2)
                act.nop(nofuse=True)
                act.activation(grp[u][2][0:m, :], grp[u][1][0:m, :], ACT.Square).then_inc(f_sq2, 1)

            def root2_f(n, k, u):
                m = parts_of(n)
                act.wait_ge(f_var, n + 1)
                act.nop(nofuse=True)
                act.activation(stats[u][0:m, 5 * NPP:6 * NPP], stats[u][0:m, 4 * NPP:5 * NPP], ACT.Sqrt,
                               bias=eps_ln[0:m, :], scale=1.0 / F).then_inc(f_std2, 1)

            def store_f(n, k, u):
                act.wait_ge(f_y, 2 * n + 2)
                act.dma_start(group(out, n), grp[u][1][0:parts_of(n), :]).then_inc(f_out[u], 16)

            stepped(act, [(norm_f, 1), (root2_f, 4), (root1_f, 1), (square_f, 3), (store_f, 4)], NG + 1, F_DEEP)
            for u in range(F_DEEP):
                act.wait_ge(f_out[u], 16 * ((NG + 1 - u + F_DEEP - 1) // F_DEEP))
            phase_end(act, 6)

        @block.tensor
        def _(pe):
            pe.wait_ge(c_pool, 5)
            for q, tile in enumerate((n_dstf, n_dsts, n_srcf, n_ew)):
                if q < 2:
                    pe.wait_ge(c_rows, q + 1)
                if q == 3:
                    pe.wait_ge(c_nat, 16 * 9)
                for j in range(TPC):
                    last = nc.tensor.transpose(psum[:, q, j * NCH:(j + 1) * NCH], tile[:, j * P:(j + 1) * P],
                                               ident[0:NCH, 0:NCH])
                last.then_inc(c_tr, 1)

            def count(lo, hi, start=False, stop=False):
                for b in range(2):
                    last = nc.tensor.matmul(psum[:, 4 + b, 0:HB], lo, hi[:, b * HB:(b + 1) * HB],
                                            start=start, stop=stop)
                last.then_inc(h_free, 1)

            pe.wait_ge(h_made, 1)
            count(oh_l[0], oh_h[0], start=True)

            def count_tile(n, k, u):
                pe.wait_ge(h_made, n + 2)
                count(oh_l[u], oh_h[u], stop=isinstance(n, int) and n == NT - 1)

            stepped(pe, [(count_tile, 0)], NT - 8, 8)
            for u in range(8):
                count_tile(NT - 8 + u, NT // 8 - 1, u)
            pe.wait_ge(h_v, 1)
            pe.wait_ge(c_pool, 10)
            for b in range(2):
                nc.tensor.matmul(psum[:, b, 0:HB], upper, cnt[:, b * HB:(b + 1) * HB], start=True, stop=True)
                last = nc.tensor.matmul(psum[:, 2 + b, 0:HB], ones, cnt[:, b * HB:(b + 1) * HB], start=True, stop=True)
            last.then_inc(h_pe, 1)
            pe.wait_ge(h_v, H_STEPS)
            for b in range(NB):
                w = min(P, HI - b * P)
                if b >= 4:
                    pe.wait_ge(h_pos, b - 3)
                for q, t in enumerate((last_c, first_c)):
                    last = nc.tensor.transpose(psum[0:w, 4 + b % 4, q * P:(q + 1) * P], t[:, b * P:b * P + w],
                                               ident[:, :])
                last.then_inc(h_tr, 1)
            phase_end(pe, 1)

            def front0(n, k, u):
                w = u % 2
                pe.wait_ge(q0["xi"], n + 1)
                pe.wait_ge(q0["d_got"][u], 64 * k + 64)
                freed(pe, q0["xt_ready"], n)
                pe.nop(nofuse=True)
                for j in range(TPC):
                    last = nc.tensor.transpose(p_t[w][:, j * P:(j + 1) * P], fx3(u)[:, j, 0:P], ident[:, :])
                last.then_inc(q0["t_ready"], 1)

            def mid0(n, k, u):
                w = u % 2
                pe.wait_ge(q0["xt_ready"], n + 1)
                freed(pe, q0["ms_ready"], n)
                pe.nop(nofuse=True)
                nc.tensor.matmul(p_m[w][0:F, :], w_x[:, 0:F], xt[w], start=True, stop=True).then_inc(q0["m_ready"], 1)
                freed(pe, q0["part_ready"], n)
                pe.nop(nofuse=True)
                nc.tensor.matmul(p_p[w], w_x[:, F:3 * F], xt[w], start=True, stop=True).then_inc(q0["p_ready"], 1)

            def by_edge(bank, rows_t, done):
                for j in range(TPC):
                    last = nc.tensor.transpose(bank[:, j * F:(j + 1) * F], rows_t[0:F, j * P:(j + 1) * P],
                                               ident[0:F, 0:F])
                last.then_inc(done, 1)

            def back0(n, k, u):
                w = u % 2
                pe.wait_ge(q0["scan"], n + 1)
                freed(pe, q0["ts_ready"], n)
                pe.nop(nofuse=True)
                by_edge(p_b[w], fs[w], q0["b_ready"])

            stepped(pe, [(front0, 0), (mid0, 1), (back0, 2)], NCH, 4)
            phase_end(pe, 2)

            for l in (1, 2):
                s = q12[l]
                width = P if l == 1 else F

                def front(n, k, u):
                    w = u % 2
                    pe.wait_ge(q12_in[u], 48 * (l - 1) * uses(u) + 48 * k + 48)
                    pe.wait_ge(s["d_got"][u], 64 * k + 64)
                    freed(pe, s["g_ready"], n)
                    freed(pe, s["o_ready"], n)
                    pe.nop(nofuse=True)
                    for j in range(TPC):
                        last = nc.tensor.transpose(p_t[w][:, j * P:(j + 1) * P], fx3(u)[:, j, 0:P], ident[:, :])
                    last.then_inc(s["t_ready"], 1)

                def mid(n, k, u):
                    w = u % 2
                    pe.wait_ge(s["g_ready"], n + 1)
                    pe.wait_ge(s["o_ready"], n + 1)
                    freed(pe, s["s_ready"], n)
                    pe.nop(nofuse=True)
                    nc.tensor.matmul(p_p[w][0:width, :], w_o[l - 1][:, :], xt[w], start=True, stop=True).then_inc(s["p_ready"], 1)
                    freed(pe, s["gmax"], n)
                    pe.nop(nofuse=True)
                    by_edge(p_b[w], xt[w], s["gb_ready"])

                def back1(n, k, u):
                    w = u % 2
                    pe.wait_ge(s["scan"], n + 1)
                    freed(pe, s["ts_ready"], n)
                    pe.nop(nofuse=True)
                    by_edge(p_m[w], fs[w], s["fb_ready"])

                stepped(pe, [(front, 0), (mid, 1)] + ([(back1, 2)] if l == 1 else []), NCH, 4)
                phase_end(pe, l + 2)

            def by_edge3(n, k, u):
                w = u % 2
                pe.wait_ge(q3["scan"], n + 1)
                freed(pe, q3["gmax"], n)
                pe.nop(nofuse=True)
                by_edge(p_b[w], fs[w], q3["gb_ready"])

            def transpose3(n, k, u):
                w = u % 2
                pe.wait_ge(q3["y_ready"], 2 * n + 2)
                freed(pe, q3["yts"], n)
                pe.nop(nofuse=True)
                for j in range(TPC):
                    last = nc.tensor.transpose(p_t[w][0:F, j * P:(j + 1) * P], yy[u][:, j * F:(j + 1) * F], ident[:, :])
                last.then_inc(q3["yt_ready"], 1)

            def project3(n, k, u):
                w = u % 2
                pe.wait_ge(q3["yts"], n + 1)
                freed(pe, q3["zs"], n)
                pe.nop(nofuse=True)
                for j in range(TPC):
                    last = nc.tensor.matmul(p_m[w][:, j * F:(j + 1) * F], xt[w][0:F, j * P:(j + 1) * P], w_p[:, :],
                                            start=True, stop=True)
                last.then_inc(q3["z_ready"], 1)

            def sum3(n, k, u):
                w = u % 2
                pe.wait_ge(q3["zs"], n + 1)
                pe.wait_ge(q3["eq"], n + 1)
                freed(pe, q3["ga_ready"], n)
                pe.nop(nofuse=True)
                for j in range(TPC):
                    last = nc.tensor.matmul(p_p[w][:, j * F:(j + 1) * F], eq[w][:, j * P:(j + 1) * P],
                                            zs[w][:, j * F:(j + 1) * F], start=True, stop=True)
                last.then_inc(q3["sum_ready"], 1)

            stepped(pe, [(transpose3, 2), (sum3, 4), (by_edge3, 0), (project3, 2)], NCH, 4)
            phase_end(pe, 5)
            phase_end(pe, 6)

        @block.vector
        def _(ve):
            v = nc.vector
            chained = {}

            def link(ins, counter):
                chained[counter.name] = chained.get(counter.name, 0) + 1
                ins.then_inc(counter, 1)
                ve.wait_ge(counter, chained[counter.name])

            v.memset(n_dst, N).then_inc(c_memset, 1)
            v.memset(n_src, N)
            v.memset(n_next, N)
            v.memset(n_ew, 0.0)
            link(v.memset(n_prev, N), c_v)
            v.memset(n_prev[0:1, 0:1], -1).then_inc(c_memset, 1)
            v.memset(ones, 1.0)
            v.memset(eps_ln[:, :], EPS_LN)
            v.memset(zero[:, :], 0.0)
            v.memset(fill[1][:, :], 0.0).then_inc(c_zero, 1)
            v.memset(oh_l[0], 0.0)
            v.memset(oh_h[0], 0.0).then_inc(h_made, 1)

            def column(q):
                return psum[:, q, 0:NT].rearrange("p (j c) -> p j c", c=NCH)

            def by_j(a):
                return a.rearrange("p (c j) -> p j c", j=TPC)

            ve.wait_ge(c_din, 32)
            link(v.tensor_copy(n_dstf, n_dst), c_rows)
            ve.wait_ge(c_tr, 1)
            v.tensor_scalar(by_j(dst_g[:, :]), column(0), float(N - 1), None, ALU.min).then_inc(c_dst, 1)
            v.tensor_copy(by_j(lo_f), column(0))
            link(v.tensor_copy(by_j(hi_i), column(0)), c_v)
            link(v.tensor_scalar(hi_i, hi_i, 7, None, ALU.arith_shift_right), c_v)
            link(v.tensor_copy(hi_f, hi_i), c_v)
            link(v.scalar_tensor_tensor(out=lo_f, in0=hi_f, scalar=-float(P), in1=lo_f, op0=ALU.mult, op1=ALU.add), c_v)
            ve.wait_ge(c_nat, 16 * 9)
            ve.wait_ge(c_memset, 2)
            ve.wait_ge(c_pool, 4)
            v.tensor_tensor(n_same, n_dst, n_prev, ALU.is_equal).then_inc(c_same, 1)
            v.tensor_tensor(n_last, n_dst, n_next, ALU.not_equal)
            v.tensor_copy(n_srcf, n_src).then_inc(c_same, 1)
            link(v.tensor_tensor(n_dsts, n_dstf, n_dummy, ALU.subtract), c_v)
            link(v.tensor_tensor(n_dsts, n_dsts, n_last, ALU.mult), c_v)
            v.tensor_tensor(n_dsts, n_dsts, n_dummy, ALU.add).then_inc(c_rows, 1)
            ve.wait_ge(c_tr, 4)
            v.tensor_copy(by_j(dst_s[:, :]), column(1))
            v.tensor_scalar(by_j(src_g[:, :]), column(2), float(N - 1), None, ALU.min)
            v.tensor_copy(by_j(src_f[:, :]), column(2))
            link(v.tensor_copy(by_j(ew[:, :]), column(3)), c_v)
            ve.wait_ge(c_pool, 10)

            def one_hot(n, k, u):
                if u == 0:
                    ve.wait_ge(h_free, n - 3 if again(n, 8) else 1)
                if u == 4 and again(n, 8):
                    ve.wait_ge(h_free, n - 3)
                v.tensor_scalar(oh_h[u], iota_h, hi_f[:, bass.ds(n, 1)], None, ALU.is_equal)
                v.tensor_scalar(oh_l[u], iota_l, lo_f[:, bass.ds(n, 1)], None, ALU.is_equal).then_inc(h_made, 1)

            stepped(ve, [(one_hot, 0)], NT, 8)
            ve.wait_ge(c_wts, 16 * 23)
            v.tensor_tensor(w_x[0:F, :], w_x[0:F, :], w_b[:, 0:3 * F], ALU.subtract)
            v.tensor_tensor(w_o[0][0:F, :], w_o[0][0:F, :], w_b[:, 3 * F:5 * F], ALU.subtract)
            v.tensor_tensor(w_o[1][0:F, :], w_o[1][0:F, :], w_b[:, 5 * F:6 * F], ALU.subtract)
            v.tensor_copy(byf(fill[0][:, :]), b_row.unsqueeze(1).to_broadcast([P, NFILL // P, F]))
            ve.wait_ge(h_free, NT + 1)
            ve.wait_ge(c_out, 16 * 5)

            def halves(a):
                return a.rearrange("p (b h) -> p b h", b=2)

            link(v.tensor_copy(halves(cnt), psum[:, 4:6, 0:HB]), h_v)
            link(v.memset(last_c, 0.0), h_v)
            ve.wait_ge(h_pe, 1)
            link(v.tensor_copy(halves(tot), psum[:, 2:4, 0:HB]), h_v)
            link(v.tensor_tensor_scan(run, last_c, tot, 0.0, ALU.add, ALU.add), h_v)
            link(v.tensor_tensor(run, run, tot, ALU.subtract), h_v)
            link(v.tensor_tensor(halves(run), halves(run), psum[:, 0:2, 0:HB], ALU.add), h_v)
            link(v.tensor_scalar(tot, cnt, 0.0, None, ALU.is_gt), h_v)
            link(v.scalar_tensor_tensor(out=last_c, in0=run, scalar=-1.0 - ZROW, in1=tot, op0=ALU.add, op1=ALU.mult), h_v)
            link(v.tensor_scalar(last_c, last_c, float(ZROW), None, ALU.add), h_v)
            link(v.tensor_tensor(first_c, run, cnt, ALU.subtract), h_v)
            link(v.scalar_tensor_tensor(out=first_c, in0=first_c, scalar=-float(ZROW), in1=tot, op0=ALU.add, op1=ALU.mult), h_v)
            link(v.tensor_scalar(first_c, first_c, float(ZROW), None, ALU.add), h_v)
            assert chained[h_v.name] == H_STEPS
            for b in range(NB):
                w = min(P, HI - b * P)
                ve.wait_ge(h_tr, b + 1)
                v.tensor_copy(pos_n[0:w, b * 2 * P:(b + 1) * 2 * P].rearrange("p (l q) -> p q l", q=2),
                              psum[0:w, 4 + b % 4, 0:2 * P].rearrange("p (q l) -> p q l", q=2)).then_inc(h_pos, 1)

            def node_steps():
                def center_a(phase, k):
                    _, per, m = nodes_of(phase, k)
                    c = before(phase, k)
                    hv, gv, sv = byf(a_h[0:m, 0:per * F]), byf(a_gm[0:m, 0:per * 16], 16), a_st[0:m, 0:per]
                    ve.wait_ge(a_in, 16 * c + 16)
                    v.tensor_reduce(gv, hv.rearrange("p k (g q) -> p k g q", q=4), X, ALU.max).then_inc(a_v, 1)
                    ve.wait_ge(a_v, 3 * c + 1)
                    v.tensor_tensor(hv[:, :, 0:16], hv[:, :, 0:16], gv, ALU.add).then_inc(a_v, 1)
                    ve.wait_ge(a_v, 3 * c + 2)
                    v.tensor_reduce(sv, hv, X, ALU.add).then_inc(a_v, 1)
                    ve.wait_ge(a_v, 3 * c + 3)
                    if phase > 1:
                        ve.wait_ge(a_out, 16 * c)
                    v.scalar_tensor_tensor(out=byf(a_c[0:m, 0:per * F]), in0=spread(sv, F), scalar=-1.0 / F,
                                           in1=hv, op0=ALU.mult, op1=ALU.add).then_inc(a_sub, 1)

                def variance_a(phase, k):
                    _, per, m = nodes_of(phase, k)
                    ve.wait_ge(a_sq, before(phase, k) + 1)
                    v.tensor_reduce(a_st[0:m, NPP:NPP + per], byf(a_s[0:m, 0:per * F]), X, ALU.add).then_inc(a_var, 1)

                def scale_a(phase, k):
                    _, per, m = nodes_of(phase, k)
                    hv, rv = byf(a_c[0:m, 0:per * F]), a_st[0:m, 3 * NPP:3 * NPP + per]
                    ve.wait_ge(a_std, before(phase, k) + 1)
                    v.reciprocal(rv, a_st[0:m, 2 * NPP:2 * NPP + per]).then_inc(a_y, 1)
                    ve.wait_ge(a_y, 2 * before(phase, k) + 1)
                    v.tensor_tensor(hv, hv, spread(rv, F), ALU.mult).then_inc(a_y, 1)

                return center_a, variance_a, scale_a

            def nodes_stage(phase):
                center_a, variance_a, scale_a = node_steps()
                return in_fours(phase, {0: [(scale_a, -1)], 2: [(center_a, 0)], 3: [(variance_a, 0)]})

            phase_end(ve, 1)

            def scan(l, out_, before, data, flags, n, done):
                if isinstance(n, int) and n == 0:
                    start = zero[0:F, :]
                else:
                    ve.wait_ge(done, n)
                    start = end_col(before[0:F, :], l)
                ve.nop(nofuse=True)
                v.tensor_tensor_scan(back(out_[0:F, :], l), back(flags[0:F, :], l), back(data[0:F, :], l), start,
                                     ALU.mult, ALU.max).then_inc(done, 1)

            def add_max(l, n, u, src_rows, first, maxed, added):
                v.tensor_reduce(byf(gm[u], 16), src_rows.rearrange("p j (g q) -> p j g q", q=4), X, ALU.max).then_inc(maxed, 1)
                ve.wait_ge(maxed, n + 1)
                ve.nop(nofuse=True)
                ins = v.tensor_tensor(xl_at(l, n, first, first + 16), xl_at(l, n, first, first + 16), byf(gm[u], 16), ALU.add)
                if added is not None:
                    ins.then_inc(added, 1)

            def take0(n, k, u):
                w = u % 2
                ve.wait_ge(q0["d_got"][u], 64 * k + 64)
                ve.wait_ge(q0["xi"], n + 1)
                ve.nop(nofuse=True)
                for q in range(2):
                    v.tensor_copy(cols(pos_g[q], 0, n), fx3(u)[:, :, P + q])
                add_max(0, n, w, fx3(u)[:, :, 0:F], 0, q0["taken"], None)

            def scan0(n, k, u):
                w = u % 2
                ve.wait_ge(q0["d_in"][u], 16 * k + 16)
                ve.wait_ge(q0["ms_ready"], n + 1)
                freed(ve, q0["b_ready"], n)
                scan(0, fs[w], fs[1 - w], ms[w], sn[u], n, q0["scan"])

            for fn in node_steps():
                fn(1, 0)
            stepped(ve, [(take0, 0), (scan0, 2), (nodes_stage(2), 0)], NCH, 4)
            phase_end(ve, 2)

            for l in (1, 2):
                s = q12[l]
                width = P if l == 1 else F

                def complete(n, k, u):
                    w = u % 2
                    ve.wait_ge(s["t_ready"], n + 1)
                    ve.wait_ge(q12_in[u], 48 * (l - 1) * uses(u) + 48 * k + 48)
                    freed(ve, s["gb_ready"], n)
                    scan(l, xt[w], xt[1 - w], p_t[w], sn[u], n, s["g_ready"])

                def message(n, k, u):
                    w = u % 2
                    ve.wait_ge(s["p_ready"], n + 1)
                    if l == 1:
                        stored(ve, s["d_part"][w], n, 2 * k + u // 2)
                    v.tensor_tensor(ms[w][0:width, :], p_p[w][0:width, :], pl[u][0:width, :], ALU.add).then_inc(s["s_ready"], 1)
                    ve.wait_ge(s["s_ready"], n + 1)
                    if l == 1:
                        freed(ve, s["fb_ready"], n)
                    else:
                        stored(ve, s["d_table"][w], n, 2 * k + u // 2)
                    scan(l, fs[w], fs[1 - w], ms[w], sn[u], n, s["scan"])

                def maxima(n, k, u):
                    w = u % 2
                    ve.wait_ge(s["gb_ready"], n + 1)
                    add_max(l, n, w, byf(p_b[w][:, 0:TPC * F]), 16 * l, s["gmax"], None)

                stepped(ve, [(complete, 0), (message, 1), (maxima, 1), (nodes_stage(l + 2), 0)], NCH, 4)
                phase_end(ve, l + 2)

            def scan3(n, k, u):
                w = u % 2
                ve.wait_ge(q3["d_in"][u], 48 * k + 48)
                freed(ve, q3["gb_ready"], n)
                scan(3, fs[w], fs[1 - w], pl[u], sn[u], n, q3["scan"])

            def center3(n, k, u):
                w = u % 2
                ve.wait_ge(q3["gb_ready"], n + 1)
                add_max(3, n, w, byf(p_b[w][:, 0:TPC * F]), 48, q3["gmax"], q3["sub"])
                ve.wait_ge(q3["sub"], 3 * n + 1)
                ve.nop(nofuse=True)
                v.tensor_reduce(st3[w][:, 0:TPC], xl_at(3, n), X, ALU.add).then_inc(q3["sub"], 1)
                ve.wait_ge(q3["sub"], 3 * n + 2)
                stored(ve, q3["d_y"][u], n, k, 64, 4)
                freed(ve, q3["yt_ready"], n, depth=4)
                ve.nop(nofuse=True)
                v.scalar_tensor_tensor(out=byf(yy[u]), in0=spread(st3[w][:, 0:TPC], F), scalar=-1.0 / F,
                                       in1=xl_at(3, n), op0=ALU.mult, op1=ALU.add).then_inc(q3["sub"], 1)

            def same_src3(n, k, u):
                w = u % 2
                freed(ve, q3["sum_ready"], n)
                ve.nop(nofuse=True)
                eq3 = byf(eq[w], P)
                v.tensor_tensor(eq3, byf(sr[u], P), spread(cols(src_f, 3, n), P), ALU.is_equal).then_inc(q3["eq"], 1)
                ve.wait_ge(q3["eq"], n + 1)
                v.tensor_tensor(byf(eqm, P), eq3, mask[:, :, :], ALU.mult).then_inc(q3["eqc"], 1)
                ve.wait_ge(q3["eqc"], 3 * n + 1)
                v.tensor_reduce(dup, byf(eqm, P), X, ALU.max).then_inc(q3["eqc"], 1)
                ve.wait_ge(q3["eqc"], 3 * n + 2)
                ve.nop(nofuse=True)
                v.scalar_tensor_tensor(out=off, in0=cols(src_f, 3, n), scalar=dummy_f[:, :], in1=dup,
                                       op0=ALU.subtract, op1=ALU.mult).then_inc(q3["eqc"], 1)
                ve.wait_ge(q3["eqc"], 3 * n + 3)
                for q in range(2):
                    freed(ve, q3["d_add"][q], n, 32, 4)
                ve.nop(nofuse=True)
                v.tensor_tensor(add_i[u], cols(src_f, 3, n), off, ALU.subtract).then_inc(q3["add_i"], 1)

            def variance3(n, k, u):
                w = u % 2
                ve.wait_ge(q3["sq"], n + 1)
                v.tensor_reduce(st3[w][:, TPC:2 * TPC], byf(sq3[w]), X, ALU.add).then_inc(q3["var"], 1)

            def scale3(n, k, u):
                w = u % 2
                ve.wait_ge(q3["std"], n + 1)
                v.reciprocal(st3[w][:, 3 * TPC:4 * TPC], st3[w][:, 2 * TPC:3 * TPC]).then_inc(q3["y_ready"], 1)
                ve.wait_ge(q3["y_ready"], 2 * n + 1)
                v.tensor_tensor(byf(yy[u]), byf(yy[u]), spread(st3[w][:, 3 * TPC:4 * TPC], F), ALU.mult).then_inc(q3["y_ready"], 1)

            def weigh3(n, k, u):
                w = u % 2
                ve.wait_ge(q3["z_ready"], n + 1)
                freed(ve, q3["sum_ready"], n)
                ve.nop(nofuse=True)
                v.tensor_tensor(byf(zs[w]), byf(p_m[w][:, 0:TPC * F]), spread(cols(ew, 3, n), F), ALU.mult).then_inc(q3["zs"], 1)

            stepped(ve, [(center3, 1), (scan3, 0), (variance3, 1), (weigh3, 3), (scale3, 1), (same_src3, 3)], NCH, 4)
            phase_end(ve, 5)

            def unit_f(n, k, u):
                m = parts_of(n)
                st = stats[u]
                ve.wait_ge(f_std1, n + 1)
                v.tensor_scalar(st[0:m, 2 * NPP:3 * NPP], st[0:m, NPP:2 * NPP], EPS_NORM, None, ALU.max).then_inc(f_unit, 1)
                ve.wait_ge(f_unit, 3 * n + 1)
                v.reciprocal(st[0:m, 3 * NPP:4 * NPP], st[0:m, 2 * NPP:3 * NPP]).then_inc(f_unit, 1)
                ve.wait_ge(f_unit, 3 * n + 2)
                scale_rows(v, n, u, 0, V_NODES).then_inc(f_unit, 1)

            def center_f(n, k, u):
                m = parts_of(n)
                st, hv = stats[u], byf(grp[u][1])[0:m]
                ve.wait_ge(f_h, 2 * n + 2)
                v.tensor_reduce(st[0:m, 6 * NPP:7 * NPP], hv, X, ALU.add).then_inc(f_sub, 1)
                ve.wait_ge(f_sub, 2 * n + 1)
                v.scalar_tensor_tensor(out=hv, in0=spread(st[0:m, 6 * NPP:7 * NPP], F), scalar=-1.0 / F, in1=hv,
                                       op0=ALU.mult, op1=ALU.add).then_inc(f_sub, 1)

            def variance_f(n, k, u):
                m = parts_of(n)
                ve.wait_ge(f_sq2, n + 1)
                v.tensor_reduce(stats[u][0:m, 4 * NPP:5 * NPP], byf(grp[u][2])[0:m], X, ALU.add).then_inc(f_var, 1)

            def scale_f(n, k, u):
                m = parts_of(n)
                ve.wait_ge(f_std2, n + 1)
                v.reciprocal(stats[u][0:m, 7 * NPP:8 * NPP], stats[u][0:m, 5 * NPP:6 * NPP]).then_inc(f_y, 1)
                ve.wait_ge(f_y, 2 * n + 1)
                v.tensor_tensor(byf(grp[u][1])[0:m], byf(grp[u][1])[0:m], spread(stats[u][0:m, 7 * NPP:8 * NPP], F),
                                ALU.mult).then_inc(f_y, 1)

            stepped(ve, [(unit_f, 2), (center_f, 3), (scale_f, 4), (variance_f, 3)], NG + 1, F_DEEP)
            phase_end(ve, 6)


_INS = ["x", "src", "dst", "edge_weight", "L0_gnn_W0", "L0_gnn_b0", "L0_gnn_W1", "L0_gnn_b1", "L0_gnn_W2",
        "L0_gnn_b2", "L1_gnn_weight", "L1_gnn_bias"]
_OUTS = [((N, F), "float32")]


def kernel(**inputs):
    import numpy as _np
    import concourse.bacc as _bacc
    from concourse import mybir as _mybir
    from concourse.bass_utils import run_bass_kernel_spmd as _run

    nc = _bacc.Bacc("TRN2", target_bir_lowering=False, num_devices=1)
    arrays, args = {}, []
    for name in _INS:
        a = _np.ascontiguousarray(inputs[name])
        arrays[f"in_{name}_dram"] = a
        args.append(nc.dram_tensor(f"in_{name}_dram", a.shape, _mybir.dt.from_np(a.dtype), kind="ExternalInput").ap())
    for i, (shape, dtype) in enumerate(_OUTS):
        dt = _mybir.dt.from_np(_np.dtype(dtype))
        args.append(nc.dram_tensor(f"out_{i}_dram", shape, dt, kind="ExternalOutput").ap())
    build(nc, *args)
    r = _run(nc, [arrays], core_ids=[0])
    return r.results[0]["out_0_dram"]
```
